# Optimizing a Trainium2 kernel written in Bass

```python
import numpy as np
import jax
import jax.numpy as jnp

def _softmax(x, axis=-1):
    return jax.nn.softmax(x, axis=axis)

def _gelu(x):
    return jax.nn.gelu(x, approximate=True)

def _silu(x):
    return jax.nn.silu(x)

def _sigmoid(x):
    return jax.nn.sigmoid(x)

def _layernorm(x, axis=-1, eps=1e-05):
    m = jnp.mean(x, axis=axis, keepdims=True)
    v = jnp.var(x, axis=axis, keepdims=True)
    return (x - m) / jnp.sqrt(v + eps)

def _scatter_add(tgt, idx, src, axis=0):
    return tgt.at[idx].add(src)

def _segment_sum(src, seg, n):
    return jax.ops.segment_sum(src, seg, n)
kernel_name = 'mk_gps_d2_gnn_r32_b480da'

def setup_inputs(seed: int=0):
    np.random.seed(seed)
    _w = jnp.asarray

    def _rec_inputs():
        import jax
        import jax.numpy as jnp
        _gk = jax.random.key(seed)
        x = -7.329e-05 + 0.9999 * jax.random.normal(jax.random.fold_in(_gk, 1), (3125, 256), jnp.float32)
        src = jax.random.randint(jax.random.fold_in(_gk, 2), (50000,), 0, 3125, jnp.int32)
        dst = jax.random.randint(jax.random.fold_in(_gk, 3), (50000,), 0, 3125, jnp.int32)
        _o = jnp.argsort(dst, stable=True)
        src = src[_o]
        dst = dst[_o]
        edge_weight = jax.random.uniform(jax.random.fold_in(_gk, 13), (50000,), jnp.float32, 0.0, 0.03125)
        return (x, src, dst, edge_weight)
    x, src, dst, edge_weight = _rec_inputs()

    def _L0_gnn_setup():
        import jax, jax.numpy as jnp
        import numpy as np
        N = 6250
        E = 18750
        C = 256
        key = jax.random.key(seed)
        k1, k2, k3, k4, k5 = jax.random.split(key, 5)
        x = jax.random.normal(k1, (N, C), dtype=jnp.float32)
        sources = jax.random.randint(k2, (E,), 0, N, dtype=jnp.int64)
        targets = jax.random.randint(k3, (E,), 0, N, dtype=jnp.int64)
        norm = jax.random.uniform(k4, (N, 1), dtype=jnp.float32)
        std = float(np.sqrt(2.0 / (C + C)))
        weight = jax.random.normal(k5, (C, C), dtype=jnp.float32) * std
        return {'x': x, 'sources': sources, 'targets': targets, 'norm': norm, 'weight': weight}
    _L0_gnn_all = _L0_gnn_setup()
    _L0_gnn_in = {k: v for k, v in _L0_gnn_all.items() if k in ('weight',)}
    del _L0_gnn_all

    def _L0_mix_setup():
        import jax, jax.numpy as jnp
        import numpy as np
        NHEAD = 8
        ATT_EPS = 1e-06
        LN_EPS = 1e-05

        def _layernorm(x, g, b):
            mu = jnp.mean(x, axis=-1, keepdims=True)
            var = jnp.mean(jnp.square(x - mu), axis=-1, keepdims=True)
            return (x - mu) * jax.lax.rsqrt(var + LN_EPS) * g + b
        key = jax.random.key(seed)
        ks = jax.random.split(key, 7)
        N, L, C = (4, 512, 256)
        s = 1.0 / np.sqrt(C)
        return {'x': jax.random.normal(ks[0], (N, L, C), jnp.float32), 'Wq': jax.random.normal(ks[1], (C, C), jnp.float32) * s, 'Wk': jax.random.normal(ks[2], (C, C), jnp.float32) * s, 'Wv': jax.random.normal(ks[3], (C, C), jnp.float32) * s, 'Wm': jax.random.normal(ks[4], (C, C), jnp.float32) * s, 'W1': jax.random.normal(ks[5], (2 * C, 2 * C), jnp.float32) * (1.0 / np.sqrt(2 * C)), 'W2': jax.random.normal(ks[6], (2 * C, C), jnp.float32) * (1.0 / np.sqrt(2 * C)), 'g1': jnp.ones((C,), jnp.float32), 'b1': jnp.zeros((C,), jnp.float32), 'g2': jnp.ones((C,), jnp.float32), 'b2': jnp.zeros((C,), jnp.float32)}
    _L0_mix_all = _L0_mix_setup()
    _L0_mix_in = {k: v for k, v in _L0_mix_all.items() if k in ('Wq', 'Wk', 'Wv', 'Wm', 'W1', 'W2', 'g1', 'b1', 'g2', 'b2')}
    del _L0_mix_all

    def _L0_ffn_setup():
        import jax, jax.numpy as jnp
        import numpy as np
        B, N, D = (16, 128, 256)
        NUM_EXPERTS, TOP_K, HEADS = (4, 2, 4)
        N_EDGES = 32768
        LN_EPS = 1e-05

        def _layernorm(x, g, b):
            mu = x.mean(-1, keepdims=True)
            var = ((x - mu) ** 2).mean(-1, keepdims=True)
            return (x - mu) * jax.lax.rsqrt(var + LN_EPS) * g + b

        def _forward(x, edge_index, W_gat, att_src, att_dst, b_gat, ln_gamma, ln_beta, W1, b1, W2, b2):
            Bc, Nc, Dc = x.shape
            M = Bc * Nc
            x_flat = x.reshape(M, Dc)
            h = (x_flat @ W_gat).reshape(M, HEADS, NUM_EXPERTS)
            loops = jnp.arange(M, dtype=edge_index.dtype)
            src = jnp.concatenate([edge_index[0], loops])
            dst = jnp.concatenate([edge_index[1], loops])
            a_src = (h * att_src).sum(-1)
            a_dst = (h * att_dst).sum(-1)
            e = jax.nn.leaky_relu(a_src[src] + a_dst[dst], negative_slope=0.2)
            e_max = jax.ops.segment_max(e, dst, num_segments=M)
            ee = jnp.exp(e - e_max[dst])
            denom = jax.ops.segment_sum(ee, dst, num_segments=M)
            alpha = ee / (denom[dst] + 1e-16)
            msg = h[src] * alpha[:, :, None]
            agg = jax.ops.segment_sum(msg, dst, num_segments=M).reshape(M, HEADS * NUM_EXPERTS) + b_gat
            scores = _layernorm(agg, ln_gamma, ln_beta).reshape(M, HEADS, NUM_EXPERTS).mean(1)
            scores = scores.reshape(Bc, Nc, NUM_EXPERTS)
            topk_s, topk_i = jax.lax.top_k(scores, TOP_K)
            w = jax.nn.softmax(topk_s, axis=-1)
            out = jnp.zeros_like(x)
            for ei in range(NUM_EXPERTS):
                g = jnp.where(topk_i == ei, w, 0.0).sum(-1)
                hh = jax.nn.gelu(x @ W1[ei] + b1[ei], approximate=False)
                out = out + g[..., None] * (hh @ W2[ei] + b2[ei])
            return out
        key = jax.random.key(seed)
        ks = jax.random.split(key, 8)
        s = 0.05
        return {'x': jax.random.normal(ks[0], (B, N, D), jnp.float32), 'W_gat': jax.random.normal(ks[1], (D, HEADS * NUM_EXPERTS), jnp.float32) * s, 'att_src': jax.random.normal(ks[2], (HEADS, NUM_EXPERTS), jnp.float32) * s, 'att_dst': jax.random.normal(ks[3], (HEADS, NUM_EXPERTS), jnp.float32) * s, 'b_gat': jnp.zeros((HEADS * NUM_EXPERTS,), jnp.float32), 'ln_gamma': jnp.ones((HEADS * NUM_EXPERTS,), jnp.float32), 'ln_beta': jnp.zeros((HEADS * NUM_EXPERTS,), jnp.float32), 'W1': jax.random.normal(ks[4], (NUM_EXPERTS, D, 2 * D), jnp.float32) * s, 'b1': jnp.zeros((NUM_EXPERTS, 2 * D), jnp.float32), 'W2': jax.random.normal(ks[5], (NUM_EXPERTS, 2 * D, D), jnp.float32) * s, 'b2': jnp.zeros((NUM_EXPERTS, D), jnp.float32), 'edge_index': jax.random.randint(ks[6], (2, N_EDGES), 0, B * N, jnp.int32)}
    _L0_ffn_all = _L0_ffn_setup()
    _L0_ffn_in = {k: v for k, v in _L0_ffn_all.items() if k in ('W_gat', 'att_src', 'att_dst', 'b_gat', 'ln_gamma', 'ln_beta', 'W1', 'b1', 'W2', 'b2', 'edge_index')}
    del _L0_ffn_all

    def _L1_gnn_setup():
        import jax, jax.numpy as jnp
        import numpy as np
        N_NODES = 3125
        N_EDGES = 100000
        D_IN = 256
        N_BLOCKS = 4
        D_OUT = 256

        def _spmm(edge_src, edge_dst, edge_weight, feats, n_nodes):
            msgs = edge_weight[:, None] * feats[edge_src]
            return jax.ops.segment_sum(msgs, edge_dst, num_segments=n_nodes)
        key = jax.random.key(seed)
        ks = jax.random.split(key, 6)
        x = jax.random.normal(ks[0], (N_NODES, D_IN), dtype=jnp.float32)
        edge_src = jax.random.randint(ks[1], (N_EDGES,), 0, N_NODES, dtype=jnp.int32)
        edge_dst = jax.random.randint(ks[2], (N_EDGES,), 0, N_NODES, dtype=jnp.int32)
        edge_weight = jax.random.uniform(ks[3], (N_EDGES,), dtype=jnp.float32) / 32.0
        stdv_w = 1.0 / np.sqrt(D_OUT)
        shared_weight = jax.random.uniform(ks[4], (D_IN * N_BLOCKS, D_OUT), minval=-stdv_w, maxval=stdv_w, dtype=jnp.float32)
        stdv_b = 1.0 / np.sqrt(D_OUT)
        output_bias = jax.random.uniform(ks[5], (D_OUT,), minval=-stdv_b, maxval=stdv_b, dtype=jnp.float32)
        return {'x': x, 'edge_src': edge_src, 'edge_dst': edge_dst, 'edge_weight': edge_weight, 'shared_weight': shared_weight, 'output_bias': output_bias}
    _L1_gnn_all = _L1_gnn_setup()
    _L1_gnn_in = {k: v for k, v in _L1_gnn_all.items() if k in ('shared_weight', 'output_bias')}
    del _L1_gnn_all

    def _L1_mix_setup():
        import jax, jax.numpy as jnp
        import numpy as np
        A, Bc, Cc = (0.5, 1.0, 1.0)
        H = 8
        EPS = 1e-12

        def _normalize(t):
            n = jnp.linalg.norm(t, axis=-1, keepdims=True)
            return t / jnp.maximum(n, EPS)
        key = jax.random.key(seed)
        ks = jax.random.split(key, 5)
        B, N, C = (8, 64, 256)
        D = C // H
        x = jax.random.normal(ks[0], (B, N, C), dtype=jnp.float32)
        Wqkv = jax.random.normal(ks[1], (3 * H * D, C), dtype=jnp.float32) * 0.02
        bqkv = jnp.zeros((3 * H * D,), dtype=jnp.float32)
        Wproj = jax.random.normal(ks[2], (C, H * D), dtype=jnp.float32) * 0.02
        bproj = jnp.zeros((C,), dtype=jnp.float32)
        temperature = jnp.ones((1, H, 1, 1), dtype=jnp.float32)
        return {'x': x, 'Wqkv': Wqkv, 'bqkv': bqkv, 'Wproj': Wproj, 'bproj': bproj, 'temperature': temperature}
    _L1_mix_all = _L1_mix_setup()
    _L1_mix_in = {k: v for k, v in _L1_mix_all.items() if k in ('Wqkv', 'bqkv', 'Wproj', 'bproj', 'temperature')}
    del _L1_mix_all

    def _L1_ffn_setup():
        import jax, jax.numpy as jnp
        import numpy as np
        B, T, D, H, E = (16, 128, 256, 512, 8)
        key = jax.random.key(seed)
        ks = jax.random.split(key, 5)
        x = jax.random.normal(ks[0], (B, T, D), dtype=jnp.float32)
        gate_w = jax.random.normal(ks[1], (D, E), dtype=jnp.float32) * 0.02
        gate_b = jnp.zeros((E,), dtype=jnp.float32)
        W1 = jax.random.normal(ks[2], (E, D, H), dtype=jnp.float32) * 0.02
        b1 = jnp.zeros((E, H), dtype=jnp.float32)
        W2 = jax.random.normal(ks[3], (E, H, D), dtype=jnp.float32) * 0.02
        b2 = jnp.zeros((E, D), dtype=jnp.float32)
        return {'x': x, 'gate_w': gate_w, 'gate_b': gate_b, 'W1': W1, 'b1': b1, 'W2': W2, 'b2': b2}
    _L1_ffn_all = _L1_ffn_setup()
    _L1_ffn_in = {k: v for k, v in _L1_ffn_all.items() if k in ('gate_w', 'gate_b', 'W1', 'b1', 'W2', 'b2')}
    del _L1_ffn_all
    return {'x': x, 'src': src, 'dst': dst, 'edge_weight': edge_weight, 'L0_gnn_weight': _L0_gnn_in['weight'], 'L0_mix_Wq': _L0_mix_in['Wq'], 'L0_mix_Wk': _L0_mix_in['Wk'], 'L0_mix_Wv': _L0_mix_in['Wv'], 'L0_mix_Wm': _L0_mix_in['Wm'], 'L0_mix_W1': _L0_mix_in['W1'], 'L0_mix_W2': _L0_mix_in['W2'], 'L0_mix_g1': _L0_mix_in['g1'], 'L0_mix_b1': _L0_mix_in['b1'], 'L0_mix_g2': _L0_mix_in['g2'], 'L0_mix_b2': _L0_mix_in['b2'], 'L0_ffn_W_gat': _L0_ffn_in['W_gat'], 'L0_ffn_att_src': _L0_ffn_in['att_src'], 'L0_ffn_att_dst': _L0_ffn_in['att_dst'], 'L0_ffn_b_gat': _L0_ffn_in['b_gat'], 'L0_ffn_ln_gamma': _L0_ffn_in['ln_gamma'], 'L0_ffn_ln_beta': _L0_ffn_in['ln_beta'], 'L0_ffn_W1': _L0_ffn_in['W1'], 'L0_ffn_b1': _L0_ffn_in['b1'], 'L0_ffn_W2': _L0_ffn_in['W2'], 'L0_ffn_b2': _L0_ffn_in['b2'], 'L0_ffn_edge_index': _L0_ffn_in['edge_index'], 'L1_gnn_shared_weight': _L1_gnn_in['shared_weight'], 'L1_gnn_output_bias': _L1_gnn_in['output_bias'], 'L1_mix_Wqkv': _L1_mix_in['Wqkv'], 'L1_mix_bqkv': _L1_mix_in['bqkv'], 'L1_mix_Wproj': _L1_mix_in['Wproj'], 'L1_mix_bproj': _L1_mix_in['bproj'], 'L1_mix_temperature': _L1_mix_in['temperature'], 'L1_ffn_gate_w': _L1_ffn_in['gate_w'], 'L1_ffn_gate_b': _L1_ffn_in['gate_b'], 'L1_ffn_W1': _L1_ffn_in['W1'], 'L1_ffn_b1': _L1_ffn_in['b1'], 'L1_ffn_W2': _L1_ffn_in['W2'], 'L1_ffn_b2': _L1_ffn_in['b2']}

def reference(x, src, dst, edge_weight, L0_gnn_weight, L0_mix_Wq, L0_mix_Wk, L0_mix_Wv, L0_mix_Wm, L0_mix_W1, L0_mix_W2, L0_mix_g1, L0_mix_b1, L0_mix_g2, L0_mix_b2, L0_ffn_W_gat, L0_ffn_att_src, L0_ffn_att_dst, L0_ffn_b_gat, L0_ffn_ln_gamma, L0_ffn_ln_beta, L0_ffn_W1, L0_ffn_b1, L0_ffn_W2, L0_ffn_b2, L0_ffn_edge_index, L1_gnn_shared_weight, L1_gnn_output_bias, L1_mix_Wqkv, L1_mix_bqkv, L1_mix_Wproj, L1_mix_bproj, L1_mix_temperature, L1_ffn_gate_w, L1_ffn_gate_b, L1_ffn_W1, L1_ffn_b1, L1_ffn_W2, L1_ffn_b2):
    import jax
    import jax.numpy as jnp

    def _L0_gnn_ref(x, sources, targets, norm, weight):
        import jax, jax.numpy as jnp
        import numpy as np
        N = 6250
        E = 18750
        C = 256
        agg = x.at[targets].add(x[sources])
        h = norm * agg
        return h @ weight

    def _L0_mix_ref(x, Wq, Wk, Wv, Wm, W1, W2, g1, b1, g2, b2):
        import jax, jax.numpy as jnp
        import numpy as np
        NHEAD = 8
        ATT_EPS = 1e-06
        LN_EPS = 1e-05

        def _layernorm(x, g, b):
            mu = jnp.mean(x, axis=-1, keepdims=True)
            var = jnp.mean(jnp.square(x - mu), axis=-1, keepdims=True)
            return (x - mu) * jax.lax.rsqrt(var + LN_EPS) * g + b
        N, L, C = x.shape
        H = NHEAD
        D = C // H
        q = (x @ Wq).reshape(N, L, H, D)
        k = (x @ Wk).reshape(N, L, H, D)
        v = (x @ Wv).reshape(N, L, H, D)
        Q = jax.nn.elu(q) + 1.0
        K = jax.nn.elu(k) + 1.0
        v = v / L
        KV = jnp.einsum('nshd,nshv->nhdv', K, v)
        Z = 1.0 / (jnp.einsum('nlhd,nhd->nlh', Q, K.sum(axis=1)) + ATT_EPS)
        msg = jnp.einsum('nlhd,nhdv,nlh->nlhv', Q, KV, Z) * L
        msg = msg.reshape(N, L, C) @ Wm
        msg = _layernorm(msg, g1, b1)
        h = jnp.concatenate([x, msg], axis=-1) @ W1
        h = jax.nn.relu(h) @ W2
        msg = _layernorm(h, g2, b2)
        return x + msg

    def _L0_ffn_ref(x, W_gat, att_src, att_dst, b_gat, ln_gamma, ln_beta, W1, b1, W2, b2, edge_index):
        import jax, jax.numpy as jnp
        import numpy as np
        B, N, D = (16, 128, 256)
        NUM_EXPERTS, TOP_K, HEADS = (4, 2, 4)
        N_EDGES = 32768
        LN_EPS = 1e-05

        def _layernorm(x, g, b):
            mu = x.mean(-1, keepdims=True)
            var = ((x - mu) ** 2).mean(-1, keepdims=True)
            return (x - mu) * jax.lax.rsqrt(var + LN_EPS) * g + b

        def _forward(x, edge_index, W_gat, att_src, att_dst, b_gat, ln_gamma, ln_beta, W1, b1, W2, b2):
            Bc, Nc, Dc = x.shape
            M = Bc * Nc
            x_flat = x.reshape(M, Dc)
            h = (x_flat @ W_gat).reshape(M, HEADS, NUM_EXPERTS)
            loops = jnp.arange(M, dtype=edge_index.dtype)
            src = jnp.concatenate([edge_index[0], loops])
            dst = jnp.concatenate([edge_index[1], loops])
            a_src = (h * att_src).sum(-1)
            a_dst = (h * att_dst).sum(-1)
            e = jax.nn.leaky_relu(a_src[src] + a_dst[dst], negative_slope=0.2)
            e_max = jax.ops.segment_max(e, dst, num_segments=M)
            ee = jnp.exp(e - e_max[dst])
            denom = jax.ops.segment_sum(ee, dst, num_segments=M)
            alpha = ee / (denom[dst] + 1e-16)
            msg = h[src] * alpha[:, :, None]
            agg = jax.ops.segment_sum(msg, dst, num_segments=M).reshape(M, HEADS * NUM_EXPERTS) + b_gat
            scores = _layernorm(agg, ln_gamma, ln_beta).reshape(M, HEADS, NUM_EXPERTS).mean(1)
            scores = scores.reshape(Bc, Nc, NUM_EXPERTS)
            topk_s, topk_i = jax.lax.top_k(scores, TOP_K)
            w = jax.nn.softmax(topk_s, axis=-1)
            out = jnp.zeros_like(x)
            for ei in range(NUM_EXPERTS):
                g = jnp.where(topk_i == ei, w, 0.0).sum(-1)
                hh = jax.nn.gelu(x @ W1[ei] + b1[ei], approximate=False)
                out = out + g[..., None] * (hh @ W2[ei] + b2[ei])
            return out
        return _forward(x, edge_index, W_gat, att_src, att_dst, b_gat, ln_gamma, ln_beta, W1, b1, W2, b2)

    def _L1_gnn_ref(x, edge_src, edge_dst, edge_weight, shared_weight, output_bias):
        import jax, jax.numpy as jnp
        import numpy as np
        N_NODES = 3125
        N_EDGES = 100000
        D_IN = 256
        N_BLOCKS = 4
        D_OUT = 256

        def _spmm(edge_src, edge_dst, edge_weight, feats, n_nodes):
            msgs = edge_weight[:, None] * feats[edge_src]
            return jax.ops.segment_sum(msgs, edge_dst, num_segments=n_nodes)
        n_nodes, d_in = x.shape
        n_blocks = shared_weight.shape[0] // d_in
        feats = [x]
        cur = x
        for _ in range(n_blocks - 1):
            cur = _spmm(edge_src, edge_dst, edge_weight, cur, n_nodes)
            feats.append(cur)
        concat = jnp.concatenate(feats, axis=1)
        return concat @ shared_weight + output_bias

    def _L1_mix_ref(x, Wqkv, bqkv, Wproj, bproj, temperature):
        import jax, jax.numpy as jnp
        import numpy as np
        A, Bc, Cc = (0.5, 1.0, 1.0)
        H = 8
        EPS = 1e-12

        def _normalize(t):
            n = jnp.linalg.norm(t, axis=-1, keepdims=True)
            return t / jnp.maximum(n, EPS)
        B, N, C = x.shape
        D = C // H
        scale = float(D) ** 0.25
        qkv = (x @ Wqkv.T + bqkv).reshape(B, N, 3, H, D)
        qkv = jnp.transpose(qkv, (2, 0, 3, 1, 4))
        q, k, v = (qkv[0], qkv[1], qkv[2])
        q = q * scale
        v1 = jnp.concatenate([jnp.ones((B, H, N, 1), dtype=v.dtype), v], axis=-1)
        qn = _normalize(q) * (scale * temperature)
        kn = _normalize(k) * scale
        vN = v1 / N
        kv_mod = jnp.einsum('bhni,bhnj,bhne->bhije', kn, kn, vN)
        kv = jnp.einsum('bhnd,bhne->bhde', kn, vN)
        vsum = jnp.sum(vN, axis=-2)[:, :, None, :]
        y = A * jnp.einsum('bhni,bhnj,bhije->bhne', qn, qn, kv_mod) + scale ** 2 * Bc * jnp.einsum('bhnd,bhde->bhne', qn, kv) + scale ** 4 * Cc * vsum
        y_norm, y = (y[..., :1], y[..., 1:])
        y = y / y_norm
        out = jnp.transpose(y, (0, 2, 1, 3)).reshape(B, N, H * D)
        return out @ Wproj.T + bproj

    def _L1_ffn_ref(x, gate_w, gate_b, W1, b1, W2, b2):
        import jax, jax.numpy as jnp
        import numpy as np
        B, T, D, H, E = (16, 128, 256, 512, 8)
        Bb, Tt, Dd = x.shape
        Ee = gate_w.shape[1]
        xf = x.reshape(-1, Dd)
        N = xf.shape[0]
        logits = xf @ gate_w + gate_b
        probs = jax.nn.softmax(logits, axis=-1)
        top2_vals, top2_idx = jax.lax.top_k(probs, 2)
        cw = jnp.zeros((N, Ee), dtype=xf.dtype).at[jnp.arange(N)[:, None], top2_idx].add(top2_vals)

        def step(acc, params):
            w1, bb1, w2, bb2, we = params
            h = jax.nn.gelu(xf @ w1 + bb1, approximate=False)
            y = h @ w2 + bb2
            return (acc + we[:, None] * y, None)
        out, _ = jax.lax.scan(step, jnp.zeros_like(xf), (W1, b1, W2, b2, cw.T))
        return out.reshape(Bb, Tt, Dd)
    deg = jnp.maximum(jax.ops.segment_sum(jnp.ones(dst.shape, jnp.float32), dst, num_segments=3125), 1.0)
    deg_isqrt = deg ** (-0.5)
    xn = _layernorm(x, axis=-1)
    x = x + _L0_gnn_ref(xn, src, dst, deg_isqrt[:, None], L0_gnn_weight) + _L0_mix_ref(xn[None], L0_mix_Wq, L0_mix_Wk, L0_mix_Wv, L0_mix_Wm, L0_mix_W1, L0_mix_W2, L0_mix_g1, L0_mix_b1, L0_mix_g2, L0_mix_b2)[0]
    x = x + _L0_ffn_ref(_layernorm(x, axis=-1)[None], L0_ffn_W_gat, L0_ffn_att_src, L0_ffn_att_dst, L0_ffn_b_gat, L0_ffn_ln_gamma, L0_ffn_ln_beta, L0_ffn_W1, L0_ffn_b1, L0_ffn_W2, L0_ffn_b2, L0_ffn_edge_index)[0]
    xn = _layernorm(x, axis=-1)
    x = x + _L1_gnn_ref(xn, src, dst, edge_weight, L1_gnn_shared_weight, L1_gnn_output_bias) + _L1_mix_ref(xn[None], L1_mix_Wqkv, L1_mix_bqkv, L1_mix_Wproj, L1_mix_bproj, L1_mix_temperature)[0]
    x = x + _L1_ffn_ref(_layernorm(x, axis=-1)[None], L1_ffn_gate_w, L1_ffn_gate_b, L1_ffn_W1, L1_ffn_b1, L1_ffn_W2, L1_ffn_b2)[0]
    return x

_drawn_inputs = setup_inputs


def setup_inputs(seed=0):
    import zlib

    import numpy as np

    out = dict(_drawn_inputs(seed))
    spreads = {'L0_mix_g1': (1.0, 0.2),
     'L0_mix_b1': (0.0, 0.1),
     'L0_mix_g2': (1.0, 0.2),
     'L0_mix_b2': (0.0, 0.1),
     'L0_ffn_b_gat': (0.0, 0.1),
     'L0_ffn_ln_gamma': (1.0, 0.2),
     'L0_ffn_ln_beta': (0.0, 0.1),
     'L0_ffn_b1': (0.0, 0.391),
     'L0_ffn_b2': (0.0, 0.293),
     'L1_mix_bqkv': (0.0, 0.666),
     'L1_mix_bproj': (0.0, 0.1),
     'L1_mix_temperature': (1.0, 0.6),
     'L1_ffn_gate_b': (0.0, 0.8),
     'L1_ffn_b1': (0.0, 0.8),
     'L1_ffn_b2': (0.0, 0.8)}
    factors = {'edge_weight': 7.063,
     'L0_ffn_att_src': 4.065,
     'L0_ffn_att_dst': 4.462,
     'L1_gnn_output_bias': 4.024,
     'L1_mix_Wqkv': 4.576,
     'L1_mix_Wproj': 3.405,
     'L1_ffn_gate_w': 5.376,
     'L1_ffn_W1': 7.537,
     'L1_ffn_W2': 7.037}
    for name, (base, spread) in spreads.items():
        noise = np.random.default_rng([zlib.crc32(name.encode()), seed]).standard_normal(out[name].shape)
        drawn = base * np.exp(spread * noise) if base else spread * noise
        out[name] = jnp.asarray(drawn.astype(out[name].dtype))
    for name, factor in factors.items():
        out[name] = (out[name] * factor).astype(out[name].dtype)
    return out
```

```python
from contextlib import ExitStack

import concourse.bass as bass
from concourse import mybir
from concourse.alu_op_type import AluOpType as ALU

ACT = mybir.ActivationFunctionType
AX = mybir.AxisListType
F32 = mybir.dt.float32
BF16 = mybir.dt.bfloat16
I32 = mybir.dt.int32

P = 128
N = 3125
C = 256
NT = -(-N // P)
NP = NT * P
TI = 5
TURNS = NT // TI
W = TI * P
HALF = W // 2
LAST = N - (NT - 1) * P
LN_EPS = 1e-5
BUCKETS = NT + 1

E_MAIN = 50000
E_GAT = 32768
GROUP = 16


def chunk_bound(edges):
    return -(-(-(-(edges + NT * (P - 1)) // P)) // GROUP) * GROUP


CH_MAIN = chunk_bound(E_MAIN)
CH_GAT = chunk_bound(E_GAT)
BIG = 1e30
LANE = 1


def gps_kernel(nc, a, out):
    HEADS0, HD0 = 8, 32
    EXP0, EXP1 = 4, 8
    HID = 512
    GH = 4
    GE = 4
    R2 = 17
    FG = R2 + 2
    FC = -(-FG * 32 // P)
    SCALE1 = float(32) ** 0.25

    ctx = ExitStack()
    with ctx:
        def sb(name, shape, dt=F32):
            return ctx.enter_context(nc.sbuf_tensor(name, shape, dt))

        def sem(name):
            return ctx.enter_context(nc.semaphore(name))

        def dram(name, shape, dt=F32):
            return nc.dram_tensor(name, shape, dt, kind="Internal").ap()

        xn_d = [dram(f"xn_d{i}", [NP, C]) for i in range(3)]
        cur_d = [dram(f"cur_d{i}", [NP, C]) for i in range(3)]
        src_tab_d = dram("src_tab_d", [NP, 32])
        dst_tab_d = dram("dst_tab_d", [NP, 8])
        PADROWS = 8
        rec_main_d = dram("rec_main_d", [P * (CH_MAIN + PADROWS), 4], I32)
        rec_gat_d = dram("rec_gat_d", [P * (CH_GAT + PADROWS), 4], I32)

        X = sb("X", [P, NT * C])
        ACC = sb("ACC", [P, NT * 257])
        rec_main = sb("rec_main", [P, CH_MAIN * 4], I32)
        rec_gat = sb("rec_gat", [P, CH_GAT * 4], I32)
        ident = sb("ident", [P, P])
        ident_b = sb("ident_b", [P, 4 * P], BF16)
        iota_row = sb("iota_row", [P, P])
        upper = sb("upper", [P, P])
        ones = sb("ones", [P, P])
        head_mask = sb("head_mask", [P, P])
        valid = sb("valid", [P, NT])
        eps_ln = sb("eps_ln", [P, 1])
        WT = sb("WT", [P, 16384])
        WS = sb("WS", [P, 2048])
        ROWS = sb("ROWS", [P, 2560])
        XS = sb("XS", [P, TI * C])
        XT = sb("XT", [P, 2 * W])
        BUF = sb("BUF", [P, 11520])
        bn = sb("bn", [P, NT * 6])
        mv = sb("mv", [P, NT * 2])
        sd = sb("sd", [P, NT])
        rs = sb("rs", [P, NT])
        gates = sb("gates", [P, NT * 8])
        tile_main = sb("tile_main", [1, CH_MAIN], I32)
        tile_gat = sb("tile_gat", [1, CH_GAT], I32)
        ib = [sb("ibA", [P, GROUP // 2], I32), sb("ibB", [P, GROUP // 2], I32)]
        ps = ctx.enter_context(nc.psum_tensor("ps", [P, 8 * 512], F32))

        def bank(b, n=512, off=0, rows=P):
            return ps[0:rows, b * 512 + off:b * 512 + off + n]

        def v3(ap, b):
            return ap.rearrange("p (a b) -> p a b", b=b)

        XS3 = v3(XS[:, :], C)
        XT3 = v3(XT[:, :], W)

        consts_ok = sem("consts_ok")
        x_in = sem("x_in")
        pool_waits = sem("pool_waits")
        round_pe, round_act, round_dve = sem("round_pe"), sem("round_act"), sem("round_dve")
        rounds = {"pe": round_pe, "act": round_act, "dve": round_dve}

        def rendezvous(e, who, n):
            e.drain().then_inc(rounds[who], 1)
            for other, s in rounds.items():
                if other != who:
                    e.wait_ge(s, n)

        def pool_wait(e, q, value):
            e.wait_ge(q, value)
            e.sem_inc(pool_waits, 1)

        def tiles_of(table, k):
            return nc.values_load_multi_w_load_instructions(
                table[0:1, bass.ds(k * GROUP, GROUP)], [mybir.EngineType.DVE], min_val=0, max_val=NT - 1,
                skip_runtime_bounds_check_because="the sort writes counts of buckets, 0 to NT - 1")[1]

        pe_waits = sem("pe_waits")

        R = {}
        count = 0
        for name, n in (("mixA", TURNS), ("mixA_end", 1), ("mixB", TURNS), ("hop0", 1), ("gnn0", TURNS),
                        ("lnb", 1), ("gatp", TURNS), ("gatp_end", 1), ("gatA", 1), ("gatB", 1), ("ffn0", TURNS),
                        ("lnc", 1), ("hop1", 1), ("hop2", 1), ("hop3", 1), ("gnn1", 4 * TURNS), ("m1w", 1),
                        ("m1A", TURNS), ("m1A_end", 1), ("m1B", TURNS), ("lnd", 1), ("gate1", TURNS), ("gate1_end", 1),
                        ("ffn1", TURNS)):
            R[name] = count
            count += n

        class Sort:
            def __init__(s, name, edges, cols, per, turns, chunks, rec_sb, rec_d, tiles, at):
                s.name, s.edges, s.cols, s.per, s.turns, s.chunks = name, edges, cols, per, turns, chunks
                assert cols == 2 * per * turns and P * cols >= edges
                s.rec_sb, s.rec_d, s.tiles = rec_sb, rec_d, tiles
                s.rec = WT[:, at:at + cols * 4].bitcast(I32)
                s.pos = WT[:, at + cols * 4:at + cols * 5].bitcast(I32)
                s.ids = [sb(f"{name}_ids{i}", [P, per], I32) for i in range(2)]
                s.rows = [sb(f"{name}_rows{i}", [P, per * 4], I32) for i in range(2)]
                s.loaded = sem(name + "_loaded")
                s.cleared = sem(name + "_cleared")
                s.count_ok = sem(name + "_count_ok")
                s.sums_ok = sem(name + "_sums_ok")
                s.pos_ok = sem(name + "_pos_ok")
                s.slot = sem(name + "_slot")
                s.scat = [sem(f"{name}_scat{i}") for i in range(2)]
                s.back = sem(name + "_back")

        main = Sort("main", E_MAIN, 392, 14, 14, CH_MAIN, rec_main, rec_main_d, tile_main, 10240)
        gat = Sort("gat", E_GAT, 256, 16, 8, CH_GAT, rec_gat, rec_gat_d, tile_gat, 12288)
        SCOLS = 392
        s_dst = BUF[:, 0:SCOLS].bitcast(I32)
        s_tile = BUF[:, 400:400 + SCOLS].bitcast(I32)
        s_tilef = BUF[:, 800:800 + SCOLS]
        s_mask = BUF[:, 1200:1200 + SCOLS]
        s_scan = BUF[:, 1600:1600 + SCOLS]
        s_rank = BUF[:, 2000:2000 + SCOLS]
        s_tmp = BUF[:, 2400:2400 + SCOLS]
        s_src = BUF[:, 2800:2800 + SCOLS].bitcast(I32)
        s_w = BUF[:, 3200:3200 + SCOLS]
        s_tmpi = BUF[:, 3600:3600 + SCOLS].bitcast(I32)
        s_cnt = BUF[:, 4000:4000 + BUCKETS]
        s_base = BUF[:, 4032:4032 + BUCKETS]
        s_chk = BUF[:, 4064:4064 + BUCKETS]
        s_chki = BUF[:, 4096:4096 + BUCKETS].bitcast(I32)
        s_end = BUF[:, 4128:4128 + BUCKETS]
        s_iota = BUF[:, 4160:4160 + CH_MAIN]
        s_tidx = BUF[:, 4600:4600 + CH_MAIN]
        zeros = BUF[:, 5200:5200 + (CH_MAIN + PADROWS) * 4].bitcast(I32)
        sort_free = sem("sort_free")

        def sort_loads(sp, s, src, dst, w):
            full = s.edges // s.cols
            rest = s.edges - full * s.cols
            todo = [(s_src, src), (s_dst, dst)] + ([(s_w, w)] if w is not None else [])
            n = 0
            for tile, ap in todo:
                sp.dma_start(tile[0:full, 0:s.cols], ap[0:full * s.cols].rearrange("(p c) -> p c", c=s.cols)
                             ).then_inc(s.loaded, 16)
                n += 16
                if rest:
                    sp.dma_start(tile[full:full + 1, 0:rest], ap[full * s.cols:s.edges].rearrange("(p c) -> p c", p=1)
                                 ).then_inc(s.loaded, 16)
                    n += 16
            return n

        n_main = 96
        n_gat = 32

        def sort_dve(e, s, n_loaded, weighted):
            cols = s.cols
            dst, tile_i, tilef = s_dst[:, 0:cols], s_tile[:, 0:cols], s_tilef[:, 0:cols]
            mask, scan, rank, tmp = s_mask[:, 0:cols], s_scan[:, 0:cols], s_rank[:, 0:cols], s_tmp[:, 0:cols]
            tmpi = s_tmpi[:, 0:cols]
            e.wait_ge(s.loaded, n_loaded)
            e.tensor_scalar(tile_i, dst, 7, None, ALU.arith_shift_right)
            e.memset(rank, 0.0)
            e.drain()
            e.tensor_copy(tilef, tile_i)
            e.drain()
            for t in range(BUCKETS):
                e.tensor_scalar(mask, tilef, float(t), None, ALU.is_equal)
                e.drain()
                e.tensor_tensor_scan(scan, mask, mask, 0.0, ALU.add, ALU.max)
                e.drain()
                e.tensor_copy(s_cnt[:, t:t + 1], scan[:, cols - 1:cols])
                e.tensor_tensor(tmp, mask, scan, ALU.mult)
                e.drain()
                e.tensor_tensor(rank, rank, tmp, ALU.add)
                e.drain()
            e.drain().then_inc(s.count_ok, 1)
            e.wait_ge(s.sums_ok, 1)
            e.tensor_scalar(s_chk, bank(7, BUCKETS, 64), float(P - 1), None, ALU.add)
            e.tensor_copy(s_base, bank(7, BUCKETS, 0))
            e.drain()
            e.tensor_copy(s_chki, s_chk)
            e.drain()
            e.tensor_scalar(s_chki, s_chki, 7, None, ALU.arith_shift_right)
            e.drain()
            e.tensor_copy(s_chk, s_chki)
            e.drain()
            e.tensor_tensor_scan(s_end, s_chk, s_chk, 0.0, ALU.add, ALU.max)
            e.drain()
            e.tensor_tensor(s_chk, s_end, s_chk, ALU.subtract)
            e.drain()
            e.tensor_scalar(s_chk, s_chk, float(P), -1.0, ALU.mult, ALU.add)
            e.drain()
            e.tensor_tensor(s_base, s_base, s_chk, ALU.add)
            e.drain()
            for t in range(BUCKETS):
                e.tensor_scalar(mask, tilef, float(t), s_base[:, t:t + 1], ALU.is_equal, ALU.mult)
                e.drain()
                e.tensor_tensor(rank, rank, mask, ALU.add)
                e.drain()
            e.tensor_copy(tmpi, rank)
            e.drain()
            e.tensor_scalar(tile_i, tmpi, 7, None, ALU.arith_shift_right)
            e.tensor_scalar(tmpi, tmpi, 127, None, ALU.bitwise_and)
            e.drain()
            e.tensor_copy(tmp, tile_i)
            e.tensor_copy(scan, tmpi)
            e.drain()
            e.scalar_tensor_tensor(tmp, scan, float(s.chunks + PADROWS), tmp, ALU.mult, ALU.add)
            e.drain()
            e.tensor_copy(s.pos[:, :], tmp)
            rec = v3(s.rec[:, :], 4)
            recf = v3(s.rec[:, :].bitcast(F32), 4)
            e.tensor_copy(rec[:, :, 0], s_src[:, 0:cols])
            e.tensor_scalar(tile_i, dst, 127, None, ALU.bitwise_and)
            e.drain()
            e.tensor_scalar(mask, tilef, float(NT), None, ALU.is_lt)
            e.tensor_copy(recf[:, :, LANE], tile_i)
            if weighted:
                e.tensor_copy(recf[:, :, 2], s_w[:, 0:cols])
            else:
                e.tensor_copy(rec[:, :, 2], dst)
            e.drain()
            e.tensor_copy(recf[:, :, 3], mask)
            e.memset(s_tidx[0:1, 0:s.chunks], 0.0)
            e.drain()
            for t in range(NT):
                e.scalar_tensor_tensor(s_tidx[0:1, 0:s.chunks], s_iota[0:1, 0:s.chunks], s_end[0:1, t:t + 1],
                                       s_tidx[0:1, 0:s.chunks], ALU.is_ge, ALU.add)
                e.drain()
            e.tensor_scalar(s_tidx[0:1, 0:s.chunks], s_tidx[0:1, 0:s.chunks], float(NT - 1), None, ALU.min)
            e.drain()
            e.tensor_copy(s.tiles[0:1, :], s_tidx[0:1, 0:s.chunks])
            e.drain().then_inc(s.pos_ok, 1)

        def sort_pe(pe, s):
            pe.wait_ge(s.count_ok, 1)
            pe.matmul(bank(7, BUCKETS, 0), upper[:, :], s_cnt, start=True, stop=True)
            pe.matmul(bank(7, BUCKETS, 64), ones[:, :], s_cnt, start=True, stop=True).then_inc(s.sums_ok, 1)

        def sort_pool(e, s):
            e.wait_ge(s.pos_ok, 1)
            pool_wait(e, s.cleared, 16)
            dest = s.rec_d
            with e.Fori(0, s.turns) as k:
                for half in range(2):
                    col = k * (2 * s.per) + half * s.per
                    e.tensor_copy(s.ids[half][:, :], s.pos[:, bass.ds(col, s.per)])
                    e.tensor_copy(s.rows[half][:, :], s.rec[:, bass.ds(col * 4, s.per * 4)]).then_inc(s.slot, 1)
                    pool_wait(e, s.slot, k * 2 + (half + 1))
                    for j in range(s.per):
                        e.indirect_dma_start(dest, bass.IndirectOffsetOnAxis(ap=s.ids[half][:, j:j + 1], axis=0),
                                             s.rows[half][:, 4 * j:4 * j + 4], None).then_inc(s.scat[half], 16)
                for half in range(2):
                    e.wait_ge(s.scat[half], (k + 1) * (16 * s.per))

        class Norm:
            def __init__(s, name, table):
                s.table = table
                s.var_ok, s.sd_ok, s.xn_ok, s.out = (sem(f"{name}_{x}") for x in ("var_ok", "sd_ok", "xn_ok", "out"))

        norms = [Norm("ln0", xn_d[0]), Norm("ln1", xn_d[1]), Norm("ln2", xn_d[2]), Norm("ln3", xn_d[0])]

        def norm_dve(e, s):
            with e.Fori(0, NT) as t:
                e.bn_stats(bn[:, bass.ds(t * 6, 6)], X[:, bass.ds(t * C, C)])
            e.drain()
            for t in range(NT):
                e.bn_aggr(mv[:, t * 2:t * 2 + 2], bn[:, t * 6:t * 6 + 6])
            e.drain().then_inc(s.var_ok, 1)
            e.wait_ge(s.sd_ok, 1)
            e.reciprocal(rs[:, :], sd[:, :])
            e.drain()
            with e.Fori(0, NT) as t:
                e.tensor_scalar(ACC[:, bass.ds(t * 257, C)], X[:, bass.ds(t * C, C)], mv[:, bass.ds(t * 2, 1)],
                                rs[:, bass.ds(t, 1)], ALU.subtract, ALU.mult)
            e.drain().then_inc(s.xn_ok, 1)

        def norm_act(e, s):
            e.wait_ge(s.var_ok, 1)
            e.activation(sd[:, :], v3(mv[:, :], 2)[:, :, 1], ACT.Sqrt, bias=eps_ln[:, 0:1]).then_inc(s.sd_ok, 1)

        def acc_to_dram(sp, table, done):
            sp.dma_start(table.rearrange("(t p) c -> p t c", p=P), v3(ACC[:, :], 257)[:, :, 0:C]).then_inc(done, 16)

        class Front:
            xs_in, xt_tp, xt_out = sem("xs_in"), sem("xt_tp"), sem("xt_out")
            turns_before = loads = 0

            def __init__(s, loads=True):
                s.before, s.loads_before = Front.turns_before, Front.loads
                Front.turns_before += TURNS
                Front.loads += TURNS if loads else 0

            def tiles(s, turn, n):
                return turn * TI + (s.before * TI + n)

            def loaded(s, turn):
                return turn * 16 + (s.loads_before * 16 + 16)

        def rows_of(table, s):
            return table[bass.ds(s * W, W), :].rearrange("(j p) c -> p j c", p=P)

        def front_sp(sp, f, table, more=()):
            sp.dma_start(XS3, table[0:W, :].rearrange("(j p) c -> p j c", p=P)).then_inc(f.xs_in, 16)
            with sp.Fori(1, TURNS) as s:
                sp.wait_ge(f.xt_tp, f.tiles(s, 0))
                for q, per in more:
                    sp.wait_ge(q, s * per)
                sp.dma_start(XS3, rows_of(table, s)).then_inc(f.xs_in, 16)

        def front_pe(pe, f, s):
            for j in range(TI):
                if j == 0:
                    pe.wait_ge(f.xs_in, f.loaded(s))
                if j >= 2:
                    pe.wait_ge(f.xt_out, f.tiles(s, j - 1))
                for c in range(2):
                    mm = pe.transpose(bank(j % 2, P, c * P), XS3[:, j, c * P:(c + 1) * P], ident[:, :])
                mm.then_inc(f.xt_tp, 1)

        def front_act(e, f, s):
            for j in range(TI):
                e.wait_ge(f.xt_tp, f.tiles(s, j + 1))
                e.activation(XT3[:, :, j * P:(j + 1) * P], v3(bank(j % 2, 2 * P), P), ACT.Copy).then_inc(f.xt_out, 1)

        fronts = {n: Front(n != "fg") for n in ("fa", "fb", "fg", "fp", "ff", "f0", "f1", "f2", "f3", "fm", "fn",
                                                "fq", "fe")}

        wk_wv = v3(WT[:, 0:1024], 512)
        wq0 = v3(WT[:, 1024:1536], 256)
        wm0 = v3(WT[:, 1536:2048], 256)
        w1m = v3(WT[:, 2048:4096], 512)
        w2m = v3(WT[:, 4096:5120], 256)
        wg0 = v3(WT[:, 5120:5632], 256)
        g1r, b1r, g2r, b2r = (ROWS[:, i * C:(i + 1) * C] for i in range(4))
        w_in0 = sem("w_in0")

        MN = BUF[:, 0:TI * C]
        EX = BUF[:, 1280:1280 + TI * C]
        KS = BUF[:, 2560:2560 + TI * C]
        VS = BUF[:, 3840:3840 + TI * 258]
        KR = BUF[:, 5200:5200 + TI * C]
        KVA = WS[:, 0:258]
        KVB = WS[:, 260:516]
        ZB = WS[:, 516:772]
        VALS = WS[:, 780:785]
        kv_mm, kv_mn, kv_ex, ks_ok, vs_ok, kva_mm = (sem("kv_" + x) for x in ("mm", "mn", "ex", "ks", "vs", "acc"))
        vals_ok = sem("vals_ok")

        def mixA_pe(pe, s):
            f = fronts["fa"]
            front_pe(pe, f, s)
            for j in range(TI):
                pe.wait_ge(f.xt_out, f.tiles(s, j + 1))
                if j >= 3:
                    pe.wait_ge(vs_ok, s * TI + (j - 2))
                for c in range(2):
                    mm = pe.matmul(bank(2 + j % 3), XT3[:, c, j * P:(j + 1) * P], wk_wv[:, c, :],
                                   start=(c == 0), stop=(c == 1))
                mm.then_inc(kv_mm, 1)
            for j in range(TI):
                pe.wait_ge(ks_ok, s * TI + (j + 1))
                pe.wait_ge(vs_ok, s * TI + (j + 1))
                for h in range(2):
                    mm = pe.matmul(bank(5 + h, 129), KS[:, j * C + h * P:j * C + (h + 1) * P],
                                   VS[:, j * 258 + h * 129:j * 258 + (h + 1) * 129],
                                   start=(j == 0), stop=(j == TI - 1))
            mm.then_inc(kva_mm, 1)

        def mixA_act(e, s):
            front_act(e, fronts["fa"], s)
            for j in range(TI):
                if j == 0:
                    e.wait_ge(vals_ok, s + 1)
                e.wait_ge(kv_mm, s * TI + (j + 1))
                e.activation(KR[:, j * C:(j + 1) * C], bank(2 + j % 3, C), ACT.Copy)
                e.activation(v3(VS[:, j * 258:(j + 1) * 258], 129)[:, :, 0:P], v3(bank(2 + j % 3, C, C), P),
                             ACT.Copy, scale=VALS[:, j:j + 1])
                e.activation(v3(VS[:, j * 258:(j + 1) * 258], 129)[:, :, P:P + 1], v3(ones[:, 0:2], 1),
                             ACT.Copy, scale=VALS[:, j:j + 1])
                e.drain().then_inc(vs_ok, 1)
            for j in range(TI):
                e.wait_ge(kv_mn, s * TI + (j + 1))
                e.activation(EX[:, j * C:(j + 1) * C], MN[:, j * C:(j + 1) * C], ACT.Exp).then_inc(kv_ex, 1)

        def mixA_dve(e, s):
            e.tensor_copy(VALS, valid[:, bass.ds(s * TI, TI)]).then_inc(vals_ok, 1)
            for j in range(TI):
                e.wait_ge(vs_ok, s * TI + (j + 1))
                e.tensor_scalar(MN[:, j * C:(j + 1) * C], KR[:, j * C:(j + 1) * C], 0.0, None, ALU.min
                                ).then_inc(kv_mn, 1)
            for i in range(TI):
                e.wait_ge(kv_ex, s * TI + (i + 1))
                e.scalar_tensor_tensor(KS[:, i * C:(i + 1) * C], KR[:, i * C:(i + 1) * C], 0.0,
                                       EX[:, i * C:(i + 1) * C], ALU.max, ALU.add).then_inc(ks_ok, 1)
            e.wait_ge(kva_mm, s + 1)
            for h in range(2):
                e.tensor_tensor(KVA[:, h * 129:(h + 1) * 129], bank(5 + h, 129), KVA[:, h * 129:(h + 1) * 129], ALU.add)

        QN = BUF[:, 0:4 * HALF]
        QE = BUF[:, 1280:1280 + 4 * HALF]
        QT = v3(BUF[:, 2560:2560 + 2 * W], W)
        RD = BUF[:, 0:4 * HALF]
        MT = v3(BUF[:, 3840:3840 + 2 * W], W)
        LM = BUF[:, 5120:5120 + TI * C]
        XM = v3(BUF[:, 6400:6400 + 2 * W], W)
        HT = BUF[:, 7680:7680 + 4 * W]
        (q_mm, q_mn, q_ex, q_ok, nd_mm, mt_ok, m_mm, m_var, m_sd, lm_ok, lm_tp, xm_ok, h_mm, ht_ok, y_mm, y_var,
         y_sd, xb_ok) = (sem("b_" + x) for x in (
             "q_mm", "q_mn", "q_ex", "q_ok", "nd_mm", "mt_ok", "m_mm", "m_var", "m_sd", "lm_ok", "lm_tp", "xm_ok",
             "h_mm", "ht_ok", "y_mm", "y_var", "y_sd", "xb_ok"))
        NUMBANK = (6, 7, 0, 1)

        def mixB_pe(pe, s):
            f = fronts["fb"]
            front_pe(pe, f, s)
            pe.wait_ge(f.xt_out, f.tiles(s, TI))
            for i in range(4):
                mc, hf = i // 2, i % 2
                for c in range(2):
                    mm = pe.matmul(bank(2 + i, HALF), wq0[:, c, mc * P:(mc + 1) * P],
                                   XT3[:, c, hf * HALF:(hf + 1) * HALF], start=(c == 0), stop=(c == 1))
                mm.then_inc(q_mm, 1)
            for i in range(4):
                mc, hf = i // 2, i % 2
                pe.wait_ge(q_ok, s * 4 + (i + 1))
                q = QT[:, mc, hf * HALF:(hf + 1) * HALF]
                pe.matmul(bank(NUMBANK[i], HALF), KVB[:, mc * P:(mc + 1) * P], q, start=True, stop=True)
                pe.matmul(bank(2 + i, HALF), ZB[:, mc * P:(mc + 1) * P], q, start=True, stop=True).then_inc(nd_mm, 1)
            pe.wait_ge(mt_ok, s + 1)
            for j in range(TI):
                for c in range(2):
                    mm = pe.matmul(bank(2 + j, C), MT[:, c, j * P:(j + 1) * P], wm0[:, c, :],
                                   start=(c == 0), stop=(c == 1))
                mm.then_inc(m_mm, 1)
            for j in range(TI):
                if j == 0:
                    pe.wait_ge(lm_ok, s + 1)
                if j >= 2:
                    pe.wait_ge(xm_ok, s * TI + (j - 1))
                for c in range(2):
                    mm = pe.transpose(bank(j % 2, P, c * P), LM[:, j * C + c * P:j * C + (c + 1) * P], ident[:, :])
                mm.then_inc(lm_tp, 1)
            pe.wait_ge(xm_ok, s * TI + TI)
            for i in range(8):
                mc, hf = i // 2, i % 2
                if i >= 6:
                    pe.wait_ge(ht_ok, s * 8 + (i - 5))
                for c in range(4):
                    src = XT3 if c < 2 else XM
                    mm = pe.matmul(bank(2 + i % 6, HALF), w1m[:, c, mc * P:(mc + 1) * P],
                                   src[:, c % 2, hf * HALF:(hf + 1) * HALF], start=(c == 0), stop=(c == 3))
                mm.then_inc(h_mm, 1)
            pe.wait_ge(ht_ok, s * 8 + 8)
            for j in range(TI):
                for c in range(4):
                    mm = pe.matmul(bank(2 + j, C), HT[:, c * W + j * P:c * W + (j + 1) * P], w2m[:, c, :],
                                   start=(c == 0), stop=(c == 3))
                mm.then_inc(y_mm, 1)

        def mixB_act(e, s):
            front_act(e, fronts["fb"], s)
            for i in range(4):
                e.wait_ge(q_mn, s * 4 + (i + 1))
                e.activation(QE[:, i * HALF:(i + 1) * HALF], QN[:, i * HALF:(i + 1) * HALF], ACT.Exp).then_inc(q_ex, 1)
            e.wait_ge(m_var, s + 1)
            e.activation(sd[:, 0:TI], v3(mv[:, 0:2 * TI], 2)[:, :, 1], ACT.Sqrt, bias=eps_ln[:, 0:1]).then_inc(m_sd, 1)
            for j in range(TI):
                e.wait_ge(lm_tp, s * TI + (j + 1))
                e.activation(XM[:, :, j * P:(j + 1) * P], v3(bank(j % 2, 2 * P), P), ACT.Copy).then_inc(xm_ok, 1)
            for i in range(8):
                mc, hf = i // 2, i % 2
                e.wait_ge(h_mm, s * 8 + (i + 1))
                e.activation(HT[:, mc * W + hf * HALF:mc * W + (hf + 1) * HALF], bank(2 + i % 6, HALF), ACT.Relu
                             ).then_inc(ht_ok, 1)
            e.wait_ge(y_var, s + 1)
            e.activation(sd[:, 0:TI], v3(mv[:, 0:2 * TI], 2)[:, :, 1], ACT.Sqrt, bias=eps_ln[:, 0:1]).then_inc(y_sd, 1)

        def norm_five(e, s, mm, var, sdq, g, b):
            for j in range(TI):
                e.wait_ge(mm, s * TI + (j + 1))
                e.bn_stats(bn[:, j * 6:(j + 1) * 6], bank(2 + j, C))
            e.drain()
            for j in range(TI):
                e.bn_aggr(mv[:, 2 * j:2 * j + 2], bn[:, j * 6:(j + 1) * 6])
            e.drain().then_inc(var, 1)
            e.wait_ge(sdq, s + 1)
            e.reciprocal(rs[:, 0:TI], sd[:, 0:TI])
            e.drain()
            for j in range(TI):
                e.tensor_scalar(LM[:, j * C:(j + 1) * C], bank(2 + j, C), mv[:, 2 * j:2 * j + 1], rs[:, j:j + 1],
                                ALU.subtract, ALU.mult)
            e.drain()
            lm3 = v3(LM, C)
            e.tensor_tensor(lm3, lm3, g.rearrange("p (o c) -> p o c", o=1).to_broadcast([P, TI, C]), ALU.mult)
            e.drain()
            e.tensor_tensor(lm3, lm3, b.rearrange("p (o c) -> p o c", o=1).to_broadcast([P, TI, C]), ALU.add)
            e.drain()

        def mixB_dve(e, s):
            e.wait_ge(Front.xs_in, fronts["fb"].loaded(s))
            e.tensor_tensor(X[:, bass.ds(s * (TI * C), TI * C)], X[:, bass.ds(s * (TI * C), TI * C)], XS[:, :], ALU.add
                            ).then_inc(xb_ok, 1)
            for i in range(4):
                e.wait_ge(q_mm, s * 4 + (i + 1))
                e.tensor_scalar(QN[:, i * HALF:(i + 1) * HALF], bank(2 + i, HALF), 0.0, None, ALU.min).then_inc(q_mn, 1)
            for i in range(4):
                e.wait_ge(q_ex, s * 4 + (i + 1))
                e.scalar_tensor_tensor(QT[:, i // 2, (i % 2) * HALF:(i % 2 + 1) * HALF], bank(2 + i, HALF), 0.0,
                                       QE[:, i * HALF:(i + 1) * HALF], ALU.max, ALU.add).then_inc(q_ok, 1)
            for i in range(4):
                e.wait_ge(nd_mm, s * 4 + (i + 1))
                e.tensor_scalar(RD[:, i * HALF:(i + 1) * HALF], bank(2 + i, HALF), 1e-6, None, ALU.add)
            e.drain()
            e.reciprocal(RD, RD)
            e.drain()
            for i in range(4):
                e.tensor_tensor(MT[:, i // 2, (i % 2) * HALF:(i % 2 + 1) * HALF], bank(NUMBANK[i], HALF),
                                RD[:, i * HALF:(i + 1) * HALF], ALU.mult)
            e.drain().then_inc(mt_ok, 1)
            norm_five(e, s, m_mm, m_var, m_sd, g1r, b1r)
            e.drain().then_inc(lm_ok, 1)
            norm_five(e, s, y_mm, y_var, y_sd, g2r, b2r)
            e.tensor_tensor(X[:, bass.ds(s * (TI * C), TI * C)], X[:, bass.ds(s * (TI * C), TI * C)], LM, ALU.add)

        G = BUF[:, 0:GROUP * 257]
        OH = BUF[:, 4112:4112 + GROUP * P]
        HOT = BUF[:, 6160:6160 + GROUP * P]
        WTS = BUF[:, 8208:8208 + GROUP]
        rec3f = v3(rec_main[:, :].bitcast(F32), 4)
        HB = 4

        class Hop:
            ids = sem("hop_ids")
            rows = [sem(f"hop_rows{i}") for i in range(4)]
            hot, oh, mm, add = sem("hop_hot"), sem("hop_oh"), sem("hop_mm"), sem("hop_add")

            def __init__(s, number, table, field):
                s.table, s.field = table, field
                s.turns0 = number * (CH_MAIN // GROUP)

        hops = [Hop(0, xn_d[0], 3), Hop(1, xn_d[2], 2), Hop(2, cur_d[0], 2), Hop(3, cur_d[1], 2)]

        def hop_pool(e, s):
            with e.Fori(0, CH_MAIN // GROUP) as k:
                for half in range(2):
                    pool_wait(e, s.mm, k * GROUP + (s.turns0 * GROUP + 8 * (half + 1)))
                    e.tensor_copy(ib[half][:, :], v3(rec_main[:, bass.ds((k * GROUP + 8 * half) * 4, 32)], 4)[:, :, 0]
                                  ).then_inc(s.ids, 1)
                    pool_wait(e, s.ids, k * 2 + (s.turns0 * 2 + half + 1))
                    for j in range(8):
                        slot = 8 * half + j
                        e.indirect_dma_start(G[:, slot * 257:slot * 257 + C], None, s.table,
                                             bass.IndirectOffsetOnAxis(ap=ib[half][:, j:j + 1], axis=0)
                                             ).then_inc(s.rows[slot // 4], 16)

        def hop_pe(pe, s):
            with pe.Fori(0, CH_MAIN // GROUP) as k:
                for j in range(GROUP):
                    if j % 4 == 0:
                        pe.wait_ge(s.rows[j // 4], k * 64 + (s.turns0 * 64 + 64))
                    pe.wait_ge(s.oh, k * GROUP + (s.turns0 * GROUP + j + 1))
                    pe.wait_ge(s.add, k * GROUP + (s.turns0 * GROUP + j + 1))
                    pe.matmul(bank(j % HB, 257), OH[:, j * P:(j + 1) * P], G[:, j * 257:(j + 1) * 257],
                              start=True, stop=True).then_inc(s.mm, 1)

        def one_hots(e, dst, lanes, k, op):
            lane = v3(lanes[:, bass.ds(k * (GROUP * 4), GROUP * 4)], 4)[:, :, LANE:LANE + 1].to_broadcast([P, GROUP, P])
            column = iota_row[:, :].rearrange("p (o c) -> p o c", o=1).to_broadcast([P, GROUP, P])
            return e.tensor_tensor(v3(dst, P), column, lane, op)

        def hop_act(e, s):
            with e.Fori(0, CH_MAIN // GROUP) as k:
                e.wait_ge(s.hot, k + (s.turns0 + 1))
                for j in range(GROUP):
                    e.activation(OH[:, j * P:(j + 1) * P], HOT[:, j * P:(j + 1) * P], ACT.Copy, scale=WTS[:, j:j + 1]
                                 ).then_inc(s.oh, 1)

        def hop_dve(e, s):
            recf = rec_main[:, :].bitcast(F32)
            with e.Fori(0, CH_MAIN // GROUP) as k:
                e.tensor_scalar(WTS, v3(recf[:, bass.ds(k * (GROUP * 4), GROUP * 4)], 4)[:, :, s.field], 1.0, None, ALU.mult)
                one_hots(e, HOT, recf, k, ALU.is_equal)
                e.drain().then_inc(s.hot, 1)
                tiles = tiles_of(tile_main, k)
                for j in range(GROUP):
                    e.wait_ge(s.mm, k * GROUP + (s.turns0 * GROUP + j + 1 + GROUP))
                    dst = ACC[:, bass.ds(tiles[j] * 257, 257)]
                    e.tensor_tensor(dst, bank(j % HB, 257), dst, ALU.add)
                    e.drain().then_inc(s.add, 1)

        DEG = WS[:, 800:825]
        g0_rows, g0_mm, deg_ok, dsd_ok = sem("g0_rows"), sem("g0_mm"), sem("deg_ok"), sem("dsd_ok")

        def gnn0_pe(pe, s):
            f = fronts["fg"]
            for j in range(TI):
                if j == 0:
                    pe.wait_ge(g0_rows, s + 1)
                if j >= 2:
                    pe.wait_ge(f.xt_out, f.tiles(s, j - 1))
                for c in range(2):
                    mm = pe.transpose(bank(j % 2, P, c * P), XS3[:, j, c * P:(c + 1) * P], ident[:, :])
                mm.then_inc(f.xt_tp, 1)
            for j in range(TI):
                pe.wait_ge(f.xt_out, f.tiles(s, j + 1))
                for c in range(2):
                    mm = pe.matmul(bank(2 + j, C), XT3[:, c, j * P:(j + 1) * P], wg0[:, c, :],
                                   start=(c == 0), stop=(c == 1))
                mm.then_inc(g0_mm, 1)

        def gnn0_dve(e, s):
            for j in range(TI):
                e.tensor_scalar(XS3[:, j, :], ACC[:, bass.ds((s * TI + j) * 257, C)], DEG[:, bass.ds(s * TI + j, 1)],
                                None, ALU.mult)
            e.drain().then_inc(g0_rows, 1)
            add_banks(e, s, g0_mm)

        def add_banks(e, s, mm, before=0):
            for j in range(TI):
                e.wait_ge(mm, s * TI + (before + j + 1))
                x = X[:, bass.ds((s * TI + j) * C, C)]
                e.tensor_tensor(x, bank(2 + j, C), x, ALU.add)

        def narrow_pe(pe, f, s, w, n, mm):
            front_pe(pe, f, s)
            for j in range(TI):
                pe.wait_ge(f.xt_out, f.tiles(s, j + 1))
                for c in range(2):
                    m = pe.matmul(bank(2 + j, n), XT3[:, c, j * P:(j + 1) * P], w[:, c, :], start=(c == 0), stop=(c == 1))
                m.then_inc(mm, 1)

        def narrow_dve(e, s, dst, pitch, n, mm):
            for j in range(TI):
                e.wait_ge(mm, s * TI + (j + 1))
                e.tensor_scalar(dst[:, bass.ds((s * TI + j) * pitch, n)], bank(2 + j, n), 1.0, None, ALU.mult)

        wgat = v3(WS[:, 900:932], 16)
        wgate = v3(WS[:, 940:956], 8)
        attrow = ROWS[:, 1024:1104]
        SRT = WT[:, 8192:8192 + NT * 20]
        DTT = WT[:, 8700:8700 + NT * 8]
        MX = WT[:, 8900:9000]
        ES = WT[:, 9000:9100]
        SC = WT[:, 9100:9200]
        AG = WT[:, 9200:9200 + NT * 20]
        GT = WT[:, 9700:9700 + NT * 16]
        GG = WT[:, 10240:10240 + CH_GAT * 20]
        STB = BUF[:, 2624:2624 + NT * 32]
        SPL = BUF[:, 3424:3474].bitcast(BF16)
        REST = BUF[:, 3480:3580]
        GSL = BUF[:, 0:GROUP * 32]
        DSL = BUF[:, 320:320 + GROUP * 8]
        EE = BUF[:, 448:448 + GROUP * 4]
        MSG = BUF[:, 512:512 + GROUP * 20]
        RED = BUF[:, 832:832 + GROUP * 4]
        OM = BUF[:, 1024:2048].bitcast(BF16)
        ASRC = BUF[:, 2048:2048 + GH * 96]
        SELF = BUF[:, 2592:2592 + GROUP]
        AT = BUF[0:96, 3600:3856].bitcast(BF16)
        SEL = BUF[:, 2568:2568 + GROUP // 2].bitcast(BF16)
        OHG = BUF[:, 4096:4096 + GROUP * P]
        gp_mm, src_ready, src_out, dst_ready, dst_out = (sem(x) for x in (
            "gp_mm", "src_ready", "src_out", "dst_ready", "dst_out"))
        gat_ids = sem("gat_ids")
        gat_rows = [sem(f"gat_rows{i}") for i in range(2)]
        gat_oh, gat_mm, gat_add, gat_tp, gat_at, gat_msg, gat_e, gat_ex = (sem("gat_" + x) for x in (
            "oh", "mm", "add", "tp", "at", "msg", "e", "ex"))
        gat_kept = sem("gat_kept")
        GTURNS = CH_GAT // GROUP
        sc_var, sc_sd, sc_e, sc_ex = (sem("sc_" + x) for x in ("var", "sd", "e", "ex"))

        def gat_pool(e, second):
            t0 = GTURNS if second else 0
            slots, width, table, field = (DSL, 8, dst_tab_d, 2) if second else (GSL, 32, src_tab_d, 0)
            with e.Fori(0, GTURNS) as k:
                for half in range(2):
                    if second:
                        pool_wait(e, gat_e, k * 2 + (half + 1))
                    else:
                        pool_wait(e, gat_kept, k * 2 + (half + 1))
                    e.tensor_copy(ib[half][:, :], v3(rec_gat[:, bass.ds((k * GROUP + 8 * half) * 4, 32)], 4)[:, :, field]
                                  ).then_inc(gat_ids, 1)
                    pool_wait(e, gat_ids, k * 2 + (t0 * 2 + half + 1))
                    for j in range(8):
                        slot = 8 * half + j
                        e.indirect_dma_start(slots[:, slot * width:(slot + 1) * width], None, table,
                                             bass.IndirectOffsetOnAxis(ap=ib[half][:, j:j + 1], axis=0)
                                             ).then_inc(gat_rows[half], 16)

        def gatA_act(e):
            with e.Fori(0, GTURNS) as k:
                e.wait_ge(gat_tp, k + 1)
                e.activation(AT, bank(4, 512, 0, 96), ACT.Copy).then_inc(gat_at, 1)

        def gatA_pe(pe):
            with pe.Fori(0, GTURNS) as k:
                for half in range(2):
                    pe.wait_ge(gat_kept, k * 2 + (3 + half))
                pe.wait_ge(gat_at, k + 1)
                for h in range(GH):
                    mm = pe.transpose(bank(4, P, h * P, 96), ASRC[:, h * 96:(h + 1) * 96], ident[:, :])
                mm.then_inc(gat_tp, 1)
                pe.wait_ge(gat_at, k + 2)
                pe.wait_ge(gat_oh, k + 1)
                for j in range(GROUP):
                    pe.wait_ge(gat_add, k * GROUP + (j + 1))
                    pe.matmul(bank(j % 4), SEL[0:96, j:j + 1].to_broadcast([96, P]), AT, start=True, stop=False)
                    pe.matmul(bank(j % 4), OM[:, j * P:(j + 1) * P], ident_b[:, :], start=False, stop=True
                              ).then_inc(gat_mm, 1)

        def gatA_dve(e):
            with e.Fori(0, GTURNS) as k:
                one_hots(e, OM, rec_gat[:, :].bitcast(F32), k, ALU.not_equal)
                e.drain().then_inc(gat_oh, 1)
                tiles = tiles_of(tile_gat, k)
                for half in range(2):
                    e.wait_ge(gat_rows[half], k * 128 + 128)
                    rows = v3(GSL[:, 256 * half:256 * half + 256], 32)
                    e.tensor_scalar(v3(GG[:, bass.ds((k * GROUP + 8 * half) * 20, 160)], 20), rows[:, :, 0:20], 1.0, None,
                                    ALU.mult)
                    e.tensor_copy(ASRC.rearrange("p (h q j) -> p j q h", h=GH, q=3)[:, 8 * half:8 * half + 8],
                                  rows[:, :, 20:32].rearrange("p j (q h) -> p j q h", q=3))
                    e.drain().then_inc(gat_kept, 1)
                for j in range(GROUP):
                    e.wait_ge(gat_mm, k * GROUP + (j + 1 + GROUP))
                    e.tensor_reduce(RED[:, j * 4:j * 4 + 4], v3(bank(j % 4), P), AX.X, ALU.max)
                    e.drain().then_inc(gat_add, 1)
                    m = MX[:, bass.ds(tiles[j] * 4, 4)]
                    e.tensor_tensor(m, m, RED[:, j * 4:j * 4 + 4], ALU.max)
                e.drain()

        def gatB_act(e):
            with e.Fori(0, GTURNS) as k:
                e.wait_ge(gat_e, k * 2 + 4)
                e.activation(EE, EE, ACT.Exp).then_inc(gat_ex, 1)

        def gatB_pe(pe):
            g0 = GTURNS * GROUP
            with pe.Fori(0, GTURNS) as k:
                for j in range(GROUP):
                    pe.wait_ge(gat_msg, k + 1)
                    pe.wait_ge(gat_add, k * GROUP + (g0 + j + 1))
                    pe.matmul(bank(j % 4, 20), OHG[:, j * P:(j + 1) * P], MSG[:, j * 20:(j + 1) * 20],
                              start=True, stop=True).then_inc(gat_mm, 1)

        def gatB_dve(e):
            g0 = GTURNS * GROUP
            EE3 = v3(EE, 4)
            with e.Fori(0, GTURNS) as k:
                tiles = tiles_of(tile_gat, k)
                one_hots(e, OHG, rec_gat[:, :].bitcast(F32), k, ALU.is_equal)
                gg = v3(GG[:, bass.ds(k * (GROUP * 20), GROUP * 20)], 20)
                for half in range(2):
                    lo, hi = 8 * half, 8 * half + 8
                    ee, ee3, dsl = EE[:, lo * 4:hi * 4], EE3[:, lo:hi, :], v3(DSL, 8)[:, lo:hi, :]
                    e.wait_ge(gat_rows[half], k * 128 + (GTURNS * 128 + 128))
                    seq(e, lambda: e.tensor_tensor(ee3, gg[:, lo:hi, 16:20], dsl[:, :, 0:4], ALU.add),
                        lambda: e.scalar_tensor_tensor(ee, ee, 0.2, ee, ALU.mult, ALU.max),
                        lambda: e.tensor_tensor(ee3, ee3, dsl[:, :, 4:8], ALU.subtract),
                        lambda: e.tensor_scalar(ee, ee, 0.0, None, ALU.min))
                    e.drain().then_inc(gat_e, 1)
                e.wait_ge(gat_ex, k + 1)
                e.tensor_tensor(v3(MSG, 20)[:, :, 0:16].rearrange("p g (h e) -> p g h e", h=GH),
                                gg[:, :, 0:16].rearrange("p g (h e) -> p g h e", h=GH),
                                EE3.rearrange("p g (h o) -> p g h o", o=1).to_broadcast([P, GROUP, GH, GE]), ALU.mult)
                e.tensor_copy(v3(MSG, 20)[:, :, 16:20], EE3)
                e.drain().then_inc(gat_msg, 1)
                for j in range(GROUP):
                    e.wait_ge(gat_mm, k * GROUP + (g0 + j + 1 + GROUP))
                    dst = AG[:, bass.ds(tiles[j] * 20, 20)]
                    e.tensor_tensor(dst, bank(j % 4, 20), dst, ALU.add)
                    e.drain().then_inc(gat_add, 1)

        def seq(e, *steps):
            for step in steps:
                step()
                e.drain()

        def over_tiles(row, n):
            return row.rearrange("p (o c) -> p o c", o=1).to_broadcast([P, NT, n])

        def head_sum(e, dst, tab, att, tmp):
            seq(e, lambda: e.tensor_tensor(v3(tmp, 16), tab, over_tiles(att, 16), ALU.mult),
                lambda: e.tensor_reduce(dst, tmp.rearrange("p (t h e) -> p t h e", h=GH, e=GE), AX.X, ALU.add))

        def gat_tables_dve(e):
            srt, dtt = v3(SRT, 20), v3(DTT, 8)
            head_sum(e, srt[:, :, 16:20], srt[:, :, 0:16], attrow[:, 0:16], GT)
            stb, spl, rest = v3(STB, 32), v3(SPL, 4), v3(REST, 4)
            part = [stb[:, :, 20 + 4 * q:24 + 4 * q] for q in range(3)]
            seq(e, lambda: e.tensor_copy(stb[:, :, 0:20], srt),
                lambda: e.tensor_copy(spl, srt[:, :, 16:20]),
                lambda: e.tensor_copy(part[0], spl),
                lambda: e.tensor_tensor(rest, srt[:, :, 16:20], part[0], ALU.subtract),
                lambda: e.tensor_copy(spl, rest),
                lambda: e.tensor_copy(part[1], spl),
                lambda: e.tensor_tensor(part[2], rest, part[1], ALU.subtract))
            e.drain().then_inc(src_ready, 1)
            e.memset(ASRC, 0.0)
            e.tensor_tensor(SELF, ident[:, 0:GROUP], ident[:, 32:32 + GROUP], ALU.add)
            e.drain()
            e.tensor_tensor(SEL, SELF, ident[:, 64:64 + GROUP], ALU.add)
            head_sum(e, dtt[:, :, 0:4], srt[:, :, 0:16], attrow[:, 16:32], GT)
            e.tensor_copy(v3(MX, 4), srt[:, :, 16:20])
            rf = v3(rec_gat[:, :].bitcast(F32), 4)
            e.wait_ge(gat.back, 16)
            lane = rf[:, :, LANE]
            seq(e, lambda: e.scalar_tensor_tensor(lane, lane, 1.0, rf[:, :, 3], ALU.add, ALU.mult),
                lambda: e.tensor_scalar(lane, lane, -1.0, None, ALU.add))

        def gat_max_dve(e):
            srt, dtt, mx, es, ag = v3(SRT, 20), v3(DTT, 8), v3(MX, 4), v3(ES, 4), v3(AG, 20)
            seq(e, lambda: e.tensor_tensor(mx, mx, dtt[:, :, 0:4], ALU.add),
                lambda: e.scalar_tensor_tensor(dtt[:, :, 4:8], mx, 0.2, mx, ALU.mult, ALU.max))
            e.drain().then_inc(dst_ready, 1)
            seq(e, lambda: e.tensor_tensor(es, srt[:, :, 16:20], dtt[:, :, 0:4], ALU.add),
                lambda: e.scalar_tensor_tensor(ES, ES, 0.2, ES, ALU.mult, ALU.max),
                lambda: e.tensor_tensor(es, es, dtt[:, :, 4:8], ALU.subtract))
            e.drain().then_inc(sc_e, 1)
            e.wait_ge(sc_ex, 1)
            e.tensor_copy(ag[:, :, 16:20], es)
            e.tensor_tensor(ag[:, :, 0:16].rearrange("p g (h e) -> p g h e", h=GH),
                            srt[:, :, 0:16].rearrange("p g (h e) -> p g h e", h=GH),
                            es.rearrange("p g (h o) -> p g h o", o=1).to_broadcast([P, NT, GH, GE]), ALU.mult)
            e.drain()

        def top_two(e, s, n, rank, tmp, sel):
            s3, r3, t3 = v3(s, n), v3(rank, n), v3(tmp, n)
            e.memset(rank, 0.0)
            for j in range(n):
                sj = s3[:, :, j:j + 1]
                e.tensor_tensor(t3[:, :, 0:j + 1], sj.to_broadcast([P, NT, j + 1]), s3[:, :, 0:j + 1], ALU.is_gt)
                if j + 1 < n:
                    e.tensor_tensor(t3[:, :, j + 1:n], sj.to_broadcast([P, NT, n - j - 1]), s3[:, :, j + 1:n], ALU.is_ge)
                e.drain()
                e.tensor_tensor(rank, rank, tmp, ALU.add)
                e.drain()
            e.tensor_scalar(sel, rank, 2.0, None, ALU.is_lt)
            e.drain()

        def bc(col, n):
            return col.rearrange("p (t o) -> p t o", o=1).to_broadcast([P, NT, n])

        def gat_scores_dve(e):
            ag, gt, es, sc = v3(AG, 20), v3(GT, 16), v3(ES, 4), v3(SC, 4)
            col, col2 = sd[:, :], rs[:, :]
            g4 = gt.rearrange("p t (h e) -> p t h e", h=GH)
            seq(e, lambda: e.tensor_scalar(es, ag[:, :, 16:20], 1e-16, None, ALU.add),
                lambda: e.reciprocal(ES, ES),
                lambda: e.tensor_tensor(g4, ag[:, :, 0:16].rearrange("p t (h e) -> p t h e", h=GH),
                                        es.rearrange("p g (h o) -> p g h o", o=1).to_broadcast([P, NT, GH, GE]), ALU.mult),
                lambda: e.tensor_tensor(gt, gt, over_tiles(attrow[:, 32:48], 16), ALU.add),
                lambda: e.tensor_reduce(col, gt, AX.X, ALU.add),
                lambda: e.tensor_scalar(col, col, 1.0 / 16, None, ALU.mult),
                lambda: e.tensor_tensor(gt, gt, bc(col, 16), ALU.subtract),
                lambda: e.tensor_tensor(ag[:, :, 0:16], gt, gt, ALU.mult),
                lambda: e.tensor_reduce(col, ag[:, :, 0:16], AX.X, ALU.add),
                lambda: e.tensor_scalar(col, col, 1.0 / 16, LN_EPS, ALU.mult, ALU.add))
            e.drain().then_inc(sc_var, 1)
            e.wait_ge(sc_sd, 1)
            seq(e, lambda: e.reciprocal(col, col2),
                lambda: e.tensor_tensor(gt, gt, bc(col, 16), ALU.mult),
                lambda: e.tensor_tensor(gt, gt, over_tiles(attrow[:, 48:64], 16), ALU.mult),
                lambda: e.tensor_tensor(gt, gt, over_tiles(attrow[:, 64:80], 16), ALU.add),
                lambda: e.tensor_reduce(sc, GT.rearrange("p (t h e) -> p t e h", h=GH, e=GE), AX.X, ALU.add),
                lambda: e.tensor_scalar(SC, SC, 1.0 / GH, None, ALU.mult),
                lambda: e.tensor_reduce(col, sc, AX.X, ALU.max))
            top_two(e, SC, EXP0, MX, GT[:, 0:100], ES)
            g = gates[:, 0:NT * EXP0]
            e.tensor_tensor(v3(g, 4), sc, bc(col, 4), ALU.subtract)
            e.drain().then_inc(sc_e, 1)
            e.wait_ge(sc_ex, 2)
            seq(e, lambda: e.tensor_tensor(g, g, ES, ALU.mult),
                lambda: e.tensor_reduce(col, v3(g, 4), AX.X, ALU.add),
                lambda: e.reciprocal(col2, col),
                lambda: e.tensor_tensor(v3(g, 4), v3(g, 4), bc(col2, 4), ALU.mult))

        FH = BUF[:, 0:2 * 4 * W]
        GTS = BUF[0:8, 5120:5120 + W]
        GC = WS[:, 1270:1270 + TI * 8]
        B1T = WS[:, 960:992]
        B2R = WS[0:8, 1010:1266]
        moe_gc, moe_gt, moe_gts, moe_b2, moe_b2a, moe_h, moe_ha, moe_y, moe_ya = (sem("moe_" + x) for x in (
            "gc", "gt", "gts", "b2", "b2a", "h", "ha", "y", "ya"))
        w_ffn, rows_ffn = sem("w_ffn"), sem("rows_ffn")
        YB = (6, 7, 0, 1)

        class Moe:
            def __init__(s, n, front, before):
                s.n, s.f = n, fronts[front]
                s.w1 = WT[:, 0:n * 1024].rearrange("p (e k n) -> p e k n", e=n, k=2)
                s.w2 = WT[:, n * 1024:n * 2048].rearrange("p (e k n) -> p e k n", e=n, k=4)
                s.t0 = TURNS if before else 0
                s.e0 = TURNS * before

            def turn(s, t, n):
                return t * n + s.t0 * n

        moes = [Moe(EXP0, "ff", 0), Moe(EXP1, "fe", EXP0)]

        def moe_pe(pe, m, s):
            f, E = m.f, m.n
            front_pe(pe, f, s)
            pe.wait_ge(moe_gc, m.turn(s, 1) + 1)
            for j in range(TI):
                mm = pe.transpose(bank(6 + j // 4, P, (j % 4) * P, E), GC[:, j * E:(j + 1) * E], ident[:, :])
            mm.then_inc(moe_gt, 1)
            pe.wait_ge(moe_gts, m.turn(s, 1) + 1)
            for j in range(TI):
                pe.matmul(bank(2 + j, C), GTS[0:E, j * P:(j + 1) * P], B2R[0:E, :], start=True, stop=True
                          ).then_inc(moe_b2, 1)
            pe.wait_ge(f.xt_out, f.tiles(s, TI))
            pe.wait_ge(moe_b2a, m.turn(s, TI) + TI)

            def hidden(e):
                for i in range(8):
                    mc, hf, n = i // 2, i % 2, e * 8 + i
                    if n >= 4:
                        pe.wait_ge(moe_ha, s * (8 * E) + (m.e0 * 8 + n - 3))
                    for c in range(2):
                        mm = pe.matmul(bank(2 + i % 4, HALF), m.w1[:, e, c, mc * P:(mc + 1) * P],
                                       XT3[:, c, hf * HALF:(hf + 1) * HALF], start=(c == 0), stop=(c == 1))
                    mm.then_inc(moe_h, 1)

            hidden(0)
            for e in range(E):
                if e + 1 < E:
                    hidden(e + 1)
                pe.wait_ge(moe_ha, s * (8 * E) + (m.e0 * 8 + 8 * (e + 1)))
                for j in range(TI):
                    n = e * TI + j
                    if n >= 4:
                        pe.wait_ge(moe_ya, s * (TI * E) + (m.e0 * TI + n - 3))
                    for c in range(4):
                        at = (e % 2) * 4 * W + c * W + j * P
                        mm = pe.matmul(bank(YB[n % 4], C), FH[:, at:at + P], m.w2[:, e, c, :], start=(c == 0),
                                       stop=(c == 3))
                    mm.then_inc(moe_y, 1)

        def moe_act(e, m, s):
            E = m.n
            front_act(e, m.f, s)
            e.wait_ge(moe_gt, m.turn(s, 1) + 1)
            e.activation(GTS[0:E, 0:4 * P], bank(6, 4 * P, 0, E), ACT.Copy)
            e.activation(GTS[0:E, 4 * P:5 * P], bank(7, P, 0, E), ACT.Copy)
            e.drain().then_inc(moe_gts, 1)
            for x in range(E):
                for i in range(8):
                    mc, hf = i // 2, i % 2
                    e.wait_ge(moe_h, s * (8 * E) + (m.e0 * 8 + x * 8 + i + 1))
                    if i == 0 and x >= 2:
                        e.wait_ge(moe_y, s * (TI * E) + (m.e0 * TI + TI * (x - 1)))
                    at = (x % 2) * 4 * W + mc * W + hf * HALF
                    e.activation(FH[:, at:at + HALF], bank(2 + i % 4, HALF), ACT.Gelu, bias=B1T[:, x * 4 + mc:x * 4 + mc + 1]
                                 ).then_inc(moe_ha, 1)

        def moe_dve(e, m, s):
            E = m.n
            e.tensor_scalar(GC[:, 0:TI * E], gates[:, bass.ds(s * (TI * E), TI * E)], 1.0, None, ALU.mult
                            ).then_inc(moe_gc, 1)
            for j in range(TI):
                x = X[:, bass.ds((s * TI + j) * C, C)]
                e.wait_ge(moe_b2, m.turn(s, TI) + (j + 1))
                e.tensor_tensor(x, bank(2 + j, C), x, ALU.add).then_inc(moe_b2a, 1)
            for i in range(E):
                e.drain()
                for j in range(TI):
                    n = i * TI + j
                    x = X[:, bass.ds((s * TI + j) * C, C)]
                    e.wait_ge(moe_y, s * (TI * E) + (m.e0 * TI + n + 1))
                    e.scalar_tensor_tensor(x, bank(YB[n % 4], C), GC[:, j * E + i:j * E + i + 1], x, ALU.mult, ALU.add
                                           ).then_inc(moe_ya, 1)

        wsh = v3(WT[:, 0:2048], C)
        g1_mm = sem("g1_mm")

        def gnn1_pe(pe, i, s):
            f = fronts[f"f{i}"]
            front_pe(pe, f, s)
            for j in range(TI):
                pe.wait_ge(f.xt_out, f.tiles(s, j + 1))
                for c in range(2):
                    mm = pe.matmul(bank(2 + j, C), XT3[:, c, j * P:(j + 1) * P], wsh[:, 2 * i + c, :],
                                   start=(c == 0), stop=(c == 1))
                mm.then_inc(g1_mm, 1)

        wqkv = v3(WT[:, 2048:3584], C)
        wqkvT = v3(WT[:, 3584:5120], 768)
        wproj = v3(WT[:, 5120:5632], C)
        wprojT = v3(WT[:, 5632:6144], C)
        HV = 33
        MF = WT[:, 6144:6144 + FC * 8 * HV]
        F0 = WT[:, 7680:7680 + 8 * FC * P]
        F1 = BUF[:, 0:8 * FC * P]
        HS = 4 * FG * 32
        MFT = BUF[0:HV, 0:2 * HS]
        YT = WT[0:HV, 12800:12800 + 8 * P]
        KV = BUF[:, 5120:5120 + TI * 512]
        V1 = BUF[:, 7680:7680 + TI * 8 * HV]
        K2 = BUF[:, 9088:9088 + 2 * 512]
        SQ = BUF[:, 10112:10112 + C]
        OB = BUF[:, 5120 + 1280:5120 + 2560]
        XO = v3(BUF[:, 7680:7680 + 2 * W], W)
        RN = WS[:, 1320:1360]
        RI = WS[:, 1360:1400]
        TS = WS[:, 1400:1408]
        coef = WS[:, 1000:1000 + FC]
        bq, bkv = ROWS[:, 0:C], ROWS[:, C:3 * C]
        bproj, obias, temp = ROWS[:, 768:1024], ROWS[:, 1104:1360], ROWS[:, 1360:1368]
        w_in1, rows_in1 = sem("w_in1"), sem("rows_in1")
        (m_tp, m_te, m_kv, m_sq, m_rt, m_f, m_fu, m_done, m_fq, m_ft, m_y1, m_ob, m_xo, m_xe, m_p) = (
            sem("m1_" + x) for x in ("tp", "te", "kv", "sq", "rt", "f", "fu", "done", "fq", "ft", "y", "ob", "xo",
                                     "xe", "p"))
        m_ke, m_k2, m_fp, m_ma, m_yt, m_z = (sem("m1_" + x) for x in ("ke", "k2", "fp", "ma", "yt", "z"))

        def weights_pe(pe):
            pe.wait_ge(w_in1, 48)
            blocks = [(wqkv[:, r, c * P:(c + 1) * P]) for c in range(2) for r in range(6)]
            blocks += [(wproj[:, r, c * P:(c + 1) * P]) for c in range(2) for r in range(2)]
            for i, b in enumerate(blocks):
                mm = pe.transpose(bank(i // 4, P, (i % 4) * P), b, ident[:, :])
            mm.then_inc(m_tp, 1)

        def weights_act(e):
            e.wait_ge(m_tp, 1)
            e.activation(WT[:, 3584:4096], bank(0), ACT.Copy)
            e.activation(WT[:, 4096:4608], bank(1), ACT.Copy)
            e.activation(WT[:, 4608:5120], bank(2), ACT.Copy)
            e.activation(WT[:, 5632:6144], bank(3), ACT.Copy)

        def features(e, dst, k2, heads, offsets, linear=True):
            k3 = v3(k2, 64)
            f3 = dst.rearrange("p (h g i) -> p h g i", h=heads, i=32)
            for r in offsets:
                e.tensor_tensor(f3[:, :, r, :], k3[:, :, 0:32], k3[:, :, r:r + 32], ALU.mult)
            if linear:
                e.tensor_scalar(f3[:, :, R2, :], k3[:, :, 0:32], 1.0, None, ALU.mult)

        def norms_dve(e, j, src):
            e.tensor_tensor(SQ, src, src, ALU.mult)
            e.drain()
            e.tensor_reduce(RN[:, j * 8:(j + 1) * 8], v3(SQ, 32), AX.X, ALU.add)
            e.drain()

        def double_rows(e, j, src, k2, h0, heads):
            r = RI[:, j * 8 + h0:j * 8 + h0 + heads].rearrange("p (h o) -> p h o", o=1).to_broadcast([P, heads, 32])
            for half in range(2):
                e.tensor_tensor(v3(k2, 64)[:, :, 32 * half:32 * half + 32], v3(src, 32), r, ALU.mult)
            e.drain()

        def m1A_pe(pe, s):
            f = fronts["fm"]
            front_pe(pe, f, s)
            for j in range(TI):
                pe.wait_ge(f.xt_out, f.tiles(s, TI))
                if j >= 3:
                    pe.wait_ge(m_ke, s * TI + (j - 2))
                for c in range(2):
                    mm = pe.matmul(bank(j % 3), XT3[:, c, j * P:(j + 1) * P], wqkvT[:, c, C:3 * C],
                                   start=(c == 0), stop=(c == 1))
                mm.then_inc(m_kv, 1)
            for n in range(2 * TI):
                half, j = n // TI, n % TI
                pe.wait_ge(m_f, s * (2 * TI) + (n + 1))
                pe.wait_ge(m_fp, s * (2 * TI) + (n + 1))
                if n == TI:
                    pe.wait_ge(m_ma, s * 2 + 1)
                for h in range(4):
                    v = V1[:, (j * 8 + half * 4 + h) * HV:(j * 8 + half * 4 + h + 1) * HV]
                    at = (n % 2) * 4 * FC * P + h * FC * P
                    pe.matmul(bank(3 + h, 512, 0, HV), v, F0[:, at:at + 512], start=(j == 0), stop=(j == TI - 1))
                    mm = pe.matmul(bank(7, 96, h * 96, HV), v, F0[:, at + 512:at + 608],
                                   start=(j == 0 and h == 0), stop=(j == TI - 1), skip_group_check=True)
                mm.then_inc(m_fu, 1)

        def m1A_end_pe(pe):
            pe.wait_ge(m_ma, 2 * TURNS)
            for c in range(FC):
                rows = min(P, FG * 32 - c * P)
                for h in range(8):
                    at = (h // 4) * HS + ((h % 4) * 512 + c * P if c < 4 else 2048 + (h % 4) * 96)
                    mm = pe.transpose(bank(c, HV, h * HV, rows), MFT[:, at:at + rows], ident[0:HV, 0:HV])
            mm.then_inc(m_tp, 1)

        POOL_R = 12

        def m1A_pool(e):
            with e.Fori(0, TURNS) as s:
                for n in range(2 * TI):
                    pool_wait(e, m_k2, s * (2 * TI) + (n + 1))
                    if n >= 2:
                        pool_wait(e, m_fu, s * (2 * TI) + (n - 1))
                    features(e, F0[:, (n % 2) * 2560:(n % 2 + 1) * 2560], K2[:, (n % 2) * 512:(n % 2) * 512 + 256], 4,
                             range(POOL_R, R2), False)
                    e.drain().then_inc(m_fp, 1)

        def m1A_dve(e, s):
            for j in range(TI):
                e.wait_ge(m_kv, s * TI + (j + 1))
                e.tensor_tensor(KV[:, j * 512:(j + 1) * 512], bank(j % 3), bkv, ALU.add)
                e.drain().then_inc(m_ke, 1)
            for j in range(TI):
                k = KV[:, j * 512:j * 512 + C]
                norms_dve(e, j, k)
                v1 = v3(V1[:, j * 8 * HV:(j + 1) * 8 * HV], HV)
                vd = valid[:, bass.ds(s * TI + j, 1)]
                e.tensor_scalar(v1[:, :, 1:HV], v3(KV[:, j * 512 + C:(j + 1) * 512], 32), vd, None, ALU.mult)
                e.tensor_scalar(v1[:, :, 0:1], v3(ones[:, 0:8], 1), vd, None, ALU.mult)
            e.drain().then_inc(m_sq, 1)
            e.wait_ge(m_rt, s + 1)
            seq(e, lambda: e.tensor_scalar(RN, RN, 1e-12, None, ALU.max),
                lambda: e.reciprocal(RI, RN),
                lambda: e.tensor_scalar(RI, RI, SCALE1, None, ALU.mult))
            def take_sums(half):
                e.wait_ge(m_fu, s * (2 * TI) + (half + 1) * TI)
                m = MFT[:, half * HS:(half + 1) * HS]
                e.tensor_tensor(m, ps[0:HV, 3 * 512:3 * 512 + HS], m, ALU.add)
                e.drain().then_inc(m_ma, 1)

            for n in range(2 * TI):
                half, j = n // TI, n % TI
                k2 = K2[:, (n % 2) * 512:(n % 2) * 512 + 256]
                if n >= 2:
                    e.wait_ge(m_fp, s * (2 * TI) + (n - 1))
                double_rows(e, j, KV[:, j * 512 + half * P:j * 512 + half * P + P], k2, 4 * half, 4)
                e.drain().then_inc(m_k2, 1)
                if n >= 2:
                    e.wait_ge(m_fu, s * (2 * TI) + (n - 1))
                features(e, F0[:, (n % 2) * 2560:(n % 2 + 1) * 2560], k2, 4, range(POOL_R))
                e.drain().then_inc(m_f, 1)
                if n == TI:
                    take_sums(0)
            take_sums(1)

        def m1_act(e, f, s, t0):
            front_act(e, f, s)
            e.wait_ge(m_sq, s + (t0 + 1))
            e.activation(RN, RN, ACT.Sqrt).then_inc(m_rt, 1)

        TB = (4, 5, 0, 1)

        def m1B_pe(pe, s):
            f = fronts["fn"]
            front_pe(pe, f, s)
            pe.wait_ge(f.xt_out, f.tiles(s, TI))
            for j in range(TI):
                for c in range(2):
                    mm = pe.matmul(bank(2 + j, C), XT3[:, c, j * P:(j + 1) * P], wqkvT[:, c, 0:C],
                                   start=(c == 0), stop=(c == 1))
                mm.then_inc(m_kv, 1)
            def back(j):
                pe.wait_ge(m_yt, s * TI + (j + 1))
                if j >= 2:
                    pe.wait_ge(m_ob, s * TI + (j - 1))
                pe.sem_inc(pe_waits, 1)
                for h in range(8):
                    mm = pe.transpose(bank(2 + j % 2, HV, h * HV), YT[:, h * P:(h + 1) * P], ident[0:HV, 0:HV])
                mm.then_inc(m_z, 1)

            for j in range(TI):
                pe.wait_ge(m_f, s * TI + (2 * NT + j + 1))
                for i in range(10):
                    n = j * 10 + i
                    if n >= 4:
                        pe.wait_ge(m_ft, s * 50 + (n - 3))
                    b = TB[n % 4]
                    for q in range(4):
                        if i < 8:
                            at = i * FC * P + q * P
                            mm = pe.transpose(bank(b, P, q * P), F0[:, at:at + P], ident[:, :])
                        else:
                            at = ((i - 8) * 4 + q) * FC * P + 4 * P
                            mm = pe.transpose(bank(b, P, q * P, 96), F0[:, at:at + 96], ident[:, :])
                    mm.then_inc(m_fq, 1)
                if j >= 1:
                    back(j - 1)
                pe.wait_ge(m_ft, s * 50 + (j * 10 + 10))
                for h in range(8):
                    for c in range(FC):
                        rows = min(P, FG * 32 - c * P)
                        at = h * 512 + c * P if c < 4 else 4096 + h * P
                        mm = pe.matmul(bank(6 + h // 4, P, (h % 4) * P, HV),
                                       MF[0:rows, c * 8 * HV + h * HV:c * 8 * HV + (h + 1) * HV], F1[0:rows, at:at + P],
                                       start=(c == 0), stop=(c == FC - 1), skip_group_check=True)
                mm.then_inc(m_y1, 1)
            back(TI - 1)
            for j in range(TI):
                if j == 0:
                    pe.wait_ge(m_ob, s * TI + TI)
                if j >= 2:
                    pe.wait_ge(m_xe, s * TI + (j - 1))
                for c in range(2):
                    mm = pe.transpose(bank(j % 2, P, c * P), OB[:, j * C + c * P:j * C + (c + 1) * P], ident[:, :])
                mm.then_inc(m_xo, 1)
            for j in range(TI):
                pe.wait_ge(m_xe, s * TI + (j + 1))
                for c in range(2):
                    mm = pe.matmul(bank(2 + j, C), XO[:, c, j * P:(j + 1) * P], wprojT[:, c, :],
                                   start=(c == 0), stop=(c == 1))
                mm.then_inc(m_p, 1)

        def m1B_act(e, s):
            m1_act(e, fronts["fn"], s, TURNS)
            def results(j):
                e.wait_ge(m_y1, s * TI + (j + 1))
                if j >= 1:
                    e.wait_ge(m_z, s * TI + j)
                e.activation(YT, ps[0:HV, 6 * 512:8 * 512], ACT.Copy).then_inc(m_yt, 1)

            for j in range(TI):
                if j >= 1:
                    results(j - 1)
                for i in range(10):
                    n = j * 10 + i
                    e.wait_ge(m_fq, s * 50 + (n + 1))
                    b = TB[n % 4]
                    if i < 8:
                        e.activation(F1[:, i * 512:(i + 1) * 512], bank(b), ACT.Copy).then_inc(m_ft, 1)
                    else:
                        e.activation(F1[0:96, 4096 + (i - 8) * 512:4096 + (i - 7) * 512], bank(b, 512, 0, 96), ACT.Copy
                                     ).then_inc(m_ft, 1)
            results(TI - 1)
            for j in range(TI):
                e.wait_ge(m_xo, s * TI + (j + 1))
                e.activation(XO[:, :, j * P:(j + 1) * P], v3(bank(j % 2, 2 * P), P), ACT.Copy).then_inc(m_xe, 1)

        def m1B_dve(e, s):
            for j in range(TI):
                e.wait_ge(m_kv, s * TI + (NT + j + 1))
                q = KV[:, j * C:(j + 1) * C]
                seq(e, lambda: e.tensor_tensor(q, bank(2 + j, C), bq, ALU.add),
                    lambda: e.tensor_scalar(q, q, SCALE1, None, ALU.mult))
                norms_dve(e, j, q)
            e.drain().then_inc(m_sq, 1)
            e.wait_ge(m_rt, s + (TURNS + 1))
            seq(e, lambda: e.tensor_scalar(RN, RN, 1e-12, None, ALU.max),
                lambda: e.reciprocal(RI, RN),
                lambda: e.tensor_tensor(v3(RI, 8), v3(RI, 8), TS.rearrange("p (o h) -> p o h", o=1).to_broadcast([P, TI, 8]),
                                        ALU.mult))

            def tile_out(j):
                e.wait_ge(m_z, s * TI + (j + 1))
                y = v3(bank(2 + j % 2, 8 * HV), HV)
                e.reciprocal(RN[:, j * 8:(j + 1) * 8].rearrange("p (h o) -> p h o", o=1), y[:, :, 0:1])
                e.drain()
                r = RN[:, j * 8:(j + 1) * 8].rearrange("p (h o) -> p h o", o=1).to_broadcast([P, 8, 32])
                e.tensor_tensor(v3(OB[:, j * C:(j + 1) * C], 32), y[:, :, 1:HV], r, ALU.mult)
                e.drain().then_inc(m_ob, 1)

            for j in range(TI):
                double_rows(e, j, KV[:, j * C:(j + 1) * C], K2[:, 0:512], 0, 8)
                if j >= 1:
                    e.wait_ge(m_fq, s * 50 + j * 10)
                features(e, F0, K2[:, 0:512], 8, range(R2))
                e.drain().then_inc(m_f, 1)
                if j >= 1:
                    tile_out(j - 1)
            tile_out(TI - 1)
            add_banks(e, s, m_p)

        LG = BUF[:, 8192:8192 + NT * 8]
        GR = BUF[:, 8448:8448 + NT * 8]
        GM = BUF[:, 8704:8704 + NT * 8]
        GSEL = BUF[:, 8960:8960 + NT * 8]
        gbrow = ROWS[:, 2000:2008]
        gl_mm, gl_e, gl_ex = sem("gl_mm"), sem("gl_e"), sem("gl_ex")

        def gates1_dve(e):
            col, col2 = sd[:, :], rs[:, :]
            lg = v3(LG, 8)
            seq(e, lambda: e.tensor_tensor(lg, lg, over_tiles(gbrow, 8), ALU.add),
                lambda: e.tensor_reduce(col, lg, AX.X, ALU.max),
                lambda: e.tensor_tensor(lg, lg, bc(col, 8), ALU.subtract))
            e.drain().then_inc(gl_e, 1)
            e.wait_ge(gl_ex, 1)
            seq(e, lambda: e.tensor_reduce(col, lg, AX.X, ALU.add),
                lambda: e.reciprocal(col2, col),
                lambda: e.tensor_tensor(lg, lg, bc(col2, 8), ALU.mult))
            top_two(e, LG, EXP1, GR, GM, GSEL)
            e.tensor_tensor(gates[:, :], LG, GSEL, ALU.mult)

        block = ctx.enter_context(nc.Block())
        w_late = sem("w_late")
        out_done = sem("out_done")
        x_done = sem("x_done")
        dve_ready = sem("dve_ready")
        hop_done, cur_out = sem("hop_done"), sem("cur_out")
        hop_init = sem("hop_init")

        def broadcast_row(ap, n):
            return ap.rearrange(
                "(o n) -> o n", o=1).to_broadcast([P, n])

        @block.sync
        def _(sp):
            full = (NT - 1) * P
            sp.wait_ge(consts_ok, 1)
            sp.dma_start(v3(X[:, 0:(NT - 1) * C], C), a["x"][0:full, :].rearrange("(t p) c -> p t c", p=P)
                         ).then_inc(x_in, 16)
            sp.dma_start(X[0:LAST, (NT - 1) * C:NT * C], a["x"][full:N, :]).then_inc(x_in, 16)
            sort_loads(sp, main, a["src"], a["dst"], a["edge_weight"])
            for s in (main, gat):
                sp.dma_start(s.rec_d.rearrange("(p c) f -> p (c f)", p=P), zeros[:, 0:(s.chunks + PADROWS) * 4]
                             ).then_inc(s.cleared, 16)
            for dst, src in ((wk_wv[:, :, 0:C], a["L0_mix_Wk"]), (wk_wv[:, :, C:2 * C], a["L0_mix_Wv"]),
                             (wq0, a["L0_mix_Wq"]), (wm0, a["L0_mix_Wm"]), (w1m, a["L0_mix_W1"]),
                             (w2m, a["L0_mix_W2"]), (wg0, a["L0_gnn_weight"])):
                sp.dma_start(dst, src.rearrange("(k p) n -> p k n", p=P)).then_inc(w_in0, 16)
            for dst, src in ((g1r, "L0_mix_g1"), (b1r, "L0_mix_b1"), (g2r, "L0_mix_g2"), (b2r, "L0_mix_b2")):
                sp.dma_start(dst, broadcast_row(a[src], C)).then_inc(w_in0, 16)
            sp.wait_ge(main.pos_ok, 1)
            sp.wait_ge(sort_free, 1)
            sort_loads(sp, gat, a["L0_ffn_edge_index"][0, :], a["L0_ffn_edge_index"][1, :], None)
            sp.wait_ge(norms[0].xn_ok, 1)
            acc_to_dram(sp, xn_d[0], norms[0].out)
            sp.wait_ge(norms[0].out, 16)
            front_sp(sp, fronts["fa"], xn_d[0])
            sp.wait_ge(Front.xt_tp, NT)
            front_sp(sp, fronts["fb"], xn_d[0], [(xb_ok, 1)])
            for s in (main, gat):
                total = 16 * s.per * s.turns
                for q in s.scat:
                    sp.wait_ge(q, total)
                sp.dma_start(s.rec_sb[:, :], s.rec_d.rearrange("(p c) f -> p (c f)", p=P)[:, 0:s.chunks * 4]
                             ).then_inc(s.back, 16)
            for ap, n in ((a["L0_ffn_att_src"].rearrange("h e -> (h e)"), 0),
                          (a["L0_ffn_att_dst"].rearrange("h e -> (h e)"), 16), (a["L0_ffn_b_gat"], 32),
                          (a["L0_ffn_ln_gamma"], 48), (a["L0_ffn_ln_beta"], 64)):
                sp.dma_start(attrow[:, n:n + 16], broadcast_row(ap, 16)).then_inc(rows_ffn, 16)
            sp.dma_start(wgat, a["L0_ffn_W_gat"].rearrange("(k p) n -> p k n", p=P)).then_inc(rows_ffn, 16)
            sp.dma_start(wgate, a["L1_ffn_gate_w"].rearrange("(k p) n -> p k n", p=P)).then_inc(rows_ffn, 16)
            sp.dma_start(gbrow, broadcast_row(a["L1_ffn_gate_b"], 8)).then_inc(rows_ffn, 16)
            sp.dma_start(B1T[:, 0:16], a["L0_ffn_b1"].rearrange("e (m p) -> p (e m)", p=P), allow_slow_non_contiguous=True).then_inc(rows_ffn, 16)
            sp.dma_start(B2R[0:EXP0, :], a["L0_ffn_b2"]).then_inc(rows_ffn, 16)
            sp.wait_ge(round_pe, R["lnb"] + 1)
            sp.dma_start(moes[0].w1, a["L0_ffn_W1"].rearrange("e (k p) n -> p e k n", p=P)).then_inc(w_ffn, 16)
            sp.dma_start(moes[0].w2, a["L0_ffn_W2"].rearrange("e (k p) n -> p e k n", p=P)).then_inc(w_ffn, 16)
            sp.wait_ge(norms[1].xn_ok, 1)
            acc_to_dram(sp, xn_d[1], norms[1].out)
            sp.wait_ge(norms[1].out, 16)
            front_sp(sp, fronts["fp"], xn_d[1])
            sp.wait_ge(src_ready, 1)
            sp.dma_start(src_tab_d.rearrange("(t p) c -> p t c", p=P), v3(STB, 32)).then_inc(src_out, 16)
            sp.wait_ge(dst_ready, 1)
            sp.dma_start(dst_tab_d.rearrange("(t p) c -> p t c", p=P), v3(DTT, 8)).then_inc(dst_out, 16)
            front_sp(sp, fronts["ff"], xn_d[1])
            sp.wait_ge(round_pe, R["lnc"] + 1)
            sp.dma_start(wsh, a["L1_gnn_shared_weight"].rearrange("(k p) n -> p k n", p=P)).then_inc(w_in1, 16)
            sp.dma_start(wqkv, a["L1_mix_Wqkv"].rearrange("(k p) n -> p k n", p=P)).then_inc(w_in1, 16)
            sp.dma_start(wproj, a["L1_mix_Wproj"].rearrange("(k p) n -> p k n", p=P)).then_inc(w_in1, 16)
            sp.dma_start(ROWS[:, 0:768], broadcast_row(a["L1_mix_bqkv"], 768)).then_inc(rows_in1, 16)
            sp.dma_start(bproj, broadcast_row(a["L1_mix_bproj"], C)).then_inc(rows_in1, 16)
            sp.dma_start(obias, broadcast_row(a["L1_gnn_output_bias"], C)).then_inc(rows_in1, 16)
            sp.dma_start(temp, broadcast_row(a["L1_mix_temperature"].rearrange("a h b c -> (a h b c)"), 8)
                         ).then_inc(rows_in1, 16)
            sp.wait_ge(norms[2].xn_ok, 1)
            acc_to_dram(sp, xn_d[2], norms[2].out)
            for i in range(3):
                sp.wait_ge(hop_done, i + 1)
                acc_to_dram(sp, cur_d[i], cur_out)
            sp.wait_ge(cur_out, 48)
            for i, table in enumerate([xn_d[2]] + cur_d):
                if i:
                    sp.wait_ge(Front.xt_tp, fronts[f"f{i}"].before * TI)
                front_sp(sp, fronts[f"f{i}"], table)
            for i in ("fm", "fn"):
                sp.wait_ge(Front.xt_tp, fronts[i].before * TI)
                front_sp(sp, fronts[i], xn_d[2])
            sp.wait_ge(round_pe, R["lnd"] + 1)
            sp.dma_start(moes[1].w1, a["L1_ffn_W1"].rearrange("e (k p) n -> p e k n", p=P)).then_inc(w_ffn, 16)
            sp.dma_start(moes[1].w2, a["L1_ffn_W2"].rearrange("e (k p) n -> p e k n", p=P)).then_inc(w_ffn, 16)
            sp.dma_start(B1T[:, 0:32], a["L1_ffn_b1"].rearrange("e (m p) -> p (e m)", p=P), allow_slow_non_contiguous=True).then_inc(w_ffn, 16)
            sp.dma_start(B2R[0:EXP1, :], a["L1_ffn_b2"]).then_inc(w_ffn, 16)
            sp.wait_ge(norms[3].xn_ok, 1)
            acc_to_dram(sp, xn_d[0], norms[3].out)
            sp.wait_ge(norms[3].out, 16)
            front_sp(sp, fronts["fq"], xn_d[0])
            sp.wait_ge(Front.xt_tp, fronts["fe"].before * TI)
            front_sp(sp, fronts["fe"], xn_d[0])
            sp.wait_ge(x_done, 1)
            sp.dma_start(out[0:full, :].rearrange("(t p) c -> p t c", p=P), v3(X[:, 0:(NT - 1) * C], C)
                         ).then_inc(out_done, 16)
            sp.dma_start(out[full:N, :], X[0:LAST, (NT - 1) * C:NT * C]).then_inc(out_done, 16)
            sp.wait_ge(out_done, 32)

        @block.gpsimd
        def _(e):
            e.memset(ones[:, :], 1.0)
            e.memset(eps_ln[:, :], LN_EPS)
            e.memset(valid[:, :], 1.0)
            e.memset(zeros, 0)
            e.memset(X[:, (NT - 1) * C:NT * C], 0.0)
            e.memset(s_src, 0)
            e.memset(s_dst, NP)
            e.memset(s_w, 0.0)
            e.iota(iota_row[:, :], [[1, P]], base=0, channel_multiplier=0, allow_small_or_imprecise_dtypes=True)
            e.iota(s_iota, [[1, CH_MAIN]], base=0, channel_multiplier=0, allow_small_or_imprecise_dtypes=True)
            e.drain()
            e.affine_select(out=ident[:, :], in_=ones[:, :], compare_op=ALU.is_equal, fill=0.0, base=0,
                            pattern=[[1, P]], channel_multiplier=-1)
            e.affine_select(out=upper[:, :], in_=ones[:, :], compare_op=ALU.is_gt, fill=0.0, base=0,
                            pattern=[[1, P]], channel_multiplier=-1)
            e.affine_select(out=v3(head_mask[:, :], 32), in_=v3(ones[:, :], 32), compare_op=ALU.is_ge, fill=0.0,
                            base=0, pattern=[[-32, 4], [0, 32]], channel_multiplier=1)
            e.affine_select(out=valid[:, NT - 1:NT], in_=ones[:, 0:1], compare_op=ALU.is_gt, fill=0.0, base=LAST,
                            pattern=[[0, 1]], channel_multiplier=-1)
            e.drain()
            e.affine_select(out=v3(head_mask[:, :], 32), in_=v3(head_mask[:, :], 32), compare_op=ALU.is_ge, fill=0.0,
                            base=31, pattern=[[32, 4], [0, 32]], channel_multiplier=-1)
            for b in range(4):
                e.tensor_scalar(ident_b[:, b * P:(b + 1) * P], ident[:, :], -BIG, None, ALU.mult)
            e.drain().then_inc(consts_ok, 1)
            e.sem_inc(Hop.mm, GROUP)
            e.sem_inc(Hop.add, HB)
            e.sem_inc(gat_mm, GROUP)
            e.sem_inc(gat_add, HB)
            e.sem_inc(gat_at, 1)
            e.sem_inc(gat_e, 2)
            sort_pool(e, main)
            sort_pool(e, gat)
            for i in (0,):
                pool_wait(e, hop_init, 1)
                hop_pool(e, hops[0])
            e.sem_inc(gat_kept, 2)
            pool_wait(e, src_out, 16)
            pool_wait(e, dve_ready, 1)
            gat_pool(e, False)
            pool_wait(e, dst_out, 16)
            gat_pool(e, True)
            for i in range(3):
                pool_wait(e, hop_init, i + 2)
                hop_pool(e, hops[i + 1])
            m1A_pool(e)

        @block.tensor
        def _(pe):
            sort_pe(pe, main)
            sort_pe(pe, gat)
            pe.wait_ge(w_in0, 16 * 11)
            with pe.Fori(0, TURNS) as s:
                mixA_pe(pe, s)
                rendezvous(pe, "pe", s + (R["mixA"] + 1))
            rendezvous(pe, "pe", R["mixA_end"] + 1)
            with pe.Fori(0, TURNS) as s:
                mixB_pe(pe, s)
                rendezvous(pe, "pe", s + (R["mixB"] + 1))
            hop_pe(pe, hops[0])
            rendezvous(pe, "pe", R["hop0"] + 1)
            with pe.Fori(0, TURNS) as s:
                gnn0_pe(pe, s)
                rendezvous(pe, "pe", s + (R["gnn0"] + 1))
            rendezvous(pe, "pe", R["lnb"] + 1)
            pe.wait_ge(rows_ffn, 160)
            with pe.Fori(0, TURNS) as s:
                narrow_pe(pe, fronts["fp"], s, wgat, 16, gp_mm)
                rendezvous(pe, "pe", s + (R["gatp"] + 1))
            rendezvous(pe, "pe", R["gatp_end"] + 1)
            gatA_pe(pe)
            rendezvous(pe, "pe", R["gatA"] + 1)
            gatB_pe(pe)
            rendezvous(pe, "pe", R["gatB"] + 1)
            pe.wait_ge(w_ffn, 32)
            with pe.Fori(0, TURNS) as s:
                moe_pe(pe, moes[0], s)
                rendezvous(pe, "pe", s + (R["ffn0"] + 1))
            rendezvous(pe, "pe", R["lnc"] + 1)
            for i in range(3):
                hop_pe(pe, hops[i + 1])
                rendezvous(pe, "pe", R[f"hop{i + 1}"] + 1)
            pe.wait_ge(w_in1, 48)
            for i in range(4):
                with pe.Fori(0, TURNS) as s:
                    gnn1_pe(pe, i, s)
                    rendezvous(pe, "pe", s + (R["gnn1"] + i * TURNS + 1))
            weights_pe(pe)
            rendezvous(pe, "pe", R["m1w"] + 1)
            with pe.Fori(0, TURNS) as s:
                m1A_pe(pe, s)
                rendezvous(pe, "pe", s + (R["m1A"] + 1))
            m1A_end_pe(pe)
            rendezvous(pe, "pe", R["m1A_end"] + 1)
            with pe.Fori(0, TURNS) as s:
                m1B_pe(pe, s)
                rendezvous(pe, "pe", s + (R["m1B"] + 1))
            rendezvous(pe, "pe", R["lnd"] + 1)
            with pe.Fori(0, TURNS) as s:
                narrow_pe(pe, fronts["fq"], s, wgate, 8, gl_mm)
                rendezvous(pe, "pe", s + (R["gate1"] + 1))
            rendezvous(pe, "pe", R["gate1_end"] + 1)
            pe.wait_ge(w_ffn, 96)
            with pe.Fori(0, TURNS) as s:
                moe_pe(pe, moes[1], s)
                rendezvous(pe, "pe", s + (R["ffn1"] + 1))

        @block.scalar
        def _(e):
            e.wait_ge(consts_ok, 1)
            norm_act(e, norms[0])
            with e.Fori(0, TURNS) as s:
                mixA_act(e, s)
                rendezvous(e, "act", s + (R["mixA"] + 1))
            rendezvous(e, "act", R["mixA_end"] + 1)
            with e.Fori(0, TURNS) as s:
                mixB_act(e, s)
                rendezvous(e, "act", s + (R["mixB"] + 1))
            hop_act(e, hops[0])
            e.wait_ge(deg_ok, 1)
            e.activation(sd[:, :], DEG, ACT.Sqrt).then_inc(dsd_ok, 1)
            rendezvous(e, "act", R["hop0"] + 1)
            with e.Fori(0, TURNS) as s:
                front_act(e, fronts["fg"], s)
                rendezvous(e, "act", s + (R["gnn0"] + 1))
            rendezvous(e, "act", R["lnb"] + 1)
            norm_act(e, norms[1])
            with e.Fori(0, TURNS) as s:
                front_act(e, fronts["fp"], s)
                rendezvous(e, "act", s + (R["gatp"] + 1))
            rendezvous(e, "act", R["gatp_end"] + 1)
            gatA_act(e)
            rendezvous(e, "act", R["gatA"] + 1)
            e.wait_ge(sc_e, 1)
            e.activation(ES, ES, ACT.Exp).then_inc(sc_ex, 1)
            gatB_act(e)
            rendezvous(e, "act", R["gatB"] + 1)
            e.wait_ge(sc_var, 1)
            e.activation(rs[:, :], sd[:, :], ACT.Sqrt).then_inc(sc_sd, 1)
            e.wait_ge(sc_e, 2)
            e.activation(gates[:, 0:NT * EXP0], gates[:, 0:NT * EXP0], ACT.Exp).then_inc(sc_ex, 1)
            e.wait_ge(rows_ffn, 160)
            with e.Fori(0, TURNS) as s:
                moe_act(e, moes[0], s)
                rendezvous(e, "act", s + (R["ffn0"] + 1))
            rendezvous(e, "act", R["lnc"] + 1)
            norm_act(e, norms[2])
            for i in range(3):
                hop_act(e, hops[i + 1])
                rendezvous(e, "act", R[f"hop{i + 1}"] + 1)
            for i in range(4):
                with e.Fori(0, TURNS) as s:
                    front_act(e, fronts[f"f{i}"], s)
                    rendezvous(e, "act", s + (R["gnn1"] + i * TURNS + 1))
            weights_act(e)
            rendezvous(e, "act", R["m1w"] + 1)
            with e.Fori(0, TURNS) as s:
                m1_act(e, fronts["fm"], s, 0)
                rendezvous(e, "act", s + (R["m1A"] + 1))
            rendezvous(e, "act", R["m1A_end"] + 1)
            with e.Fori(0, TURNS) as s:
                m1B_act(e, s)
                rendezvous(e, "act", s + (R["m1B"] + 1))
            rendezvous(e, "act", R["lnd"] + 1)
            norm_act(e, norms[3])
            with e.Fori(0, TURNS) as s:
                front_act(e, fronts["fq"], s)
                rendezvous(e, "act", s + (R["gate1"] + 1))
            e.wait_ge(gl_e, 1)
            e.activation(LG, LG, ACT.Exp).then_inc(gl_ex, 1)
            rendezvous(e, "act", R["gate1_end"] + 1)
            e.wait_ge(w_ffn, 96)
            with e.Fori(0, TURNS) as s:
                moe_act(e, moes[1], s)
                rendezvous(e, "act", s + (R["ffn1"] + 1))

        @block.vector
        def _(e):
            e.wait_ge(consts_ok, 1)
            sort_dve(e, main, n_main, True)
            e.drain().then_inc(sort_free, 1)
            e.wait_ge(x_in, 32)
            norm_dve(e, norms[0])
            sort_dve(e, gat, n_gat, False)
            e.memset(KVA, 0.0)
            e.drain()
            with e.Fori(0, TURNS) as s:
                mixA_dve(e, s)
                rendezvous(e, "dve", s + (R["mixA"] + 1))
            for h in range(2):
                e.tensor_tensor(KVB[:, h * P:(h + 1) * P], KVA[:, h * 129:h * 129 + P], head_mask[:, :], ALU.mult)
                e.tensor_scalar(ZB[:, h * P:(h + 1) * P], head_mask[:, :], KVA[:, h * 129 + P:h * 129 + P + 1], None,
                                ALU.mult)
            rendezvous(e, "dve", R["mixA_end"] + 1)
            with e.Fori(0, TURNS) as s:
                mixB_dve(e, s)
                rendezvous(e, "dve", s + (R["mixB"] + 1))
            e.memset(v3(ACC[:, :], 257)[:, :, C:C + 1], 0.0)
            e.memset(v3(G, 257)[:, :, C:C + 1], 1.0)
            e.wait_ge(main.back, 16)
            e.drain().then_inc(hop_init, 1)
            hop_dve(e, hops[0])
            e.tensor_scalar(DEG, v3(ACC[:, :], 257)[:, :, C], 1.0, None, ALU.max)
            e.drain().then_inc(deg_ok, 1)
            e.wait_ge(dsd_ok, 1)
            e.reciprocal(DEG, sd[:, :])
            rendezvous(e, "dve", R["hop0"] + 1)
            with e.Fori(0, TURNS) as s:
                gnn0_dve(e, s)
                rendezvous(e, "dve", s + (R["gnn0"] + 1))
            rendezvous(e, "dve", R["lnb"] + 1)
            norm_dve(e, norms[1])
            e.wait_ge(rows_ffn, 160)
            with e.Fori(0, TURNS) as s:
                narrow_dve(e, s, SRT, 20, 16, gp_mm)
                rendezvous(e, "dve", s + (R["gatp"] + 1))
            gat_tables_dve(e)
            e.drain().then_inc(dve_ready, 1)
            rendezvous(e, "dve", R["gatp_end"] + 1)
            gatA_dve(e)
            rendezvous(e, "dve", R["gatA"] + 1)
            gat_max_dve(e)
            gatB_dve(e)
            rendezvous(e, "dve", R["gatB"] + 1)
            gat_scores_dve(e)
            with e.Fori(0, TURNS) as s:
                moe_dve(e, moes[0], s)
                rendezvous(e, "dve", s + (R["ffn0"] + 1))
            rendezvous(e, "dve", R["lnc"] + 1)
            norm_dve(e, norms[2])
            x3 = v3(X[:, :], C)
            e.wait_ge(rows_in1, 64)
            e.tensor_tensor(x3, x3, over_tiles(bproj, C), ALU.add)
            e.drain()
            e.tensor_tensor(x3, x3, over_tiles(obias, C), ALU.add)
            e.tensor_scalar(TS, temp, SCALE1, None, ALU.mult)
            e.wait_ge(norms[2].out, 16)
            for i in range(3):
                if i:
                    e.wait_ge(cur_out, 16 * i)
                e.memset(ACC[:, :], 0.0)
                if i == 0:
                    e.memset(v3(G, 257)[:, :, C:C + 1], 1.0)
                e.drain().then_inc(hop_init, 1)
                hop_dve(e, hops[i + 1])
                e.drain().then_inc(hop_done, 1)
                rendezvous(e, "dve", R[f"hop{i + 1}"] + 1)
            for i in range(4):
                with e.Fori(0, TURNS) as s:
                    add_banks(e, s, g1_mm, i * NT)
                    rendezvous(e, "dve", s + (R["gnn1"] + i * TURNS + 1))
            A = 0.5
            vals = [A] + [2 * A] * 15 + [A, SCALE1 ** 2, SCALE1 ** 4]
            for g, val in enumerate(vals):
                e.memset(coef[32 * (g % 4):32 * (g % 4) + 32, g // 4:g // 4 + 1], val / N)
            e.memset(MFT, 0.0)
            f3 = F0.rearrange("p (h g i) -> p h g i", h=8, i=32)
            e.memset(f3[:, :, FG - 1, :], 0.0)
            e.drain()
            e.memset(f3[:, :, FG - 1, 0:1], 1.0)
            rendezvous(e, "dve", R["m1w"] + 1)
            with e.Fori(0, TURNS) as s:
                m1A_dve(e, s)
                rendezvous(e, "dve", s + (R["m1A"] + 1))
            e.wait_ge(m_tp, 2)
            for c in range(FC):
                rows = min(P, FG * 32 - c * P)
                e.tensor_scalar(MF[0:rows, c * 8 * HV:(c + 1) * 8 * HV], bank(c, 8 * HV, 0, rows),
                                coef[0:rows, c:c + 1], None, ALU.mult)
            rendezvous(e, "dve", R["m1A_end"] + 1)
            with e.Fori(0, TURNS) as s:
                m1B_dve(e, s)
                rendezvous(e, "dve", s + (R["m1B"] + 1))
            rendezvous(e, "dve", R["lnd"] + 1)
            norm_dve(e, norms[3])
            with e.Fori(0, TURNS) as s:
                narrow_dve(e, s, LG, 8, 8, gl_mm)
                rendezvous(e, "dve", s + (R["gate1"] + 1))
            gates1_dve(e)
            rendezvous(e, "dve", R["gate1_end"] + 1)
            with e.Fori(0, TURNS) as s:
                moe_dve(e, moes[1], s)
                rendezvous(e, "dve", s + (R["ffn1"] + 1))
            e.drain().then_inc(x_done, 1)


_INS = ['x', 'src', 'dst', 'edge_weight', 'L0_gnn_weight', 'L0_mix_Wq', 'L0_mix_Wk', 'L0_mix_Wv', 'L0_mix_Wm',
        'L0_mix_W1', 'L0_mix_W2', 'L0_mix_g1', 'L0_mix_b1', 'L0_mix_g2', 'L0_mix_b2', 'L0_ffn_W_gat',
        'L0_ffn_att_src', 'L0_ffn_att_dst', 'L0_ffn_b_gat', 'L0_ffn_ln_gamma', 'L0_ffn_ln_beta', 'L0_ffn_W1',
        'L0_ffn_b1', 'L0_ffn_W2', 'L0_ffn_b2', 'L0_ffn_edge_index', 'L1_gnn_shared_weight', 'L1_gnn_output_bias',
        'L1_mix_Wqkv', 'L1_mix_bqkv', 'L1_mix_Wproj', 'L1_mix_bproj', 'L1_mix_temperature', 'L1_ffn_gate_w',
        'L1_ffn_gate_b', 'L1_ffn_W1', 'L1_ffn_b1', 'L1_ffn_W2', 'L1_ffn_b2']


def kernel(**inputs):
    import numpy as np
    import concourse.bacc as bacc
    from concourse.bass_utils import run_bass_kernel_spmd

    nc = bacc.Bacc("TRN2", target_bir_lowering=False, num_devices=1)
    arrays, args = {}, {}
    for name in _INS:
        arr = np.ascontiguousarray(inputs[name])
        arrays[f"in_{name}"] = arr
        args[name] = nc.dram_tensor(f"in_{name}", arr.shape, mybir.dt.from_np(arr.dtype), kind="ExternalInput").ap()
    out = nc.dram_tensor("out_0", (N, C), F32, kind="ExternalOutput").ap()
    gps_kernel(nc, args, out)
    r = run_bass_kernel_spmd(nc, [arrays], core_ids=[0])
    return r.results[0]["out_0"]
```

```python
from contextlib import ExitStack

import concourse.bass as bass
from concourse import mybir
from concourse.alu_op_type import AluOpType as ALU

ACT = mybir.ActivationFunctionType
AX = mybir.AxisListType
F32 = mybir.dt.float32
BF16 = mybir.dt.bfloat16
I32 = mybir.dt.int32

P = 128
N = 3125
C = 256
NT = -(-N // P)
NP = NT * P
TI = 5
TURNS = NT // TI
W = TI * P
HALF = W // 2
LAST = N - (NT - 1) * P
LN_EPS = 1e-5
BUCKETS = NT + 1

E_MAIN = 50000
E_GAT = 32768
GROUP = 16


def chunk_bound(edges):
    return -(-(-(-(edges + NT * (P - 1)) // P)) // GROUP) * GROUP


CH_MAIN = chunk_bound(E_MAIN)
CH_GAT = chunk_bound(E_GAT)
BIG = 1e30
LANE = 1


def gps_kernel(nc, a, out):
    HEADS0, HD0 = 8, 32
    EXP0, EXP1 = 4, 8
    HID = 512
    GH = 4
    GE = 4
    R2 = 17
    FG = R2 + 2
    FC = -(-FG * 32 // P)
    SCALE1 = float(32) ** 0.25

    ctx = ExitStack()
    with ctx:
        def sb(name, shape, dt=F32):
            return ctx.enter_context(nc.sbuf_tensor(name, shape, dt))

        def sem(name):
            return ctx.enter_context(nc.semaphore(name))

        def dram(name, shape, dt=F32):
            return nc.dram_tensor(name, shape, dt, kind="Internal").ap()

        xn_d = [dram(f"xn_d{i}", [NP, C]) for i in range(3)]
        cur_d = [dram(f"cur_d{i}", [NP, C]) for i in range(3)]
        src_tab_d = dram("src_tab_d", [NP, 32])
        dst_tab_d = dram("dst_tab_d", [NP, 8])
        PADROWS = 8
        rec_main_d = dram("rec_main_d", [P * (CH_MAIN + PADROWS), 4], I32)
        rec_gat_d = dram("rec_gat_d", [P * (CH_GAT + PADROWS), 4], I32)

        X = sb("X", [P, NT * C])
        ACC = sb("ACC", [P, NT * 257])
        rec_main = sb("rec_main", [P, CH_MAIN * 4], I32)
        rec_gat = sb("rec_gat", [P, CH_GAT * 4], I32)
        ident = sb("ident", [P, P])
        ident_b = sb("ident_b", [P, 4 * P], BF16)
        iota_row = sb("iota_row", [P, P])
        upper = sb("upper", [P, P])
        ones = sb("ones", [P, P])
        head_mask = sb("head_mask", [P, P])
        valid = sb("valid", [P, NT])
        eps_ln = sb("eps_ln", [P, 1])
        WT = sb("WT", [P, 16384])
        WS = sb("WS", [P, 2048])
        ROWS = sb("ROWS", [P, 2560])
        XS = sb("XS", [P, TI * C])
        XT = sb("XT", [P, 2 * W])
        BUF = sb("BUF", [P, 11520])
        bn = sb("bn", [P, NT * 6])
        mv = sb("mv", [P, NT * 2])
        sd = sb("sd", [P, NT])
        rs = sb("rs", [P, NT])
        gates = sb("gates", [P, NT * 8])
        tile_main = sb("tile_main", [1, CH_MAIN], I32)
        tile_gat = sb("tile_gat", [1, CH_GAT], I32)
        ib = [sb("ibA", [P, GROUP // 2], I32), sb("ibB", [P, GROUP // 2], I32)]
        ps = ctx.enter_context(nc.psum_tensor("ps", [P, 8 * 512], F32))

        def bank(b, n=512, off=0, rows=P):
            return ps[0:rows, b * 512 + off:b * 512 + off + n]

        def v3(ap, b):
            return ap.rearrange("p (a b) -> p a b", b=b)

        XS3 = v3(XS[:, :], C)
        XT3 = v3(XT[:, :], W)

        consts_ok = sem("consts_ok")
        x_in = sem("x_in")
        carried = sem("carried")
        round_pe, round_act, round_dve = sem("round_pe"), sem("round_act"), sem("round_dve")
        rounds = {"pe": round_pe, "act": round_act, "dve": round_dve}

        def rendezvous(e, who, n):
            e.drain().then_inc(rounds[who], 1)
            for other, s in rounds.items():
                if other != who:
                    e.wait_ge(s, n)

        def pool_wait(e, q, value):
            e.wait_ge(q, value)
            e.sem_inc(carried, 1)

        def tiles_of(table, k):
            return nc.values_load_multi_w_load_instructions(
                table[0:1, bass.ds(k * GROUP, GROUP)], [mybir.EngineType.DVE], min_val=0, max_val=NT - 1,
                skip_runtime_bounds_check_because="the sort writes counts of buckets, 0 to NT - 1")[1]

        R = {}
        count = 0
        for name, n in (("mixA", TURNS), ("mixA_end", 1), ("mixB", TURNS), ("hop0", 1), ("gnn0", TURNS),
                        ("lnb", 1), ("gatp", TURNS), ("gatp_end", 1), ("gatA", 1), ("gatB", 1), ("ffn0", TURNS),
                        ("lnc", 1), ("hop1", 1), ("hop2", 1), ("hop3", 1), ("gnn1", 4 * TURNS), ("m1w", 1),
                        ("m1A", TURNS), ("m1A_end", 1), ("m1B", TURNS), ("lnd", 1), ("gate1", TURNS), ("gate1_end", 1),
                        ("ffn1", 1), ("ffn1_end", 1)):
            R[name] = count
            count += n

        class Sort:
            loaded = sem("edges_loaded")
            count_ok = sem("count_ok")
            sums_ok = sem("sums_ok")

            def __init__(s, number, name, edges, cols, per, turns, chunks, rec_sb, rec_d, tiles, at):
                s.n = number + 1
                s.name, s.edges, s.cols, s.per, s.turns, s.chunks = name, edges, cols, per, turns, chunks
                assert cols == 2 * per * turns and P * cols >= edges
                s.rec_sb, s.rec_d, s.tiles = rec_sb, rec_d, tiles
                s.rec = WT[:, at:at + cols * 4].bitcast(I32)
                s.pos = WT[:, at + cols * 4:at + cols * 5].bitcast(I32)
                s.ids = [sb(f"{name}_ids{i}", [P, per], I32) for i in range(2)]
                s.rows = [sb(f"{name}_rows{i}", [P, per * 4], I32) for i in range(2)]
                s.cleared = sem(name + "_cleared")
                s.pos_ok = sem(name + "_pos_ok")
                s.slot = sem(name + "_slot")
                s.scat = [sem(f"{name}_scat{i}") for i in range(2)]
                s.back = sem(name + "_back")

        main = Sort(0, "main", E_MAIN, 392, 14, 14, CH_MAIN, rec_main, rec_main_d, tile_main, 10240)
        gat = Sort(1, "gat", E_GAT, 256, 16, 8, CH_GAT, rec_gat, rec_gat_d, tile_gat, 12288)
        SCOLS = 392
        s_dst = BUF[:, 0:SCOLS].bitcast(I32)
        s_tile = BUF[:, 400:400 + SCOLS].bitcast(I32)
        s_tilef = BUF[:, 800:800 + SCOLS]
        s_mask = BUF[:, 1200:1200 + SCOLS]
        s_scan = BUF[:, 1600:1600 + SCOLS]
        s_rank = BUF[:, 2000:2000 + SCOLS]
        s_tmp = BUF[:, 2400:2400 + SCOLS]
        s_src = BUF[:, 2800:2800 + SCOLS].bitcast(I32)
        s_w = BUF[:, 3200:3200 + SCOLS]
        s_tmpi = BUF[:, 3600:3600 + SCOLS].bitcast(I32)
        s_cnt = BUF[:, 4000:4000 + BUCKETS]
        s_base = BUF[:, 4032:4032 + BUCKETS]
        s_chk = BUF[:, 4064:4064 + BUCKETS]
        s_chki = BUF[:, 4096:4096 + BUCKETS].bitcast(I32)
        s_scan2 = BUF[:, 6900:6900 + SCOLS]
        s_mask2 = BUF[:, 7300:7300 + SCOLS]
        s_end = BUF[:, 4128:4128 + BUCKETS]
        s_iota = BUF[:, 4160:4160 + CH_MAIN]
        s_tidx = BUF[:, 4600:4600 + CH_MAIN]
        zeros = BUF[:, 5200:5200 + (CH_MAIN + PADROWS) * 4].bitcast(I32)
        sort_free = sem("sort_free")

        def sort_loads(sp, s, src, dst, w):
            full = s.edges // s.cols
            rest = s.edges - full * s.cols
            todo = [(s_src, src), (s_dst, dst)] + ([(s_w, w)] if w is not None else [])
            n = 0
            for tile, ap in todo:
                sp.dma_start(tile[0:full, 0:s.cols], ap[0:full * s.cols].rearrange("(p c) -> p c", c=s.cols)
                             ).then_inc(s.loaded, 16)
                n += 16
                if rest:
                    sp.dma_start(tile[full:full + 1, 0:rest], ap[full * s.cols:s.edges].rearrange("(p c) -> p c", p=1)
                                 ).then_inc(s.loaded, 16)
                    n += 16
            return n

        n_main = 96
        n_gat = n_main + 32

        def sort_dve(e, s, n_loaded, weighted):
            cols = s.cols
            dst, tile_i, tilef = s_dst[:, 0:cols], s_tile[:, 0:cols], s_tilef[:, 0:cols]
            mask, scan, rank, tmp = s_mask[:, 0:cols], s_scan[:, 0:cols], s_rank[:, 0:cols], s_tmp[:, 0:cols]
            tmpi = s_tmpi[:, 0:cols]
            e.wait_ge(s.loaded, n_loaded)
            e.tensor_scalar(tile_i, dst, 7, None, ALU.arith_shift_right)
            e.memset(rank, 0.0)
            e.drain()
            e.tensor_copy(tilef, tile_i)
            e.drain()
            for t in range(BUCKETS):
                e.tensor_scalar((mask, tmp)[t % 2], tilef, float(t), 0.0, ALU.is_equal, ALU.add, s_cnt[:, t:t + 1])
                if t % 2:
                    e.drain()
            e.drain().then_inc(s.count_ok, 1)
            e.wait_ge(s.sums_ok, s.n)
            e.tensor_scalar(s_chk, bank(7, BUCKETS, 64), float(P - 1), None, ALU.add)
            e.tensor_copy(s_base, bank(7, BUCKETS, 0))
            e.drain()
            e.tensor_copy(s_chki, s_chk)
            e.drain()
            e.tensor_scalar(s_chki, s_chki, 7, None, ALU.arith_shift_right)
            e.drain()
            e.tensor_copy(s_chk, s_chki)
            e.drain()
            e.tensor_tensor_scan(s_end, s_chk, s_chk, 0.0, ALU.add, ALU.max)
            e.drain()
            e.tensor_tensor(s_chk, s_end, s_chk, ALU.subtract)
            e.drain()
            e.tensor_scalar(s_chk, s_chk, float(P), None, ALU.mult)
            e.drain()
            e.tensor_tensor(s_base, s_base, s_chk, ALU.add)
            e.drain()
            scans, masks, sums = (scan, s_scan2[:, 0:cols]), (mask, s_mask2[:, 0:cols]), (rank, tmp)
            e.memset(tmp, 0.0)
            for t in range(0, BUCKETS, 2):
                for i in range(2):
                    e.tensor_scalar(masks[i], tilef, float(t + i), None, ALU.is_equal)
                e.drain()
                for i in range(2):
                    e.tensor_tensor_scan(scans[i], masks[i], masks[i], s_base[:, t + i:t + i + 1], ALU.add, ALU.max)
                e.drain()
                for i in range(2):
                    e.tensor_tensor(scans[i], masks[i], scans[i], ALU.mult)
                e.drain()
                for i in range(2):
                    e.tensor_tensor(sums[i], sums[i], scans[i], ALU.add)
            e.drain()
            e.scalar_tensor_tensor(rank, rank, -1.0, tmp, ALU.add, ALU.add)
            e.drain()
            e.tensor_copy(tmpi, rank)
            e.drain()
            e.tensor_scalar(tile_i, tmpi, 7, None, ALU.arith_shift_right)
            e.tensor_scalar(tmpi, tmpi, 127, None, ALU.bitwise_and)
            e.drain()
            e.tensor_copy(tmp, tile_i)
            e.tensor_copy(scan, tmpi)
            e.drain()
            e.scalar_tensor_tensor(tmp, scan, float(s.chunks + PADROWS), tmp, ALU.mult, ALU.add)
            e.drain()
            e.tensor_copy(s.pos[:, :], tmp)
            rec = v3(s.rec[:, :], 4)
            recf = v3(s.rec[:, :].bitcast(F32), 4)
            e.tensor_copy(rec[:, :, 0], s_src[:, 0:cols])
            e.tensor_scalar(tile_i, dst, 127, None, ALU.bitwise_and)
            e.drain()
            e.tensor_scalar(mask, tilef, float(NT), None, ALU.is_lt)
            e.tensor_copy(recf[:, :, LANE], tile_i)
            if weighted:
                e.tensor_copy(recf[:, :, 2], s_w[:, 0:cols])
            else:
                e.tensor_copy(rec[:, :, 2], dst)
            e.drain()
            e.tensor_copy(recf[:, :, 3], mask)
            e.drain().then_inc(s.pos_ok, 1)
            e.memset(s_tidx[0:1, 0:s.chunks], 0.0)
            e.drain()
            for t in range(NT):
                e.scalar_tensor_tensor(s_tidx[0:1, 0:s.chunks], s_iota[0:1, 0:s.chunks], s_end[0:1, t:t + 1],
                                       s_tidx[0:1, 0:s.chunks], ALU.is_ge, ALU.add)
                e.drain()
            e.tensor_scalar(s_tidx[0:1, 0:s.chunks], s_tidx[0:1, 0:s.chunks], float(NT - 1), None, ALU.min)
            e.drain()
            e.tensor_copy(s.tiles[0:1, :], s_tidx[0:1, 0:s.chunks])
            e.drain()

        def sort_pe(pe, s):
            pe.wait_ge(s.count_ok, s.n)
            pe.matmul(bank(7, BUCKETS, 0), upper[:, :], s_cnt, start=True, stop=True)
            pe.matmul(bank(7, BUCKETS, 64), ones[:, :], s_cnt, start=True, stop=True).then_inc(s.sums_ok, 1)

        def sort_pool(e, s):
            e.wait_ge(s.pos_ok, 1)
            pool_wait(e, s.cleared, 16)
            dest = s.rec_d

            def half_turn(k, half):
                col = k * (2 * s.per) + half * s.per
                e.tensor_copy(s.ids[half][:, :], s.pos[:, bass.ds(col, s.per)])
                e.tensor_copy(s.rows[half][:, :], s.rec[:, bass.ds(col * 4, s.per * 4)]).then_inc(s.slot, 1)
                pool_wait(e, s.slot, k * 2 + (half + 1))
                for j in range(s.per):
                    e.indirect_dma_start(dest, bass.IndirectOffsetOnAxis(ap=s.ids[half][:, j:j + 1], axis=0),
                                         s.rows[half][:, 4 * j:4 * j + 4], None).then_inc(s.scat[half], 16)

            half_turn(0, 0)
            with e.Fori(0, s.turns - 1) as k:
                half_turn(k, 1)
                pool_wait(e, s.scat[0], (k + 1) * (16 * s.per))
                half_turn(k + 1, 0)
                pool_wait(e, s.scat[1], (k + 1) * (16 * s.per))
            half_turn(s.turns - 1, 1)

        class Norm:
            var_ok, sd_ok, xn_ok, out = (sem("ln_" + x) for x in ("var_ok", "sd_ok", "xn_ok", "out"))

            def __init__(s, number):
                s.n = number + 1
                s.written = 16 * s.n

        norms = [Norm(i) for i in range(4)]

        def norm_dve(e, s):
            with e.Fori(0, TURNS) as t:
                for j in range(TI):
                    e.bn_stats(bn[:, bass.ds((t * TI + j) * 6, 6)], X[:, bass.ds((t * TI + j) * C, C)])
            e.drain()
            for t in range(NT):
                e.bn_aggr(mv[:, t * 2:t * 2 + 2], bn[:, t * 6:t * 6 + 6])
            e.drain().then_inc(s.var_ok, 1)
            e.wait_ge(s.sd_ok, s.n)
            e.reciprocal(rs[:, :], sd[:, :])
            e.drain()
            with e.Fori(0, TURNS) as t:
                for j in range(TI):
                    n = t * TI + j
                    e.tensor_scalar(ACC[:, bass.ds(n * 257, C)], X[:, bass.ds(n * C, C)], mv[:, bass.ds(n * 2, 1)],
                                    rs[:, bass.ds(n, 1)], ALU.subtract, ALU.mult)
            e.drain().then_inc(s.xn_ok, 1)

        def norm_act(e, s):
            e.wait_ge(s.var_ok, s.n)
            e.activation(sd[:, :], v3(mv[:, :], 2)[:, :, 1], ACT.Sqrt, bias=eps_ln[:, 0:1]).then_inc(s.sd_ok, 1)

        def acc_to_dram(sp, table, done):
            sp.dma_start(table.rearrange("(t p) c -> p t c", p=P), v3(ACC[:, :], 257)[:, :, 0:C]).then_inc(done, 16)

        class Front:
            xs_in, xt_tp, xt_out = sem("xs_in"), sem("xt_tp"), sem("xt_out")
            turns_before = loads = rows = 0

            def __init__(s, loads=True):
                s.before, s.loads_before, s.rows_before = Front.turns_before, Front.loads, Front.rows
                Front.turns_before += TURNS
                Front.loads += TURNS if loads else 0
                Front.rows += 0 if loads else TURNS

            def tiles(s, turn, n):
                return turn * TI + (s.before * TI + n)

            def loaded(s, turn):
                return turn * 16 + (s.loads_before * 16 + 16)

        def rows_of(table, s):
            return table[bass.ds(s * W, W), :].rearrange("(j p) c -> p j c", p=P)

        def front_sp(sp, f, table, more=()):
            sp.dma_start(XS3, table[0:W, :].rearrange("(j p) c -> p j c", p=P)).then_inc(f.xs_in, 16)
            with sp.Fori(1, TURNS) as s:
                sp.wait_ge(f.xt_tp, f.tiles(s, 0))
                for q, per in more:
                    sp.wait_ge(q, s * per)
                sp.dma_start(XS3, rows_of(table, s)).then_inc(f.xs_in, 16)

        def front_pe(pe, f, s):
            for j in range(TI):
                if j == 0:
                    pe.wait_ge(f.xs_in, f.loaded(s))
                if j >= 2:
                    pe.wait_ge(f.xt_out, f.tiles(s, j - 1))
                for c in range(2):
                    mm = pe.transpose(bank(j % 2, P, c * P), XS3[:, j, c * P:(c + 1) * P], ident[:, :])
                mm.then_inc(f.xt_tp, 1)

        def front_act(e, f, s):
            for j in range(TI):
                e.wait_ge(f.xt_tp, f.tiles(s, j + 1))
                e.activation(XT3[:, :, j * P:(j + 1) * P], v3(bank(j % 2, 2 * P), P), ACT.Copy).then_inc(f.xt_out, 1)

        fronts = {n: Front(n not in ("fg", "fp", "fq")) for n in ("fa", "fb", "fg", "fp", "ff", "f0", "f1", "f2", "f3", "fm", "fn",
                                                "fq")}

        wk_wv = v3(WT[:, 0:1024], 512)
        wq0 = v3(WT[:, 1024:1536], 256)
        wm0 = v3(WT[:, 1536:2048], 256)
        w1m = v3(WT[:, 2048:4096], 512)
        w2m = v3(WT[:, 4096:5120], 256)
        wg0 = v3(WT[:, 5120:5632], 256)
        g1r, b1r, g2r, b2r = (ROWS[:, i * C:(i + 1) * C] for i in range(4))
        w_in0 = sem("w_in0")

        MN = BUF[:, 0:TI * C]
        EX = BUF[:, 1280:1280 + TI * C]
        KS = BUF[:, 2560:2560 + TI * C]
        VS = BUF[:, 3840:3840 + TI * 258]
        KR = BUF[:, 5200:5200 + TI * C]
        KVA = WS[:, 0:258]
        KVB = WS[:, 260:516]
        ZB = WS[:, 516:772]
        VALS = WS[:, 780:785]
        kv_mm, kv_mn, kv_ex, ks_ok, vs_ok, kva_mm = (sem("kv_" + x) for x in ("mm", "mn", "ex", "ks", "vs", "acc"))
        vals_ok = sem("vals_ok")

        def mixA_pe(pe, s):
            f = fronts["fa"]
            front_pe(pe, f, s)
            for j in range(TI):
                pe.wait_ge(f.xt_out, f.tiles(s, j + 1))
                if j >= 3:
                    pe.wait_ge(vs_ok, s * TI + (j - 2))
                for c in range(2):
                    mm = pe.matmul(bank(2 + j % 3), XT3[:, c, j * P:(j + 1) * P], wk_wv[:, c, :],
                                   start=(c == 0), stop=(c == 1))
                mm.then_inc(kv_mm, 1)
            for j in range(TI):
                pe.wait_ge(ks_ok, s * TI + (j + 1))
                pe.wait_ge(vs_ok, s * TI + (j + 1))
                for h in range(2):
                    mm = pe.matmul(bank(5 + h, 129), KS[:, j * C + h * P:j * C + (h + 1) * P],
                                   VS[:, j * 258 + h * 129:j * 258 + (h + 1) * 129],
                                   start=(j == 0), stop=(j == TI - 1))
            mm.then_inc(kva_mm, 1)

        def mixA_act(e, s):
            front_act(e, fronts["fa"], s)
            for j in range(TI):
                if j == 0:
                    e.wait_ge(vals_ok, s + 1)
                e.wait_ge(kv_mm, s * TI + (j + 1))
                e.activation(KR[:, j * C:(j + 1) * C], bank(2 + j % 3, C), ACT.Copy)
                e.activation(v3(VS[:, j * 258:(j + 1) * 258], 129)[:, :, 0:P], v3(bank(2 + j % 3, C, C), P),
                             ACT.Copy, scale=VALS[:, j:j + 1])
                e.activation(v3(VS[:, j * 258:(j + 1) * 258], 129)[:, :, P:P + 1], v3(ones[:, 0:2], 1),
                             ACT.Copy, scale=VALS[:, j:j + 1])
                e.drain().then_inc(vs_ok, 1)
            for j in range(TI):
                e.wait_ge(kv_mn, s * TI + (j + 1))
                e.activation(EX[:, j * C:(j + 1) * C], MN[:, j * C:(j + 1) * C], ACT.Exp).then_inc(kv_ex, 1)

        def mixA_dve(e, s):
            e.tensor_copy(VALS, valid[:, bass.ds(s * TI, TI)]).then_inc(vals_ok, 1)
            for j in range(TI):
                e.wait_ge(vs_ok, s * TI + (j + 1))
                e.tensor_scalar(MN[:, j * C:(j + 1) * C], KR[:, j * C:(j + 1) * C], 0.0, None, ALU.min
                                ).then_inc(kv_mn, 1)
            for i in range(TI):
                e.wait_ge(kv_ex, s * TI + (i + 1))
                e.scalar_tensor_tensor(KS[:, i * C:(i + 1) * C], KR[:, i * C:(i + 1) * C], 0.0,
                                       EX[:, i * C:(i + 1) * C], ALU.max, ALU.add).then_inc(ks_ok, 1)
            e.wait_ge(kva_mm, s + 1)
            for h in range(2):
                e.tensor_tensor(KVA[:, h * 129:(h + 1) * 129], bank(5 + h, 129), KVA[:, h * 129:(h + 1) * 129], ALU.add)

        QN = BUF[:, 0:4 * HALF]
        QE = BUF[:, 1280:1280 + 4 * HALF]
        QT = v3(BUF[:, 2560:2560 + 2 * W], W)
        RD = BUF[:, 0:4 * HALF]
        MT = v3(BUF[:, 3840:3840 + 2 * W], W)
        LM = BUF[:, 5120:5120 + TI * C]
        XM = v3(BUF[:, 6400:6400 + 2 * W], W)
        HT = BUF[:, 7680:7680 + 4 * W]
        (q_mm, q_mn, q_ex, q_ok, nd_mm, mt_ok, m_mm, m_var, m_sd, lm_ok, lm_tp, xm_ok, h_mm, ht_ok, y_mm, y_var,
         y_sd, xb_ok) = (sem("b_" + x) for x in (
             "q_mm", "q_mn", "q_ex", "q_ok", "nd_mm", "mt_ok", "m_mm", "m_var", "m_sd", "lm_ok", "lm_tp", "xm_ok",
             "h_mm", "ht_ok", "y_mm", "y_var", "y_sd", "xb_ok"))
        NUMBANK = (6, 7, 0, 1)

        def mixB_pe(pe, s):
            f = fronts["fb"]
            front_pe(pe, f, s)
            pe.wait_ge(f.xt_out, f.tiles(s, TI))
            for i in range(4):
                mc, hf = i // 2, i % 2
                for c in range(2):
                    mm = pe.matmul(bank(2 + i, HALF), wq0[:, c, mc * P:(mc + 1) * P],
                                   XT3[:, c, hf * HALF:(hf + 1) * HALF], start=(c == 0), stop=(c == 1))
                mm.then_inc(q_mm, 1)
            for i in range(4):
                mc, hf = i // 2, i % 2
                pe.wait_ge(q_ok, s * 4 + (i + 1))
                q = QT[:, mc, hf * HALF:(hf + 1) * HALF]
                pe.matmul(bank(NUMBANK[i], HALF), KVB[:, mc * P:(mc + 1) * P], q, start=True, stop=True)
                pe.matmul(bank(2 + i, HALF), ZB[:, mc * P:(mc + 1) * P], q, start=True, stop=True).then_inc(nd_mm, 1)
            pe.wait_ge(mt_ok, s + 1)
            for j in range(TI):
                for c in range(2):
                    mm = pe.matmul(bank(2 + j, C), MT[:, c, j * P:(j + 1) * P], wm0[:, c, :],
                                   start=(c == 0), stop=(c == 1))
                mm.then_inc(m_mm, 1)
            for j in range(TI):
                if j == 0:
                    pe.wait_ge(lm_ok, s + 1)
                if j >= 2:
                    pe.wait_ge(xm_ok, s * TI + (j - 1))
                for c in range(2):
                    mm = pe.transpose(bank(j % 2, P, c * P), LM[:, j * C + c * P:j * C + (c + 1) * P], ident[:, :])
                mm.then_inc(lm_tp, 1)
            pe.wait_ge(xm_ok, s * TI + TI)
            for i in range(8):
                mc, hf = i // 2, i % 2
                if i >= 6:
                    pe.wait_ge(ht_ok, s * 8 + (i - 5))
                for c in range(4):
                    src = XT3 if c < 2 else XM
                    mm = pe.matmul(bank(2 + i % 6, HALF), w1m[:, c, mc * P:(mc + 1) * P],
                                   src[:, c % 2, hf * HALF:(hf + 1) * HALF], start=(c == 0), stop=(c == 3))
                mm.then_inc(h_mm, 1)
            pe.wait_ge(ht_ok, s * 8 + 8)
            for j in range(TI):
                for c in range(4):
                    mm = pe.matmul(bank(2 + j, C), HT[:, c * W + j * P:c * W + (j + 1) * P], w2m[:, c, :],
                                   start=(c == 0), stop=(c == 3))
                mm.then_inc(y_mm, 1)

        def mixB_act(e, s):
            front_act(e, fronts["fb"], s)
            for i in range(4):
                e.wait_ge(q_mn, s * 4 + (i + 1))
                e.activation(QE[:, i * HALF:(i + 1) * HALF], QN[:, i * HALF:(i + 1) * HALF], ACT.Exp).then_inc(q_ex, 1)
            e.wait_ge(m_var, s + 1)
            e.activation(sd[:, 0:TI], v3(mv[:, 0:2 * TI], 2)[:, :, 1], ACT.Sqrt, bias=eps_ln[:, 0:1]).then_inc(m_sd, 1)
            for j in range(TI):
                e.wait_ge(lm_tp, s * TI + (j + 1))
                e.activation(XM[:, :, j * P:(j + 1) * P], v3(bank(j % 2, 2 * P), P), ACT.Copy).then_inc(xm_ok, 1)
            for i in range(8):
                mc, hf = i // 2, i % 2
                e.wait_ge(h_mm, s * 8 + (i + 1))
                e.activation(HT[:, mc * W + hf * HALF:mc * W + (hf + 1) * HALF], bank(2 + i % 6, HALF), ACT.Relu
                             ).then_inc(ht_ok, 1)
            e.wait_ge(y_var, s + 1)
            e.activation(sd[:, 0:TI], v3(mv[:, 0:2 * TI], 2)[:, :, 1], ACT.Sqrt, bias=eps_ln[:, 0:1]).then_inc(y_sd, 1)

        def norm_five(e, s, mm, var, sdq, g, b):
            for j in range(TI):
                e.wait_ge(mm, s * TI + (j + 1))
                e.bn_stats(bn[:, j * 6:(j + 1) * 6], bank(2 + j, C))
            e.drain()
            for j in range(TI):
                e.bn_aggr(mv[:, 2 * j:2 * j + 2], bn[:, j * 6:(j + 1) * 6])
            e.drain().then_inc(var, 1)
            e.wait_ge(sdq, s + 1)
            e.reciprocal(rs[:, 0:TI], sd[:, 0:TI])
            e.drain()
            for j in range(TI):
                e.tensor_scalar(LM[:, j * C:(j + 1) * C], bank(2 + j, C), mv[:, 2 * j:2 * j + 1], rs[:, j:j + 1],
                                ALU.subtract, ALU.mult)
            e.drain()
            lm3 = v3(LM, C)
            e.tensor_tensor(lm3, lm3, g.rearrange("p (o c) -> p o c", o=1).to_broadcast([P, TI, C]), ALU.mult)
            e.drain()
            e.tensor_tensor(lm3, lm3, b.rearrange("p (o c) -> p o c", o=1).to_broadcast([P, TI, C]), ALU.add)
            e.drain()

        def mixB_dve(e, s):
            e.wait_ge(Front.xs_in, fronts["fb"].loaded(s))
            e.tensor_tensor(X[:, bass.ds(s * (TI * C), TI * C)], X[:, bass.ds(s * (TI * C), TI * C)], XS[:, :], ALU.add
                            ).then_inc(xb_ok, 1)
            for i in range(4):
                e.wait_ge(q_mm, s * 4 + (i + 1))
                e.tensor_scalar(QN[:, i * HALF:(i + 1) * HALF], bank(2 + i, HALF), 0.0, None, ALU.min).then_inc(q_mn, 1)
            for i in range(4):
                e.wait_ge(q_ex, s * 4 + (i + 1))
                e.scalar_tensor_tensor(QT[:, i // 2, (i % 2) * HALF:(i % 2 + 1) * HALF], bank(2 + i, HALF), 0.0,
                                       QE[:, i * HALF:(i + 1) * HALF], ALU.max, ALU.add).then_inc(q_ok, 1)
            for i in range(4):
                e.wait_ge(nd_mm, s * 4 + (i + 1))
                e.tensor_scalar(RD[:, i * HALF:(i + 1) * HALF], bank(2 + i, HALF), 1e-6, None, ALU.add)
            e.drain()
            e.reciprocal(RD, RD)
            e.drain()
            for i in range(4):
                e.tensor_tensor(MT[:, i // 2, (i % 2) * HALF:(i % 2 + 1) * HALF], bank(NUMBANK[i], HALF),
                                RD[:, i * HALF:(i + 1) * HALF], ALU.mult)
            e.drain().then_inc(mt_ok, 1)
            norm_five(e, s, m_mm, m_var, m_sd, g1r, b1r)
            e.drain().then_inc(lm_ok, 1)
            norm_five(e, s, y_mm, y_var, y_sd, g2r, b2r)
            e.tensor_tensor(X[:, bass.ds(s * (TI * C), TI * C)], X[:, bass.ds(s * (TI * C), TI * C)], LM, ALU.add)

        G = BUF[:, 0:GROUP * 257]
        OH = BUF[:, 4112:4112 + GROUP * P]
        HOT = BUF[:, 6160:6160 + GROUP * P]
        WTS = BUF[:, 8208:8208 + GROUP]
        rec3f = v3(rec_main[:, :].bitcast(F32), 4)
        HB = 4

        class Hop:
            ids = sem("hop_ids")
            rows = [sem(f"hop_rows{i}") for i in range(4)]
            hot, oh, mm, add = sem("hop_hot"), sem("hop_oh"), sem("hop_mm"), sem("hop_add")

            def __init__(s, number, table, field):
                s.table, s.field = table, field
                s.turns0 = number * (CH_MAIN // GROUP)

        hops = [Hop(0, xn_d[0], 3), Hop(1, xn_d[2], 2), Hop(2, cur_d[0], 2), Hop(3, cur_d[1], 2)]

        def hop_pool(e, s):
            with e.Fori(0, CH_MAIN // GROUP) as k:
                for half in range(2):
                    pool_wait(e, s.mm, k * GROUP + (s.turns0 * GROUP + 8 * (half + 1)))
                    e.tensor_copy(ib[half][:, :], v3(rec_main[:, bass.ds((k * GROUP + 8 * half) * 4, 32)], 4)[:, :, 0]
                                  ).then_inc(s.ids, 1)
                    pool_wait(e, s.ids, k * 2 + (s.turns0 * 2 + half + 1))
                    for j in range(8):
                        slot = 8 * half + j
                        e.indirect_dma_start(G[:, slot * 257:slot * 257 + C], None, s.table,
                                             bass.IndirectOffsetOnAxis(ap=ib[half][:, j:j + 1], axis=0)
                                             ).then_inc(s.rows[slot // 4], 16)

        def hop_pe(pe, s):
            with pe.Fori(0, CH_MAIN // GROUP) as k:
                for j in range(GROUP):
                    if j % 4 == 0:
                        pe.wait_ge(s.rows[j // 4], k * 64 + (s.turns0 * 64 + 64))
                    pe.wait_ge(s.oh, k * GROUP + (s.turns0 * GROUP + j + 1))
                    pe.wait_ge(s.add, k * GROUP + (s.turns0 * GROUP + j + 1))
                    pe.matmul(bank(j % HB, 257), OH[:, j * P:(j + 1) * P], G[:, j * 257:(j + 1) * 257],
                              start=True, stop=True).then_inc(s.mm, 1)

        def one_hots(e, dst, lanes, k, op):
            lane = v3(lanes[:, bass.ds(k * (GROUP * 4), GROUP * 4)], 4)[:, :, LANE:LANE + 1].to_broadcast([P, GROUP, P])
            column = iota_row[:, :].rearrange("p (o c) -> p o c", o=1).to_broadcast([P, GROUP, P])
            return e.tensor_tensor(v3(dst, P), column, lane, op)

        def hop_act(e, s):
            with e.Fori(0, CH_MAIN // GROUP) as k:
                e.wait_ge(s.hot, k + (s.turns0 + 1))
                for j in range(GROUP):
                    e.activation(OH[:, j * P:(j + 1) * P], HOT[:, j * P:(j + 1) * P], ACT.Copy, scale=WTS[:, j:j + 1]
                                 ).then_inc(s.oh, 1)

        def hop_dve(e, s):
            recf = rec_main[:, :].bitcast(F32)
            with e.Fori(0, CH_MAIN // GROUP) as k:
                e.tensor_scalar(WTS, v3(recf[:, bass.ds(k * (GROUP * 4), GROUP * 4)], 4)[:, :, s.field], 1.0, None, ALU.mult)
                one_hots(e, HOT, recf, k, ALU.is_equal)
                e.drain().then_inc(s.hot, 1)
                tiles = tiles_of(tile_main, k)
                for j in range(GROUP):
                    e.wait_ge(s.mm, k * GROUP + (s.turns0 * GROUP + j + 1 + GROUP))
                    dst = ACC[:, bass.ds(tiles[j] * 257, 257)]
                    e.tensor_tensor(dst, bank(j % HB, 257), dst, ALU.add)
                    e.drain().then_inc(s.add, 1)

        DEG = WS[:, 800:825]
        g0_rows, g0_mm, deg_ok, dsd_ok = sem("g0_rows"), sem("g0_mm"), sem("deg_ok"), sem("dsd_ok")

        def gnn0_pe(pe, s):
            f = fronts["fg"]
            for j in range(TI):
                if j == 0:
                    pe.wait_ge(g0_rows, s + 1)
                if j >= 2:
                    pe.wait_ge(f.xt_out, f.tiles(s, j - 1))
                for c in range(2):
                    mm = pe.transpose(bank(j % 2, P, c * P), XS3[:, j, c * P:(c + 1) * P], ident[:, :])
                mm.then_inc(f.xt_tp, 1)
            for j in range(TI):
                pe.wait_ge(f.xt_out, f.tiles(s, j + 1))
                for c in range(2):
                    mm = pe.matmul(bank(2 + j, C), XT3[:, c, j * P:(j + 1) * P], wg0[:, c, :],
                                   start=(c == 0), stop=(c == 1))
                mm.then_inc(g0_mm, 1)

        def gnn0_dve(e, s):
            for j in range(TI):
                e.tensor_scalar(XS3[:, j, :], ACC[:, bass.ds((s * TI + j) * 257, C)], DEG[:, bass.ds(s * TI + j, 1)],
                                None, ALU.mult)
            e.drain().then_inc(g0_rows, 1)
            add_banks(e, s, g0_mm)

        def add_banks(e, s, mm, before=0):
            for j in range(TI):
                e.wait_ge(mm, s * TI + (before + j + 1))
                x = X[:, bass.ds((s * TI + j) * C, C)]
                e.tensor_tensor(x, bank(2 + j, C), x, ALU.add)

        def narrow_pe(pe, f, s, w, n, mm):
            for j in range(TI):
                if j == 0:
                    pe.wait_ge(g0_rows, s + (f.rows_before + 1))
                if j >= 2:
                    pe.wait_ge(f.xt_out, f.tiles(s, j - 1))
                for c in range(2):
                    m = pe.transpose(bank(j % 2, P, c * P), XS3[:, j, c * P:(c + 1) * P], ident[:, :])
                m.then_inc(f.xt_tp, 1)
            for j in range(TI):
                pe.wait_ge(f.xt_out, f.tiles(s, j + 1))
                for c in range(2):
                    m = pe.matmul(bank(2 + j, n), XT3[:, c, j * P:(j + 1) * P], w[:, c, :], start=(c == 0), stop=(c == 1))
                m.then_inc(mm, 1)

        def narrow_dve(e, s, dst, pitch, n, mm):
            e.tensor_scalar(XS3, v3(ACC[:, bass.ds(s * (TI * 257), TI * 257)], 257)[:, :, 0:C], 1.0, None, ALU.mult
                            ).then_inc(g0_rows, 1)
            for j in range(TI):
                e.wait_ge(mm, s * TI + (j + 1))
                e.tensor_scalar(dst[:, bass.ds((s * TI + j) * pitch, n)], bank(2 + j, n), 1.0, None, ALU.mult)

        wgat = v3(WS[:, 900:932], 16)
        wgate = v3(WS[:, 940:956], 8)
        attrow = ROWS[:, 1024:1104]
        SRT = WT[:, 8192:8192 + NT * 20]
        DTT = WT[:, 8700:8700 + NT * 8]
        MX = WT[:, 8900:9000]
        ES = WT[:, 9000:9100]
        SC = WT[:, 9100:9200]
        AG = WT[:, 9200:9200 + NT * 20]
        GT = WT[:, 9700:9700 + NT * 16]
        GG = WT[:, 10240:10240 + CH_GAT * 20]
        STB = BUF[:, 2624:2624 + NT * 32]
        SPL = BUF[:, 3424:3474].bitcast(BF16)
        REST = BUF[:, 3480:3580]
        GSL = BUF[:, 0:GROUP * 32]
        DSL = BUF[:, 320:320 + GROUP * 8]
        EE = BUF[:, 448:448 + GROUP * 4]
        MSG = BUF[:, 512:512 + GROUP * 20]
        RED = BUF[:, 832:832 + GROUP * 4]
        OM = BUF[:, 1024:2048].bitcast(BF16)
        ASRC = BUF[:, 2048:2048 + GH * 96]
        SELF = BUF[:, 2592:2592 + GROUP]
        AT = BUF[0:96, 3600:3856].bitcast(BF16)
        SEL = BUF[:, 2568:2568 + GROUP // 2].bitcast(BF16)
        OHG = BUF[:, 4096:4096 + GROUP * P]
        gp_mm, src_ready, src_out, dst_ready, dst_out = (sem(x) for x in (
            "gp_mm", "src_ready", "src_out", "dst_ready", "dst_out"))
        gat_ids = sem("gat_ids")
        gat_rows = [sem(f"gat_rows{i}") for i in range(2)]
        gat_oh, gat_mm, gat_add, gat_tp, gat_at, gat_msg, gat_e, gat_ex = (sem("gat_" + x) for x in (
            "oh", "mm", "add", "tp", "at", "msg", "e", "ex"))
        gat_kept = sem("gat_kept")
        GTURNS = CH_GAT // GROUP
        sc_var, sc_sd, sc_e, sc_ex = (sem("sc_" + x) for x in ("var", "sd", "e", "ex"))

        def gat_pool(e, second):
            t0 = GTURNS if second else 0
            slots, width, table, field = (DSL, 8, dst_tab_d, 2) if second else (GSL, 32, src_tab_d, 0)
            with e.Fori(0, GTURNS) as k:
                for half in range(2):
                    if second:
                        pool_wait(e, gat_e, k * 2 + (half + 1))
                    else:
                        pool_wait(e, gat_kept, k * 2 + (half + 1))
                    e.tensor_copy(ib[half][:, :], v3(rec_gat[:, bass.ds((k * GROUP + 8 * half) * 4, 32)], 4)[:, :, field]
                                  ).then_inc(gat_ids, 1)
                    pool_wait(e, gat_ids, k * 2 + (t0 * 2 + half + 1))
                    for j in range(8):
                        slot = 8 * half + j
                        e.indirect_dma_start(slots[:, slot * width:(slot + 1) * width], None, table,
                                             bass.IndirectOffsetOnAxis(ap=ib[half][:, j:j + 1], axis=0)
                                             ).then_inc(gat_rows[half], 16)

        def gatA_act(e):
            with e.Fori(0, GTURNS) as k:
                e.wait_ge(gat_tp, k + 1)
                for half in range(2):
                    e.wait_ge(gat_rows[half], k * 128 + 128)
                    e.sem_inc(carried, 1)
                    rows = v3(GSL[:, 256 * half:256 * half + 256], 32)
                    e.activation(v3(GG[:, bass.ds((k * GROUP + 8 * half) * 20, 160)], 20), rows[:, :, 0:20], ACT.Copy)
                    for q in range(3):
                        e.activation(ASRC.rearrange("p (h q j) -> p q j h", h=GH, q=3)[:, q, 8 * half:8 * half + 8],
                                     rows[:, :, 20 + 4 * q:24 + 4 * q], ACT.Copy)
                    e.drain().then_inc(gat_kept, 1)
                e.wait_ge(gat_tp, k + 2)
                e.activation(AT, bank(4, 512, 0, 96), ACT.Copy).then_inc(gat_at, 1)

        def gatA_pe(pe):
            with pe.Fori(0, GTURNS) as k:
                for half in range(2):
                    pe.wait_ge(gat_kept, k * 2 + (3 + half))
                pe.wait_ge(gat_at, k + 1)
                for h in range(GH):
                    mm = pe.transpose(bank(4, P, h * P, 96), ASRC[:, h * 96:(h + 1) * 96], ident[:, :])
                mm.then_inc(gat_tp, 1)
                pe.wait_ge(gat_at, k + 2)
                pe.wait_ge(gat_oh, k + 1)
                for j in range(GROUP):
                    pe.wait_ge(gat_add, k * GROUP + (j + 1))
                    pe.matmul(bank(j % 4), SEL[0:96, j:j + 1].to_broadcast([96, P]), AT, start=True, stop=False)
                    pe.matmul(bank(j % 4), OM[:, j * P:(j + 1) * P], ident_b[:, :], start=False, stop=True
                              ).then_inc(gat_mm, 1)

        def gatA_dve(e):
            with e.Fori(0, GTURNS) as k:
                one_hots(e, OM, rec_gat[:, :].bitcast(F32), k, ALU.not_equal)
                e.drain().then_inc(gat_oh, 1)
                tiles = tiles_of(tile_gat, k)
                for j in range(GROUP):
                    e.wait_ge(gat_mm, k * GROUP + (j + 1 + GROUP))
                    e.tensor_reduce(RED[:, j * 4:j * 4 + 4], v3(bank(j % 4), P), AX.X, ALU.max)
                    e.drain().then_inc(gat_add, 1)
                    m = MX[:, bass.ds(tiles[j] * 4, 4)]
                    e.tensor_tensor(m, m, RED[:, j * 4:j * 4 + 4], ALU.max)
                e.drain()

        def gatB_act(e):
            with e.Fori(0, GTURNS) as k:
                e.wait_ge(gat_e, k * 2 + 4)
                e.activation(EE, EE, ACT.Exp).then_inc(gat_ex, 1)

        def gatB_pe(pe):
            g0 = GTURNS * GROUP
            with pe.Fori(0, GTURNS) as k:
                for j in range(GROUP):
                    pe.wait_ge(gat_msg, k + 1)
                    pe.wait_ge(gat_add, k * GROUP + (g0 + j + 1))
                    pe.matmul(bank(j % 4, 20), OHG[:, j * P:(j + 1) * P], MSG[:, j * 20:(j + 1) * 20],
                              start=True, stop=True).then_inc(gat_mm, 1)

        def gatB_dve(e):
            g0 = GTURNS * GROUP
            EE3 = v3(EE, 4)
            with e.Fori(0, GTURNS) as k:
                tiles = tiles_of(tile_gat, k)
                one_hots(e, OHG, rec_gat[:, :].bitcast(F32), k, ALU.is_equal)
                gg = v3(GG[:, bass.ds(k * (GROUP * 20), GROUP * 20)], 20)
                for half in range(2):
                    lo, hi = 8 * half, 8 * half + 8
                    ee, ee3, dsl = EE[:, lo * 4:hi * 4], EE3[:, lo:hi, :], v3(DSL, 8)[:, lo:hi, :]
                    e.wait_ge(gat_rows[half], k * 128 + (GTURNS * 128 + 128))
                    seq(e, lambda: e.tensor_tensor(ee3, gg[:, lo:hi, 16:20], dsl[:, :, 0:4], ALU.add),
                        lambda: e.scalar_tensor_tensor(ee, ee, 0.2, ee, ALU.mult, ALU.max),
                        lambda: e.tensor_tensor(ee3, ee3, dsl[:, :, 4:8], ALU.subtract),
                        lambda: e.tensor_scalar(ee, ee, 0.0, None, ALU.min))
                    e.drain().then_inc(gat_e, 1)
                e.wait_ge(gat_ex, k + 1)
                e.tensor_tensor(v3(MSG, 20)[:, :, 0:16].rearrange("p g (h e) -> p g h e", h=GH),
                                gg[:, :, 0:16].rearrange("p g (h e) -> p g h e", h=GH),
                                EE3.rearrange("p g (h o) -> p g h o", o=1).to_broadcast([P, GROUP, GH, GE]), ALU.mult)
                e.tensor_copy(v3(MSG, 20)[:, :, 16:20], EE3)
                e.drain().then_inc(gat_msg, 1)
                for j in range(GROUP):
                    e.wait_ge(gat_mm, k * GROUP + (g0 + j + 1 + GROUP))
                    dst = AG[:, bass.ds(tiles[j] * 20, 20)]
                    e.tensor_tensor(dst, bank(j % 4, 20), dst, ALU.add)
                    e.drain().then_inc(gat_add, 1)

        def seq(e, *steps):
            for step in steps:
                step()
                e.drain()

        def over_tiles(row, n):
            return row.rearrange("p (o c) -> p o c", o=1).to_broadcast([P, NT, n])

        def head_sum(e, dst, tab, att, tmp):
            seq(e, lambda: e.tensor_tensor(v3(tmp, 16), tab, over_tiles(att, 16), ALU.mult),
                lambda: e.tensor_reduce(dst, tmp.rearrange("p (t h e) -> p t h e", h=GH, e=GE), AX.X, ALU.add))

        def gat_tables_dve(e):
            srt, dtt = v3(SRT, 20), v3(DTT, 8)
            head_sum(e, srt[:, :, 16:20], srt[:, :, 0:16], attrow[:, 0:16], GT)
            stb, spl, rest = v3(STB, 32), v3(SPL, 4), v3(REST, 4)
            part = [stb[:, :, 20 + 4 * q:24 + 4 * q] for q in range(3)]
            seq(e, lambda: e.tensor_copy(stb[:, :, 0:20], srt),
                lambda: e.tensor_copy(spl, srt[:, :, 16:20]),
                lambda: e.tensor_copy(part[0], spl),
                lambda: e.tensor_tensor(rest, srt[:, :, 16:20], part[0], ALU.subtract),
                lambda: e.tensor_copy(spl, rest),
                lambda: e.tensor_copy(part[1], spl),
                lambda: e.tensor_tensor(part[2], rest, part[1], ALU.subtract))
            e.drain().then_inc(src_ready, 1)
            e.memset(ASRC, 0.0)
            e.tensor_tensor(SELF, ident[:, 0:GROUP], ident[:, 32:32 + GROUP], ALU.add)
            e.drain()
            e.tensor_tensor(SEL, SELF, ident[:, 64:64 + GROUP], ALU.add)
            head_sum(e, dtt[:, :, 0:4], srt[:, :, 0:16], attrow[:, 16:32], GT)
            e.tensor_copy(v3(MX, 4), srt[:, :, 16:20])
            rf = v3(rec_gat[:, :].bitcast(F32), 4)
            e.wait_ge(gat.back, 16)
            lane = rf[:, :, LANE]
            seq(e, lambda: e.scalar_tensor_tensor(lane, lane, 1.0, rf[:, :, 3], ALU.add, ALU.mult),
                lambda: e.tensor_scalar(lane, lane, -1.0, None, ALU.add))

        def gat_max_dve(e):
            srt, dtt, mx, es, ag = v3(SRT, 20), v3(DTT, 8), v3(MX, 4), v3(ES, 4), v3(AG, 20)
            seq(e, lambda: e.tensor_tensor(mx, mx, dtt[:, :, 0:4], ALU.add),
                lambda: e.scalar_tensor_tensor(dtt[:, :, 4:8], mx, 0.2, mx, ALU.mult, ALU.max))
            e.drain().then_inc(dst_ready, 1)
            seq(e, lambda: e.tensor_tensor(es, srt[:, :, 16:20], dtt[:, :, 0:4], ALU.add),
                lambda: e.scalar_tensor_tensor(ES, ES, 0.2, ES, ALU.mult, ALU.max),
                lambda: e.tensor_tensor(es, es, dtt[:, :, 4:8], ALU.subtract))
            e.drain().then_inc(sc_e, 1)
            e.wait_ge(sc_ex, 1)
            e.tensor_copy(ag[:, :, 16:20], es)
            e.tensor_tensor(ag[:, :, 0:16].rearrange("p g (h e) -> p g h e", h=GH),
                            srt[:, :, 0:16].rearrange("p g (h e) -> p g h e", h=GH),
                            es.rearrange("p g (h o) -> p g h o", o=1).to_broadcast([P, NT, GH, GE]), ALU.mult)
            e.drain()

        def top_two(e, s, n, rank, tmp, sel):
            s3, r3, t3 = v3(s, n), v3(rank, n), v3(tmp, n)
            e.memset(rank, 0.0)
            for j in range(n):
                sj = s3[:, :, j:j + 1]
                e.tensor_tensor(t3[:, :, 0:j + 1], sj.to_broadcast([P, NT, j + 1]), s3[:, :, 0:j + 1], ALU.is_gt)
                if j + 1 < n:
                    e.tensor_tensor(t3[:, :, j + 1:n], sj.to_broadcast([P, NT, n - j - 1]), s3[:, :, j + 1:n], ALU.is_ge)
                e.drain()
                e.tensor_tensor(rank, rank, tmp, ALU.add)
                e.drain()
            e.tensor_scalar(sel, rank, 2.0, None, ALU.is_lt)
            e.drain()

        def bc(col, n):
            return col.rearrange("p (t o) -> p t o", o=1).to_broadcast([P, NT, n])

        def gat_scores_dve(e):
            ag, gt, es, sc = v3(AG, 20), v3(GT, 16), v3(ES, 4), v3(SC, 4)
            col, col2 = sd[:, :], rs[:, :]
            g4 = gt.rearrange("p t (h e) -> p t h e", h=GH)
            seq(e, lambda: e.tensor_scalar(es, ag[:, :, 16:20], 1e-16, None, ALU.add),
                lambda: e.reciprocal(ES, ES),
                lambda: e.tensor_tensor(g4, ag[:, :, 0:16].rearrange("p t (h e) -> p t h e", h=GH),
                                        es.rearrange("p g (h o) -> p g h o", o=1).to_broadcast([P, NT, GH, GE]), ALU.mult),
                lambda: e.tensor_tensor(gt, gt, over_tiles(attrow[:, 32:48], 16), ALU.add),
                lambda: e.tensor_reduce(col, gt, AX.X, ALU.add),
                lambda: e.tensor_scalar(col, col, 1.0 / 16, None, ALU.mult),
                lambda: e.tensor_tensor(gt, gt, bc(col, 16), ALU.subtract),
                lambda: e.tensor_tensor(ag[:, :, 0:16], gt, gt, ALU.mult),
                lambda: e.tensor_reduce(col, ag[:, :, 0:16], AX.X, ALU.add),
                lambda: e.tensor_scalar(col, col, 1.0 / 16, LN_EPS, ALU.mult, ALU.add))
            e.drain().then_inc(sc_var, 1)
            e.wait_ge(sc_sd, 1)
            seq(e, lambda: e.reciprocal(col, col2),
                lambda: e.tensor_tensor(gt, gt, bc(col, 16), ALU.mult),
                lambda: e.tensor_tensor(gt, gt, over_tiles(attrow[:, 48:64], 16), ALU.mult),
                lambda: e.tensor_tensor(gt, gt, over_tiles(attrow[:, 64:80], 16), ALU.add),
                lambda: e.tensor_reduce(sc, GT.rearrange("p (t h e) -> p t e h", h=GH, e=GE), AX.X, ALU.add),
                lambda: e.tensor_scalar(SC, SC, 1.0 / GH, None, ALU.mult),
                lambda: e.tensor_reduce(col, sc, AX.X, ALU.max))
            top_two(e, SC, EXP0, MX, GT[:, 0:100], ES)
            g = gates[:, 0:NT * EXP0]
            e.tensor_tensor(v3(g, 4), sc, bc(col, 4), ALU.subtract)
            e.drain().then_inc(sc_e, 1)
            e.wait_ge(sc_ex, 2)
            seq(e, lambda: e.tensor_tensor(g, g, ES, ALU.mult),
                lambda: e.tensor_reduce(col, v3(g, 4), AX.X, ALU.add),
                lambda: e.reciprocal(col2, col),
                lambda: e.tensor_tensor(v3(g, 4), v3(g, 4), bc(col2, 4), ALU.mult))

        FH = BUF[:, 0:2 * 4 * W]
        GTS = BUF[0:8, 5120:5120 + W]
        GC = WS[:, 1270:1270 + TI * 8]
        B1T = WS[:, 960:992]
        B2R = WS[0:8, 1010:1266]
        moe_gc, moe_gt, moe_gts, moe_b2, moe_b2a, moe_h, moe_ha, moe_y, moe_ya = (sem("moe_" + x) for x in (
            "gc", "gt", "gts", "b2", "b2a", "h", "ha", "y", "ya"))
        w_ffn, rows_ffn = sem("w_ffn"), sem("rows_ffn")
        YB = (6, 7, 0, 1)

        class Moe:
            def __init__(s, n, front):
                s.n, s.f = n, fronts[front]
                s.w1 = WT[:, 0:n * 1024].rearrange("p (e k n) -> p e k n", e=n, k=2)
                s.w2 = WT[:, n * 1024:n * 2048].rearrange("p (e k n) -> p e k n", e=n, k=4)

        moe0 = Moe(EXP0, "ff")

        def moe_pe(pe, m, s):
            f, E = m.f, m.n
            front_pe(pe, f, s)
            pe.wait_ge(moe_gc, s + 1)
            for j in range(TI):
                mm = pe.transpose(bank(6 + j // 4, P, (j % 4) * P, E), GC[:, j * E:(j + 1) * E], ident[:, :])
            mm.then_inc(moe_gt, 1)
            pe.wait_ge(moe_gts, s + 1)
            for j in range(TI):
                pe.matmul(bank(2 + j, C), GTS[0:E, j * P:(j + 1) * P], B2R[0:E, :], start=True, stop=True
                          ).then_inc(moe_b2, 1)
            pe.wait_ge(f.xt_out, f.tiles(s, TI))
            pe.wait_ge(moe_b2a, s * TI + TI)

            def hidden(e):
                for i in range(8):
                    mc, hf, n = i // 2, i % 2, e * 8 + i
                    if n >= 4:
                        pe.wait_ge(moe_ha, s * (8 * E) + (n - 3))
                    for c in range(2):
                        mm = pe.matmul(bank(2 + i % 4, HALF), m.w1[:, e, c, mc * P:(mc + 1) * P],
                                       XT3[:, c, hf * HALF:(hf + 1) * HALF], start=(c == 0), stop=(c == 1))
                    mm.then_inc(moe_h, 1)

            hidden(0)
            for e in range(E):
                if e + 1 < E:
                    hidden(e + 1)
                pe.wait_ge(moe_ha, s * (8 * E) + (8 * (e + 1)))
                for j in range(TI):
                    n = e * TI + j
                    if n >= 4:
                        pe.wait_ge(moe_ya, s * (TI * E) + (n - 3))
                    for c in range(4):
                        at = (e % 2) * 4 * W + c * W + j * P
                        mm = pe.matmul(bank(YB[n % 4], C), FH[:, at:at + P], m.w2[:, e, c, :], start=(c == 0),
                                       stop=(c == 3))
                    mm.then_inc(moe_y, 1)

        def moe_act(e, m, s):
            E = m.n
            front_act(e, m.f, s)
            e.wait_ge(moe_gt, s + 1)
            e.activation(GTS[0:E, 0:4 * P], bank(6, 4 * P, 0, E), ACT.Copy)
            e.activation(GTS[0:E, 4 * P:5 * P], bank(7, P, 0, E), ACT.Copy)
            e.drain().then_inc(moe_gts, 1)
            for x in range(E):
                for i in range(8):
                    mc, hf = i // 2, i % 2
                    e.wait_ge(moe_h, s * (8 * E) + (x * 8 + i + 1))
                    if i == 0 and x >= 2:
                        e.wait_ge(moe_y, s * (TI * E) + (TI * (x - 1)))
                    at = (x % 2) * 4 * W + mc * W + hf * HALF
                    e.activation(FH[:, at:at + HALF], bank(2 + i % 4, HALF), ACT.Gelu, bias=B1T[:, x * 4 + mc:x * 4 + mc + 1]
                                 ).then_inc(moe_ha, 1)

        def moe_dve(e, m, s):
            E = m.n
            e.tensor_scalar(GC[:, 0:TI * E], gates[:, bass.ds(s * (TI * E), TI * E)], 1.0, None, ALU.mult
                            ).then_inc(moe_gc, 1)
            for j in range(TI):
                x = X[:, bass.ds((s * TI + j) * C, C)]
                e.wait_ge(moe_b2, s * TI + (j + 1))
                e.tensor_tensor(x, bank(2 + j, C), x, ALU.add).then_inc(moe_b2a, 1)
            for i in range(E):
                e.drain()
                for j in range(TI):
                    n = i * TI + j
                    x = X[:, bass.ds((s * TI + j) * C, C)]
                    e.wait_ge(moe_y, s * (TI * E) + (n + 1))
                    e.scalar_tensor_tensor(x, bank(YB[n % 4], C), GC[:, j * E + i:j * E + i + 1], x, ALU.mult, ALU.add
                                           ).then_inc(moe_ya, 1)

        wsh = v3(WT[:, 0:2048], C)
        g1_mm = sem("g1_mm")

        def gnn1_pe(pe, i, s):
            f = fronts[f"f{i}"]
            front_pe(pe, f, s)
            for j in range(TI):
                pe.wait_ge(f.xt_out, f.tiles(s, j + 1))
                for c in range(2):
                    mm = pe.matmul(bank(2 + j, C), XT3[:, c, j * P:(j + 1) * P], wsh[:, 2 * i + c, :],
                                   start=(c == 0), stop=(c == 1))
                mm.then_inc(g1_mm, 1)

        wqkv = v3(WT[:, 2048:3584], C)
        wqkvT = v3(WT[:, 3584:5120], 768)
        wproj = v3(WT[:, 5120:5632], C)
        wprojT = v3(WT[:, 5632:6144], C)
        HV = 33
        MF = WT[:, 6144:6144 + FC * 8 * HV]
        F0 = WT[:, 7680:7680 + 8 * FC * P]
        F1 = BUF[:, 0:8 * FC * P]
        HS = 4 * FG * 32
        MFT = BUF[0:HV, 0:2 * HS]
        YT = WT[0:HV, 12800:12800 + 8 * P]
        KV = BUF[:, 5120:5120 + TI * 512]
        V1 = BUF[:, 7680:7680 + TI * 8 * HV]
        K2 = BUF[:, 9088:9088 + 2 * 512]
        SQ = BUF[:, 10112:10112 + C]
        OB = BUF[:, 5120 + 1280:5120 + 2560]
        XO = v3(BUF[:, 7680:7680 + 2 * W], W)
        RN = WS[:, 1320:1360]
        RI = WS[:, 1360:1400]
        TS = WS[:, 1400:1408]
        coef = WS[:, 1000:1000 + FC]
        bq, bkv = ROWS[:, 0:C], ROWS[:, C:3 * C]
        bproj, obias, temp = ROWS[:, 768:1024], ROWS[:, 1104:1360], ROWS[:, 1360:1368]
        w_in1, rows_in1 = sem("w_in1"), sem("rows_in1")
        (m_tp, m_kv, m_sq, m_rt, m_f, m_fu, m_fq, m_ft, m_y1, m_ob, m_xo, m_xe, m_p) = (
            sem("m1_" + x) for x in ("tp", "kv", "sq", "rt", "f", "fu", "fq", "ft", "y", "ob", "xo",
                                     "xe", "p"))
        m_ke, m_k2, m_fp, m_ma, m_yt, m_z = (sem("m1_" + x) for x in ("ke", "k2", "fp", "ma", "yt", "z"))

        def weights_pe(pe):
            pe.wait_ge(w_in1, 48)
            blocks = [(wqkv[:, r, c * P:(c + 1) * P]) for c in range(2) for r in range(6)]
            blocks += [(wproj[:, r, c * P:(c + 1) * P]) for c in range(2) for r in range(2)]
            for i, b in enumerate(blocks):
                mm = pe.transpose(bank(i // 4, P, (i % 4) * P), b, ident[:, :])
            mm.then_inc(m_tp, 1)

        def weights_act(e):
            e.wait_ge(m_tp, 1)
            e.activation(WT[:, 3584:4096], bank(0), ACT.Copy)
            e.activation(WT[:, 4096:4608], bank(1), ACT.Copy)
            e.activation(WT[:, 4608:5120], bank(2), ACT.Copy)
            e.activation(WT[:, 5632:6144], bank(3), ACT.Copy)

        def features(e, dst, k2, heads, offsets, linear=True):
            k3 = v3(k2, 64)
            f3 = dst.rearrange("p (h g i) -> p h g i", h=heads, i=32)
            for r in offsets:
                e.tensor_tensor(f3[:, :, r, :], k3[:, :, 0:32], k3[:, :, r:r + 32], ALU.mult)
            if linear:
                e.tensor_scalar(f3[:, :, R2, :], k3[:, :, 0:32], 1.0, None, ALU.mult)

        def norms_dve(e, j, src):
            e.tensor_tensor(SQ, src, src, ALU.mult)
            e.drain()
            e.tensor_reduce(RN[:, j * 8:(j + 1) * 8], v3(SQ, 32), AX.X, ALU.add)
            e.drain()

        def double_rows(e, j, src, k2, h0, heads):
            r = RI[:, j * 8 + h0:j * 8 + h0 + heads].rearrange("p (h o) -> p h o", o=1).to_broadcast([P, heads, 32])
            for half in range(2):
                e.tensor_tensor(v3(k2, 64)[:, :, 32 * half:32 * half + 32], v3(src, 32), r, ALU.mult)
            e.drain()

        def m1A_pe(pe, s):
            f = fronts["fm"]
            front_pe(pe, f, s)
            for j in range(TI):
                pe.wait_ge(f.xt_out, f.tiles(s, TI))
                if j >= 3:
                    pe.wait_ge(m_ke, s * TI + (j - 2))
                for c in range(2):
                    mm = pe.matmul(bank(j % 3), XT3[:, c, j * P:(j + 1) * P], wqkvT[:, c, C:3 * C],
                                   start=(c == 0), stop=(c == 1))
                mm.then_inc(m_kv, 1)
            for n in range(2 * TI):
                half, j = n // TI, n % TI
                pe.wait_ge(m_f, s * (2 * TI) + (n + 1))
                pe.wait_ge(m_fp, s * (2 * TI) + (n + 1))
                if n == TI:
                    pe.wait_ge(m_ma, s * 2 + 1)
                for h in range(4):
                    v = V1[:, (j * 8 + half * 4 + h) * HV:(j * 8 + half * 4 + h + 1) * HV]
                    at = (n % 2) * 4 * FC * P + h * FC * P
                    pe.matmul(bank(3 + h, 512, 0, HV), v, F0[:, at:at + 512], start=(j == 0), stop=(j == TI - 1))
                    mm = pe.matmul(bank(7, 96, h * 96, HV), v, F0[:, at + 512:at + 608],
                                   start=(j == 0 and h == 0), stop=(j == TI - 1), skip_group_check=True)
                mm.then_inc(m_fu, 1)

        def m1A_end_pe(pe):
            pe.wait_ge(m_ma, 2 * TURNS)
            for c in range(FC):
                rows = min(P, FG * 32 - c * P)
                for h in range(8):
                    at = (h // 4) * HS + ((h % 4) * 512 + c * P if c < 4 else 2048 + (h % 4) * 96)
                    mm = pe.transpose(bank(c, HV, h * HV, rows), MFT[:, at:at + rows], ident[0:HV, 0:HV])
            mm.then_inc(m_tp, 1)

        POOL_R = 12

        def m1A_pool(e):
            with e.Fori(0, TURNS) as s:
                for n in range(2 * TI):
                    pool_wait(e, m_k2, s * (2 * TI) + (n + 1))
                    if n >= 2:
                        pool_wait(e, m_fu, s * (2 * TI) + (n - 1))
                    features(e, F0[:, (n % 2) * 2560:(n % 2 + 1) * 2560], K2[:, (n % 2) * 512:(n % 2) * 512 + 256], 4,
                             range(POOL_R, R2), False)
                    e.drain().then_inc(m_fp, 1)

        def m1A_dve(e, s):
            for j in range(TI):
                e.wait_ge(m_kv, s * TI + (j + 1))
                e.tensor_tensor(KV[:, j * 512:(j + 1) * 512], bank(j % 3), bkv, ALU.add)
                e.drain().then_inc(m_ke, 1)
            for j in range(TI):
                k = KV[:, j * 512:j * 512 + C]
                norms_dve(e, j, k)
                v1 = v3(V1[:, j * 8 * HV:(j + 1) * 8 * HV], HV)
                vd = valid[:, bass.ds(s * TI + j, 1)]
                e.tensor_scalar(v1[:, :, 1:HV], v3(KV[:, j * 512 + C:(j + 1) * 512], 32), vd, None, ALU.mult)
                e.tensor_scalar(v1[:, :, 0:1], v3(ones[:, 0:8], 1), vd, None, ALU.mult)
            e.drain().then_inc(m_sq, 1)
            e.wait_ge(m_rt, s + 1)
            seq(e, lambda: e.tensor_scalar(RN, RN, 1e-12, None, ALU.max),
                lambda: e.reciprocal(RI, RN),
                lambda: e.tensor_scalar(RI, RI, SCALE1, None, ALU.mult))
            def take_sums(half):
                e.wait_ge(m_fu, s * (2 * TI) + (half + 1) * TI)
                m = MFT[:, half * HS:(half + 1) * HS]
                e.tensor_tensor(m, ps[0:HV, 3 * 512:3 * 512 + HS], m, ALU.add)
                e.drain().then_inc(m_ma, 1)

            for n in range(2 * TI):
                half, j = n // TI, n % TI
                k2 = K2[:, (n % 2) * 512:(n % 2) * 512 + 256]
                if n >= 2:
                    e.wait_ge(m_fp, s * (2 * TI) + (n - 1))
                double_rows(e, j, KV[:, j * 512 + half * P:j * 512 + half * P + P], k2, 4 * half, 4)
                e.drain().then_inc(m_k2, 1)
                if n >= 2:
                    e.wait_ge(m_fu, s * (2 * TI) + (n - 1))
                features(e, F0[:, (n % 2) * 2560:(n % 2 + 1) * 2560], k2, 4, range(POOL_R))
                e.drain().then_inc(m_f, 1)
                if n == TI:
                    take_sums(0)
            take_sums(1)

        def m1_act(e, f, s, t0):
            front_act(e, f, s)
            e.wait_ge(m_sq, s + (t0 + 1))
            e.activation(RN, RN, ACT.Sqrt).then_inc(m_rt, 1)

        TB = (4, 5, 0, 1)

        def m1B_pe(pe, s):
            f = fronts["fn"]
            front_pe(pe, f, s)
            pe.wait_ge(f.xt_out, f.tiles(s, TI))
            for j in range(TI):
                for c in range(2):
                    mm = pe.matmul(bank(2 + j, C), XT3[:, c, j * P:(j + 1) * P], wqkvT[:, c, 0:C],
                                   start=(c == 0), stop=(c == 1))
                mm.then_inc(m_kv, 1)
            def back(j):
                pe.wait_ge(m_yt, s * TI + (j + 1))
                if j >= 2:
                    pe.wait_ge(m_ob, s * TI + (j - 1))
                pe.sem_inc(carried, 1)
                for h in range(8):
                    mm = pe.transpose(bank(2 + j % 2, HV, h * HV), YT[:, h * P:(h + 1) * P], ident[0:HV, 0:HV])
                mm.then_inc(m_z, 1)

            for j in range(TI):
                pe.wait_ge(m_f, s * TI + (2 * NT + j + 1))
                for i in range(10):
                    n = j * 10 + i
                    if n >= 4:
                        pe.wait_ge(m_ft, s * 50 + (n - 3))
                    b = TB[n % 4]
                    for q in range(4):
                        if i < 8:
                            at = i * FC * P + q * P
                            mm = pe.transpose(bank(b, P, q * P), F0[:, at:at + P], ident[:, :])
                        else:
                            at = ((i - 8) * 4 + q) * FC * P + 4 * P
                            mm = pe.transpose(bank(b, P, q * P, 96), F0[:, at:at + 96], ident[:, :])
                    mm.then_inc(m_fq, 1)
                if j >= 1:
                    back(j - 1)
                pe.wait_ge(m_ft, s * 50 + (j * 10 + 10))
                for h in range(8):
                    for c in range(FC):
                        rows = min(P, FG * 32 - c * P)
                        at = h * 512 + c * P if c < 4 else 4096 + h * P
                        mm = pe.matmul(bank(6 + h // 4, P, (h % 4) * P, HV),
                                       MF[0:rows, c * 8 * HV + h * HV:c * 8 * HV + (h + 1) * HV], F1[0:rows, at:at + P],
                                       start=(c == 0), stop=(c == FC - 1), skip_group_check=True)
                mm.then_inc(m_y1, 1)
            back(TI - 1)
            for j in range(TI):
                if j == 0:
                    pe.wait_ge(m_ob, s * TI + TI)
                if j >= 2:
                    pe.wait_ge(m_xe, s * TI + (j - 1))
                for c in range(2):
                    mm = pe.transpose(bank(j % 2, P, c * P), OB[:, j * C + c * P:j * C + (c + 1) * P], ident[:, :])
                mm.then_inc(m_xo, 1)
            for j in range(TI):
                pe.wait_ge(m_xe, s * TI + (j + 1))
                for c in range(2):
                    mm = pe.matmul(bank(2 + j, C), XO[:, c, j * P:(j + 1) * P], wprojT[:, c, :],
                                   start=(c == 0), stop=(c == 1))
                mm.then_inc(m_p, 1)

        def m1B_act(e, s):
            m1_act(e, fronts["fn"], s, TURNS)
            def results(j):
                e.wait_ge(m_y1, s * TI + (j + 1))
                if j >= 1:
                    e.wait_ge(m_z, s * TI + j)
                e.activation(YT, ps[0:HV, 6 * 512:8 * 512], ACT.Copy).then_inc(m_yt, 1)

            for j in range(TI):
                if j >= 1:
                    results(j - 1)
                for i in range(10):
                    n = j * 10 + i
                    e.wait_ge(m_fq, s * 50 + (n + 1))
                    b = TB[n % 4]
                    if i < 8:
                        e.activation(F1[:, i * 512:(i + 1) * 512], bank(b), ACT.Copy).then_inc(m_ft, 1)
                    else:
                        e.activation(F1[0:96, 4096 + (i - 8) * 512:4096 + (i - 7) * 512], bank(b, 512, 0, 96), ACT.Copy
                                     ).then_inc(m_ft, 1)
            results(TI - 1)
            for j in range(TI):
                e.wait_ge(m_xo, s * TI + (j + 1))
                e.activation(XO[:, :, j * P:(j + 1) * P], v3(bank(j % 2, 2 * P), P), ACT.Copy).then_inc(m_xe, 1)

        def m1B_dve(e, s):
            for j in range(TI):
                e.wait_ge(m_kv, s * TI + (NT + j + 1))
                q = KV[:, j * C:(j + 1) * C]
                seq(e, lambda: e.tensor_tensor(q, bank(2 + j, C), bq, ALU.add),
                    lambda: e.tensor_scalar(q, q, SCALE1, None, ALU.mult))
                norms_dve(e, j, q)
            e.drain().then_inc(m_sq, 1)
            e.wait_ge(m_rt, s + (TURNS + 1))
            seq(e, lambda: e.tensor_scalar(RN, RN, 1e-12, None, ALU.max),
                lambda: e.reciprocal(RI, RN),
                lambda: e.tensor_tensor(v3(RI, 8), v3(RI, 8), TS.rearrange("p (o h) -> p o h", o=1).to_broadcast([P, TI, 8]),
                                        ALU.mult))

            def tile_out(j):
                e.wait_ge(m_z, s * TI + (j + 1))
                y = v3(bank(2 + j % 2, 8 * HV), HV)
                e.reciprocal(RN[:, j * 8:(j + 1) * 8].rearrange("p (h o) -> p h o", o=1), y[:, :, 0:1])
                e.drain()
                r = RN[:, j * 8:(j + 1) * 8].rearrange("p (h o) -> p h o", o=1).to_broadcast([P, 8, 32])
                e.tensor_tensor(v3(OB[:, j * C:(j + 1) * C], 32), y[:, :, 1:HV], r, ALU.mult)
                e.drain().then_inc(m_ob, 1)

            for j in range(TI):
                double_rows(e, j, KV[:, j * C:(j + 1) * C], K2[:, 0:512], 0, 8)
                if j >= 1:
                    e.wait_ge(m_fq, s * 50 + j * 10)
                features(e, F0, K2[:, 0:512], 8, range(R2))
                e.drain().then_inc(m_f, 1)
                if j >= 1:
                    tile_out(j - 1)
            tile_out(TI - 1)
            add_banks(e, s, m_p)

        LG = BUF[:, 8192:8192 + NT * 8]
        GR = BUF[:, 8448:8448 + NT * 8]
        GM = BUF[:, 8704:8704 + NT * 8]
        GSEL = BUF[:, 8960:8960 + NT * 8]
        gbrow = ROWS[:, 2000:2008]
        gl_mm, gl_e, gl_ex = sem("gl_mm"), sem("gl_e"), sem("gl_ex")

        def gates1_dve(e):
            col, col2 = sd[:, :], rs[:, :]
            lg = v3(LG, 8)
            seq(e, lambda: e.tensor_tensor(lg, lg, over_tiles(gbrow, 8), ALU.add),
                lambda: e.tensor_reduce(col, lg, AX.X, ALU.max),
                lambda: e.tensor_tensor(lg, lg, bc(col, 8), ALU.subtract))
            e.drain().then_inc(gl_e, 1)
            e.wait_ge(gl_ex, 1)
            seq(e, lambda: e.tensor_reduce(col, lg, AX.X, ALU.add),
                lambda: e.reciprocal(col2, col),
                lambda: e.tensor_tensor(lg, lg, bc(col2, 8), ALU.mult))
            top_two(e, LG, EXP1, GR, GM, GSEL)
            e.tensor_tensor(gates[:, :], LG, GSEL, ALU.mult)

        UC = 3
        PAIRS = -(-(-(-(2 * N + EXP1 * (P - 1)) // P)) // UC) * UC
        TRASH = (PAIRS + 1) * P
        PLACES = TRASH + 2 * P
        xs_d = dram("xs_d", [PLACES, C])
        ys_d = dram("ys_d", [PLACES, C])
        w1x, w2x = WT[:, 0:EXP1 * 1024], WT[:, EXP1 * 1024:EXP1 * 2048]
        B1X = BUF[:, 0:EXP1 * HID]
        B2X = BUF[:, 4096:4096 + EXP1 * C]
        XC = BUF[:, 6144:6144 + UC * C]
        HX = BUF[:, 6912:6912 + UC * HID]
        HXT = BUF[:, 8448:8448 + UC * HID]
        YX = BUF[:, 9984:9984 + UC * C]
        YG = BUF[:, 0:TI * 2 * C]
        PSEL = BUF[:, 9216:9216 + NT * 8]
        PTOT = BUF[:, 9420:9420 + NT * 8]
        PSCN = BUF[:, 9624:9624 + NT * 8]
        PPOS = BUF[:, 9828:9828 + NT * 8]
        PL = [WS[:, 0:NT], WS[:, 32:32 + NT]]
        PLI = [WS[:, 64:64 + NT].bitcast(I32), WS[:, 96:96 + NT].bitcast(I32)]
        PG = [WS[:, 128:128 + NT], WS[:, 160:160 + NT]]
        PINV = WS[:, 192:192 + NT]
        PLANE = [WS[:, 224:225], WS[:, 225:226]]
        PCH, PCHI, PEND = WS[:, 232:240], WS[:, 240:248].bitcast(I32), WS[:, 248:256]
        PTMP = WS[0:1, 256:320]
        expert_of = tile_gat[0:1, 0:64]
        assert PAIRS + UC < 64
        (px_sel, px_mm, px_ok, px_scat, fx_tp, fx_xt, fx_h, fx_hb, fx_g, fx_t2, fx_ht, fx_o, fx_y, ys_out, ys_free,
         yg_used) = (sem("x_" + x) for x in (
             "sel", "mm", "ok", "scat", "tp", "xt", "h", "hb", "g", "t2", "ht", "o", "y", "out", "free", "used"))
        xc_in = [sem(f"xc_in{i}") for i in range(UC)]
        yg_rows = [sem(f"yg_rows{i}") for i in range(TI)]
        x_zero = sem("x_zero")
        XZ = 1536
        x_zeros = -(-(PLACES // P * C) // XZ) + 1

        def places_pe(pe):
            pe.wait_ge(px_sel, 1)
            pe.matmul(bank(7, NT * 8), upper[:, :], PSEL, start=True, stop=True)
            pe.matmul(bank(6, NT * 8), ones[:, :], PSEL, start=True, stop=True)
            pe.matmul(bank(5, 1), upper[:, :], ones[:, 0:1], start=True, stop=True).then_inc(px_mm, 1)

        def places_dve(e):
            sel, tot, scn, pos = v3(PSEL, 8), v3(PTOT, 8), v3(PSCN, 8), v3(PPOS, 8)
            e.tensor_tensor(sel, v3(GSEL, 8), bc(valid[:, :], 8), ALU.mult)
            e.drain().then_inc(px_sel, 1)
            e.wait_ge(px_mm, 1)
            for i in range(2):
                e.tensor_scalar(PLANE[i], bank(5, 1), float(TRASH + i * P), None, ALU.add)
            e.tensor_copy(PTOT, bank(6, NT * 8))
            e.drain()
            for x in range(EXP1):
                e.tensor_tensor_scan(scn[:, :, x], tot[:, :, x], tot[:, :, x], 0.0, ALU.add, ALU.max)
            e.drain()
            seq(e, lambda: e.tensor_scalar(PCH, scn[:, NT - 1, :], float(P - 1), None, ALU.add),
                lambda: e.tensor_copy(PCHI, PCH),
                lambda: e.tensor_scalar(PCHI, PCHI, 7, None, ALU.arith_shift_right),
                lambda: e.tensor_copy(PCH, PCHI),
                lambda: e.tensor_tensor_scan(PEND, PCH, PCH, 0.0, ALU.add, ALU.max),
                lambda: e.tensor_tensor(PCH, PEND, PCH, ALU.subtract),
                lambda: e.tensor_scalar(PCH, PCH, float(P), 1.0, ALU.mult, ALU.add),
                lambda: e.tensor_tensor(pos, scn, tot, ALU.subtract),
                lambda: e.tensor_tensor(PPOS, PPOS, bank(7, NT * 8), ALU.add),
                lambda: e.tensor_tensor(pos, pos, PCH.rearrange("p (o x) -> p o x", o=1).to_broadcast([P, NT, 8]), ALU.add),
                lambda: e.tensor_tensor(PPOS, PPOS, PSEL, ALU.mult),
                lambda: e.tensor_reduce(PL[1], pos, AX.X, ALU.max),
                lambda: e.tensor_reduce(PL[0], pos, AX.X, ALU.add),
                lambda: e.tensor_tensor(PL[0], PL[0], PL[1], ALU.subtract))
            for i, tmp in enumerate((PTOT, PSCN)):
                seq(e, lambda: e.tensor_scalar(PINV, valid[:, :], 0.0, PLANE[i], ALU.is_equal, ALU.mult),
                    lambda: e.tensor_tensor(v3(tmp, 8), pos, bc(PL[i], 8), ALU.is_equal),
                    lambda: e.tensor_tensor(tmp, tmp, gates[:, :], ALU.mult),
                    lambda: e.tensor_reduce(PG[i], v3(tmp, 8), AX.X, ALU.add),
                    lambda: e.scalar_tensor_tensor(PL[i], PL[i], -1.0, PINV, ALU.add, ALU.max),
                    lambda: e.tensor_copy(PLI[i], PL[i]))
            e.drain().then_inc(px_ok, 1)
            e.memset(PTMP, 0.0)
            e.drain()
            for x in range(EXP1 - 1):
                e.scalar_tensor_tensor(PTMP, iota_row[0:1, 0:64], PEND[0:1, x:x + 1], PTMP, ALU.is_ge, ALU.add)
                e.drain()
            e.tensor_copy(expert_of[0:1, :], PTMP)
            e.drain()

        def experts(engine, k):
            return nc.values_load_multi_w_load_instructions(
                expert_of[0:1, bass.ds(k * UC, UC + 1)], [engine], min_val=0, max_val=EXP1 - 1,
                skip_runtime_bounds_check_because="a count of seven comparisons")[1]

        def scatter_pool(e):
            pool_wait(e, px_ok, 1)
            pool_wait(e, x_zero, 16 * x_zeros)
            for t in range(NT):
                for i in range(2):
                    e.indirect_dma_start(xs_d, bass.IndirectOffsetOnAxis(ap=PLI[i][:, t:t + 1], axis=0),
                                         ACC[:, t * 257:t * 257 + C], None).then_inc(px_scat, 16)

        def chunk_rows(table, c):
            return table[bass.ds(c * P, P), :]

        def loads_sp(sp):
            sp.wait_ge(px_scat, 16 * 2 * NT)
            for i in range(UC):
                sp.dma_start(XC[:, i * C:(i + 1) * C], xs_d[i * P:(i + 1) * P, :]).then_inc(xc_in[i], 16)
            with sp.Fori(1, PAIRS // UC) as k:
                for i in range(UC):
                    sp.wait_ge(fx_tp, k * UC + (i + 1 - UC))
                    sp.dma_start(XC[:, i * C:(i + 1) * C], chunk_rows(xs_d, k * UC + i)).then_inc(xc_in[i], 16)
            sp.wait_ge(fx_tp, PAIRS + 1 - UC)
            sp.dma_start(XC[:, 0:C], xs_d[PAIRS * P:(PAIRS + 1) * P, :]).then_inc(xc_in[0], 16)

        def chunk_in(pe, c, slot, turn):
            pe.wait_ge(xc_in[slot], turn * 16 + 16)
            for h in range(2):
                mm = pe.transpose(bank(0, P, h * P), XC[:, slot * C + h * P:slot * C + (h + 1) * P], ident[:, :])
            mm.then_inc(fx_tp, 1)

        def chunk_hidden(pe, c, slot, x):
            pe.wait_ge(fx_xt, c + 1)
            pe.wait_ge(fx_hb, c + 1)
            for h in range(2):
                mm = pe.matmul(bank(1 + slot, HID), XT[:, slot * C + h * P:slot * C + (h + 1) * P],
                               w1x[:, bass.ds(x * 1024 + h * HID, HID)], start=(h == 0), stop=(h == 1))
            mm.then_inc(fx_h, 1)

        def ffn1_pe(pe):
            chunk_in(pe, 0, 0, 0)
            chunk_hidden(pe, 0, 0, experts(mybir.EngineType.PE, 0)[0])
            with pe.Fori(0, PAIRS // UC) as k:
                x = experts(mybir.EngineType.PE, k)
                for i in range(UC):
                    c, nxt = k * UC + i, (i + 1) % UC
                    chunk_in(pe, c + 1, nxt, k + (i + 1) // UC)
                    pe.wait_ge(fx_g, c + 1)
                    for h in range(4):
                        mm = pe.transpose(bank(4, P, h * P), HX[:, i * HID + h * P:i * HID + (h + 1) * P], ident[:, :])
                    mm.then_inc(fx_t2, 1)
                    chunk_hidden(pe, c + 1, nxt, x[i + 1])
                    pe.wait_ge(fx_ht, c + 1)
                    pe.wait_ge(fx_y, c + 1)
                    for h in range(4):
                        mm = pe.matmul(bank(5 + i, C), HXT[:, i * HID + h * P:i * HID + (h + 1) * P],
                                       w2x[:, bass.ds(x[i] * 1024 + h * C, C)], start=(h == 0), stop=(h == 3))
                    mm.then_inc(fx_o, 1)

        def ffn1_act(e):
            def rows(c, slot):
                e.wait_ge(fx_tp, c + 1)
                e.activation(XT[:, slot * C:(slot + 1) * C], bank(0, C), ACT.Copy).then_inc(fx_xt, 1)

            def gelu(c, slot):
                e.wait_ge(fx_hb, c + (1 + UC))
                e.activation(HX[:, slot * HID:(slot + 1) * HID], HX[:, slot * HID:(slot + 1) * HID], ACT.Gelu
                             ).then_inc(fx_g, 1)

            rows(0, 0)
            gelu(0, 0)
            with e.Fori(0, PAIRS // UC) as k:
                for i in range(UC):
                    c, nxt = k * UC + i, (i + 1) % UC
                    rows(c + 1, nxt)
                    e.wait_ge(fx_t2, c + 1)
                    e.activation(HXT[:, i * HID:(i + 1) * HID], bank(4), ACT.Copy).then_inc(fx_ht, 1)
                    gelu(c + 1, nxt)

        def ffn1_dve(e):
            def bias(c, slot, x):
                e.wait_ge(fx_h, c + 1)
                e.tensor_tensor(HX[:, slot * HID:(slot + 1) * HID], bank(1 + slot, HID), B1X[:, bass.ds(x * HID, HID)],
                                ALU.add).then_inc(fx_hb, 1)

            e.wait_ge(w_ffn, 96)
            bias(0, 0, experts(mybir.EngineType.DVE, 0)[0])
            with e.Fori(0, PAIRS // UC) as k:
                x = experts(mybir.EngineType.DVE, k)
                for i in range(UC):
                    c, nxt = k * UC + i, (i + 1) % UC
                    bias(c + 1, nxt, x[i + 1])
                    if i == 0:
                        e.wait_ge(ys_free, k + 1)
                    e.wait_ge(fx_o, c + 1)
                    e.tensor_tensor(YX[:, i * C:(i + 1) * C], bank(5 + i, C), B2X[:, bass.ds(x[i] * C, C)], ALU.add
                                    ).then_inc(fx_y, 1)

        def ffn1_pool(e):
            with e.Fori(0, PAIRS // UC) as k:
                for i in range(UC):
                    pool_wait(e, fx_y, k * UC + (i + 1 + UC))
                    e.dma_start(chunk_rows(ys_d, k * UC + i), YX[:, i * C:(i + 1) * C]).then_inc(ys_out, 16)
                pool_wait(e, ys_out, k * (16 * UC) + 16 * UC)
                e.sem_inc(ys_free, 1)

        def gather_pool(e):
            for t in range(NT):
                if t == 0:
                    pool_wait(e, yg_used, TI)
                if t >= TI:
                    pool_wait(e, yg_used, t + 1)
                for i in range(2):
                    at = (t % TI * 2 + i) * C
                    e.indirect_dma_start(YG[:, at:at + C], None, ys_d,
                                         bass.IndirectOffsetOnAxis(ap=PLI[i][:, t:t + 1], axis=0)
                                         ).then_inc(yg_rows[t % TI], 16)

        def combine_dve(e, s):
            for j in range(TI):
                x = X[:, bass.ds((s * TI + j) * C, C)]
                e.wait_ge(yg_rows[j], s * 32 + 32)
                for i in range(2):
                    e.scalar_tensor_tensor(x, YG[:, (j * 2 + i) * C:(j * 2 + i + 1) * C], PG[i][:, bass.ds(s * TI + j, 1)],
                                           x, ALU.mult, ALU.add)
                    e.drain()
                e.sem_inc(yg_used, 1)

        block = ctx.enter_context(nc.Block())
        out_done = sem("out_done")
        x_done = sem("x_done")
        dve_ready = sem("dve_ready")
        hop_done, cur_out = sem("hop_done"), sem("cur_out")
        hop_init = sem("hop_init")

        def broadcast_row(ap, n):
            return ap.rearrange(
                "(o n) -> o n", o=1).to_broadcast([P, n])

        @block.sync
        def _(sp):
            full = (NT - 1) * P
            sp.wait_ge(consts_ok, 1)
            sort_loads(sp, main, a["src"], a["dst"], a["edge_weight"])
            sp.dma_start(v3(X[:, 0:(NT - 1) * C], C), a["x"][0:full, :].rearrange("(t p) c -> p t c", p=P)
                         ).then_inc(x_in, 16)
            sp.dma_start(X[0:LAST, (NT - 1) * C:NT * C], a["x"][full:N, :]).then_inc(x_in, 16)
            for s in (main, gat):
                sp.dma_start(s.rec_d.rearrange("(p c) f -> p (c f)", p=P), zeros[:, 0:(s.chunks + PADROWS) * 4]
                             ).then_inc(s.cleared, 16)
            xz = xs_d.rearrange("(p r) c -> p (r c)", p=P)
            for i in range(x_zeros - 1):
                n = min(XZ, xz.shape[1] - i * XZ)
                sp.dma_start(xz[:, i * XZ:i * XZ + n], zeros[:, 0:n].bitcast(F32)).then_inc(x_zero, 16)
            sp.dma_start(ys_d[PAIRS * P:PLACES, :].rearrange("(p r) c -> p (r c)", p=P), zeros[:, 0:3 * C].bitcast(F32)
                         ).then_inc(x_zero, 16)
            for dst, src in ((wk_wv[:, :, 0:C], a["L0_mix_Wk"]), (wk_wv[:, :, C:2 * C], a["L0_mix_Wv"]),
                             (wq0, a["L0_mix_Wq"]), (wm0, a["L0_mix_Wm"]), (w1m, a["L0_mix_W1"]),
                             (w2m, a["L0_mix_W2"]), (wg0, a["L0_gnn_weight"])):
                sp.dma_start(dst, src.rearrange("(k p) n -> p k n", p=P)).then_inc(w_in0, 16)
            for dst, src in ((g1r, "L0_mix_g1"), (b1r, "L0_mix_b1"), (g2r, "L0_mix_g2"), (b2r, "L0_mix_b2")):
                sp.dma_start(dst, broadcast_row(a[src], C)).then_inc(w_in0, 16)
            sp.wait_ge(main.pos_ok, 1)
            sp.wait_ge(sort_free, 1)
            sort_loads(sp, gat, a["L0_ffn_edge_index"][0, :], a["L0_ffn_edge_index"][1, :], None)
            sp.wait_ge(norms[0].xn_ok, norms[0].n)
            acc_to_dram(sp, xn_d[0], norms[0].out)
            sp.wait_ge(norms[0].out, norms[0].written)
            sp.wait_ge(x_zero, 16 * x_zeros)
            front_sp(sp, fronts["fa"], xn_d[0])
            sp.wait_ge(Front.xt_tp, NT)
            front_sp(sp, fronts["fb"], xn_d[0], [(xb_ok, 1)])
            for s in (main, gat):
                total = 16 * s.per * s.turns
                for q in s.scat:
                    sp.wait_ge(q, total)
                sp.dma_start(s.rec_sb[:, :], s.rec_d.rearrange("(p c) f -> p (c f)", p=P)[:, 0:s.chunks * 4]
                             ).then_inc(s.back, 16)
            for ap, n in ((a["L0_ffn_att_src"].rearrange("h e -> (h e)"), 0),
                          (a["L0_ffn_att_dst"].rearrange("h e -> (h e)"), 16), (a["L0_ffn_b_gat"], 32),
                          (a["L0_ffn_ln_gamma"], 48), (a["L0_ffn_ln_beta"], 64)):
                sp.dma_start(attrow[:, n:n + 16], broadcast_row(ap, 16)).then_inc(rows_ffn, 16)
            sp.dma_start(wgat, a["L0_ffn_W_gat"].rearrange("(k p) n -> p k n", p=P)).then_inc(rows_ffn, 16)
            sp.dma_start(wgate, a["L1_ffn_gate_w"].rearrange("(k p) n -> p k n", p=P)).then_inc(rows_ffn, 16)
            sp.dma_start(gbrow, broadcast_row(a["L1_ffn_gate_b"], 8)).then_inc(rows_ffn, 16)
            sp.dma_start(B1T[:, 0:16], a["L0_ffn_b1"].rearrange("e (m p) -> p (e m)", p=P), allow_slow_non_contiguous=True).then_inc(rows_ffn, 16)
            sp.dma_start(B2R[0:EXP0, :], a["L0_ffn_b2"]).then_inc(rows_ffn, 16)
            sp.wait_ge(round_pe, R["lnb"] + 1)
            sp.dma_start(moe0.w1, a["L0_ffn_W1"].rearrange("e (k p) n -> p e k n", p=P)).then_inc(w_ffn, 16)
            sp.dma_start(moe0.w2, a["L0_ffn_W2"].rearrange("e (k p) n -> p e k n", p=P)).then_inc(w_ffn, 16)
            sp.wait_ge(norms[1].xn_ok, norms[1].n)
            acc_to_dram(sp, xn_d[1], norms[1].out)
            sp.wait_ge(src_ready, 1)
            sp.dma_start(src_tab_d.rearrange("(t p) c -> p t c", p=P), v3(STB, 32)).then_inc(src_out, 16)
            sp.wait_ge(dst_ready, 1)
            sp.dma_start(dst_tab_d.rearrange("(t p) c -> p t c", p=P), v3(DTT, 8)).then_inc(dst_out, 16)
            sp.wait_ge(norms[1].out, norms[1].written)
            front_sp(sp, fronts["ff"], xn_d[1])
            sp.wait_ge(round_pe, R["lnc"] + 1)
            sp.dma_start(wsh, a["L1_gnn_shared_weight"].rearrange("(k p) n -> p k n", p=P)).then_inc(w_in1, 16)
            sp.dma_start(wqkv, a["L1_mix_Wqkv"].rearrange("(k p) n -> p k n", p=P)).then_inc(w_in1, 16)
            sp.dma_start(wproj, a["L1_mix_Wproj"].rearrange("(k p) n -> p k n", p=P)).then_inc(w_in1, 16)
            sp.dma_start(ROWS[:, 0:768], broadcast_row(a["L1_mix_bqkv"], 768)).then_inc(rows_in1, 16)
            sp.dma_start(bproj, broadcast_row(a["L1_mix_bproj"], C)).then_inc(rows_in1, 16)
            sp.dma_start(obias, broadcast_row(a["L1_gnn_output_bias"], C)).then_inc(rows_in1, 16)
            sp.dma_start(temp, broadcast_row(a["L1_mix_temperature"].rearrange("a h b c -> (a h b c)"), 8)
                         ).then_inc(rows_in1, 16)
            sp.wait_ge(norms[2].xn_ok, norms[2].n)
            acc_to_dram(sp, xn_d[2], norms[2].out)
            for i in range(3):
                sp.wait_ge(hop_done, i + 1)
                acc_to_dram(sp, cur_d[i], cur_out)
            sp.wait_ge(cur_out, 48)
            for i, table in enumerate([xn_d[2]] + cur_d):
                if i:
                    sp.wait_ge(Front.xt_tp, fronts[f"f{i}"].before * TI)
                front_sp(sp, fronts[f"f{i}"], table)
            for i in ("fm", "fn"):
                sp.wait_ge(Front.xt_tp, fronts[i].before * TI)
                front_sp(sp, fronts[i], xn_d[2])
            sp.wait_ge(round_pe, R["lnd"] + 1)
            sp.dma_start(w1x.rearrange("p (e k n) -> p e k n", e=EXP1, k=2),
                         a["L1_ffn_W1"].rearrange("e (k p) n -> p e k n", p=P)).then_inc(w_ffn, 16)
            sp.dma_start(w2x.rearrange("p (e k n) -> p e k n", e=EXP1, k=4),
                         a["L1_ffn_W2"].rearrange("e (k p) n -> p e k n", p=P)).then_inc(w_ffn, 16)
            sp.dma_start(B1X, broadcast_row(a["L1_ffn_b1"].rearrange("e n -> (e n)"), EXP1 * HID)).then_inc(w_ffn, 16)
            sp.dma_start(B2X, broadcast_row(a["L1_ffn_b2"].rearrange("e n -> (e n)"), EXP1 * C)).then_inc(w_ffn, 16)
            loads_sp(sp)
            sp.wait_ge(x_done, 1)
            sp.dma_start(out[0:full, :].rearrange("(t p) c -> p t c", p=P), v3(X[:, 0:(NT - 1) * C], C)
                         ).then_inc(out_done, 16)
            sp.dma_start(out[full:N, :], X[0:LAST, (NT - 1) * C:NT * C]).then_inc(out_done, 16)
            sp.wait_ge(out_done, 32)

        @block.gpsimd
        def _(e):
            e.memset(ones[:, :], 1.0)
            e.memset(eps_ln[:, :], LN_EPS)
            e.memset(valid[:, :], 1.0)
            e.memset(zeros, 0)
            e.memset(X[:, (NT - 1) * C:NT * C], 0.0)
            e.memset(s_src, 0)
            e.memset(s_dst, NP)
            e.memset(s_w, 0.0)
            e.iota(iota_row[:, :], [[1, P]], base=0, channel_multiplier=0, allow_small_or_imprecise_dtypes=True)
            e.iota(s_iota, [[1, CH_MAIN]], base=0, channel_multiplier=0, allow_small_or_imprecise_dtypes=True)
            e.drain()
            e.affine_select(out=ident[:, :], in_=ones[:, :], compare_op=ALU.is_equal, fill=0.0, base=0,
                            pattern=[[1, P]], channel_multiplier=-1)
            e.affine_select(out=upper[:, :], in_=ones[:, :], compare_op=ALU.is_gt, fill=0.0, base=0,
                            pattern=[[1, P]], channel_multiplier=-1)
            e.affine_select(out=v3(head_mask[:, :], 32), in_=v3(ones[:, :], 32), compare_op=ALU.is_ge, fill=0.0,
                            base=0, pattern=[[-32, 4], [0, 32]], channel_multiplier=1)
            e.affine_select(out=valid[:, NT - 1:NT], in_=ones[:, 0:1], compare_op=ALU.is_gt, fill=0.0, base=LAST,
                            pattern=[[0, 1]], channel_multiplier=-1)
            e.drain()
            e.affine_select(out=v3(head_mask[:, :], 32), in_=v3(head_mask[:, :], 32), compare_op=ALU.is_ge, fill=0.0,
                            base=31, pattern=[[32, 4], [0, 32]], channel_multiplier=-1)
            for b in range(4):
                e.tensor_scalar(ident_b[:, b * P:(b + 1) * P], ident[:, :], -BIG, None, ALU.mult)
            e.drain().then_inc(consts_ok, 1)
            e.sem_inc(Hop.mm, GROUP)
            e.sem_inc(Hop.add, HB)
            e.sem_inc(gat_mm, GROUP)
            e.sem_inc(gat_add, HB)
            e.sem_inc(gat_at, 1)
            e.sem_inc(gat_tp, 1)
            e.sem_inc(gat_e, 2)
            e.sem_inc(fx_hb, UC)
            e.sem_inc(fx_y, UC)
            e.sem_inc(ys_free, 1)
            sort_pool(e, main)
            sort_pool(e, gat)
            for i in (0,):
                pool_wait(e, hop_init, 1)
                hop_pool(e, hops[0])
            e.sem_inc(gat_kept, 2)
            pool_wait(e, src_out, 16)
            pool_wait(e, dve_ready, 1)
            gat_pool(e, False)
            pool_wait(e, dst_out, 16)
            gat_pool(e, True)
            for i in range(3):
                if i == 0:
                    pool_wait(e, hop_init, 2)
                    pool_wait(e, norms[2].out, norms[2].written)
                else:
                    pool_wait(e, cur_out, 16 * i)
                hop_pool(e, hops[i + 1])
            m1A_pool(e)
            scatter_pool(e)
            ffn1_pool(e)
            gather_pool(e)

        @block.tensor
        def _(pe):
            sort_pe(pe, main)
            sort_pe(pe, gat)
            pe.wait_ge(w_in0, 16 * 11)
            with pe.Fori(0, TURNS) as s:
                mixA_pe(pe, s)
                rendezvous(pe, "pe", s + (R["mixA"] + 1))
            rendezvous(pe, "pe", R["mixA_end"] + 1)
            with pe.Fori(0, TURNS) as s:
                mixB_pe(pe, s)
                rendezvous(pe, "pe", s + (R["mixB"] + 1))
            hop_pe(pe, hops[0])
            rendezvous(pe, "pe", R["hop0"] + 1)
            with pe.Fori(0, TURNS) as s:
                gnn0_pe(pe, s)
                rendezvous(pe, "pe", s + (R["gnn0"] + 1))
            rendezvous(pe, "pe", R["lnb"] + 1)
            pe.wait_ge(rows_ffn, 160)
            with pe.Fori(0, TURNS) as s:
                narrow_pe(pe, fronts["fp"], s, wgat, 16, gp_mm)
                rendezvous(pe, "pe", s + (R["gatp"] + 1))
            rendezvous(pe, "pe", R["gatp_end"] + 1)
            gatA_pe(pe)
            rendezvous(pe, "pe", R["gatA"] + 1)
            gatB_pe(pe)
            rendezvous(pe, "pe", R["gatB"] + 1)
            pe.wait_ge(w_ffn, 32)
            with pe.Fori(0, TURNS) as s:
                moe_pe(pe, moe0, s)
                rendezvous(pe, "pe", s + (R["ffn0"] + 1))
            rendezvous(pe, "pe", R["lnc"] + 1)
            for i in range(3):
                hop_pe(pe, hops[i + 1])
                rendezvous(pe, "pe", R[f"hop{i + 1}"] + 1)
            pe.wait_ge(w_in1, 48)
            for i in range(4):
                with pe.Fori(0, TURNS) as s:
                    gnn1_pe(pe, i, s)
                    rendezvous(pe, "pe", s + (R["gnn1"] + i * TURNS + 1))
            weights_pe(pe)
            rendezvous(pe, "pe", R["m1w"] + 1)
            with pe.Fori(0, TURNS) as s:
                m1A_pe(pe, s)
                rendezvous(pe, "pe", s + (R["m1A"] + 1))
            m1A_end_pe(pe)
            rendezvous(pe, "pe", R["m1A_end"] + 1)
            with pe.Fori(0, TURNS) as s:
                m1B_pe(pe, s)
                rendezvous(pe, "pe", s + (R["m1B"] + 1))
            rendezvous(pe, "pe", R["lnd"] + 1)
            with pe.Fori(0, TURNS) as s:
                narrow_pe(pe, fronts["fq"], s, wgate, 8, gl_mm)
                rendezvous(pe, "pe", s + (R["gate1"] + 1))
            places_pe(pe)
            rendezvous(pe, "pe", R["gate1_end"] + 1)
            pe.wait_ge(w_ffn, 96)
            ffn1_pe(pe)
            rendezvous(pe, "pe", R["ffn1"] + 1)
            rendezvous(pe, "pe", R["ffn1_end"] + 1)

        @block.scalar
        def _(e):
            e.wait_ge(consts_ok, 1)
            norm_act(e, norms[0])
            with e.Fori(0, TURNS) as s:
                mixA_act(e, s)
                rendezvous(e, "act", s + (R["mixA"] + 1))
            rendezvous(e, "act", R["mixA_end"] + 1)
            with e.Fori(0, TURNS) as s:
                mixB_act(e, s)
                rendezvous(e, "act", s + (R["mixB"] + 1))
            hop_act(e, hops[0])
            e.wait_ge(deg_ok, 1)
            e.activation(sd[:, :], DEG, ACT.Sqrt).then_inc(dsd_ok, 1)
            rendezvous(e, "act", R["hop0"] + 1)
            with e.Fori(0, TURNS) as s:
                front_act(e, fronts["fg"], s)
                rendezvous(e, "act", s + (R["gnn0"] + 1))
            rendezvous(e, "act", R["lnb"] + 1)
            norm_act(e, norms[1])
            with e.Fori(0, TURNS) as s:
                front_act(e, fronts["fp"], s)
                rendezvous(e, "act", s + (R["gatp"] + 1))
            rendezvous(e, "act", R["gatp_end"] + 1)
            gatA_act(e)
            rendezvous(e, "act", R["gatA"] + 1)
            e.wait_ge(sc_e, 1)
            e.activation(ES, ES, ACT.Exp).then_inc(sc_ex, 1)
            gatB_act(e)
            rendezvous(e, "act", R["gatB"] + 1)
            e.wait_ge(sc_var, 1)
            e.activation(rs[:, :], sd[:, :], ACT.Sqrt).then_inc(sc_sd, 1)
            e.wait_ge(sc_e, 2)
            e.activation(gates[:, 0:NT * EXP0], gates[:, 0:NT * EXP0], ACT.Exp).then_inc(sc_ex, 1)
            e.wait_ge(rows_ffn, 160)
            with e.Fori(0, TURNS) as s:
                moe_act(e, moe0, s)
                rendezvous(e, "act", s + (R["ffn0"] + 1))
            rendezvous(e, "act", R["lnc"] + 1)
            norm_act(e, norms[2])
            for i in range(3):
                hop_act(e, hops[i + 1])
                rendezvous(e, "act", R[f"hop{i + 1}"] + 1)
            for i in range(4):
                with e.Fori(0, TURNS) as s:
                    front_act(e, fronts[f"f{i}"], s)
                    rendezvous(e, "act", s + (R["gnn1"] + i * TURNS + 1))
            weights_act(e)
            rendezvous(e, "act", R["m1w"] + 1)
            with e.Fori(0, TURNS) as s:
                m1_act(e, fronts["fm"], s, 0)
                rendezvous(e, "act", s + (R["m1A"] + 1))
            rendezvous(e, "act", R["m1A_end"] + 1)
            with e.Fori(0, TURNS) as s:
                m1B_act(e, s)
                rendezvous(e, "act", s + (R["m1B"] + 1))
            rendezvous(e, "act", R["lnd"] + 1)
            norm_act(e, norms[3])
            with e.Fori(0, TURNS) as s:
                front_act(e, fronts["fq"], s)
                rendezvous(e, "act", s + (R["gate1"] + 1))
            e.wait_ge(gl_e, 1)
            e.activation(LG, LG, ACT.Exp).then_inc(gl_ex, 1)
            rendezvous(e, "act", R["gate1_end"] + 1)
            ffn1_act(e)
            rendezvous(e, "act", R["ffn1"] + 1)
            rendezvous(e, "act", R["ffn1_end"] + 1)

        @block.vector
        def _(e):
            e.wait_ge(consts_ok, 1)
            sort_dve(e, main, n_main, True)
            e.drain().then_inc(sort_free, 1)
            e.wait_ge(x_in, 32)
            norm_dve(e, norms[0])
            sort_dve(e, gat, n_gat, False)
            e.memset(KVA, 0.0)
            e.drain()
            with e.Fori(0, TURNS) as s:
                mixA_dve(e, s)
                rendezvous(e, "dve", s + (R["mixA"] + 1))
            for h in range(2):
                e.tensor_tensor(KVB[:, h * P:(h + 1) * P], KVA[:, h * 129:h * 129 + P], head_mask[:, :], ALU.mult)
                e.tensor_scalar(ZB[:, h * P:(h + 1) * P], head_mask[:, :], KVA[:, h * 129 + P:h * 129 + P + 1], None,
                                ALU.mult)
            rendezvous(e, "dve", R["mixA_end"] + 1)
            with e.Fori(0, TURNS) as s:
                mixB_dve(e, s)
                rendezvous(e, "dve", s + (R["mixB"] + 1))
            e.memset(v3(ACC[:, :], 257)[:, :, C:C + 1], 0.0)
            e.memset(v3(G, 257)[:, :, C:C + 1], 1.0)
            e.wait_ge(main.back, 16)
            e.drain().then_inc(hop_init, 1)
            hop_dve(e, hops[0])
            e.tensor_scalar(DEG, v3(ACC[:, :], 257)[:, :, C], 1.0, None, ALU.max)
            e.drain().then_inc(deg_ok, 1)
            e.wait_ge(dsd_ok, 1)
            e.reciprocal(DEG, sd[:, :])
            rendezvous(e, "dve", R["hop0"] + 1)
            with e.Fori(0, TURNS) as s:
                gnn0_dve(e, s)
                rendezvous(e, "dve", s + (R["gnn0"] + 1))
            rendezvous(e, "dve", R["lnb"] + 1)
            norm_dve(e, norms[1])
            e.wait_ge(rows_ffn, 160)
            with e.Fori(0, TURNS) as s:
                narrow_dve(e, s, SRT, 20, 16, gp_mm)
                rendezvous(e, "dve", s + (R["gatp"] + 1))
            gat_tables_dve(e)
            e.drain().then_inc(dve_ready, 1)
            rendezvous(e, "dve", R["gatp_end"] + 1)
            gatA_dve(e)
            rendezvous(e, "dve", R["gatA"] + 1)
            gat_max_dve(e)
            gatB_dve(e)
            rendezvous(e, "dve", R["gatB"] + 1)
            gat_scores_dve(e)
            with e.Fori(0, TURNS) as s:
                moe_dve(e, moe0, s)
                rendezvous(e, "dve", s + (R["ffn0"] + 1))
            rendezvous(e, "dve", R["lnc"] + 1)
            e.sem_inc(hop_init, 1)
            norm_dve(e, norms[2])
            x3 = v3(X[:, :], C)
            e.wait_ge(rows_in1, 64)
            e.tensor_scalar(TS, temp, SCALE1, None, ALU.mult)
            e.wait_ge(norms[2].out, norms[2].written)
            for i in range(3):
                if i:
                    e.wait_ge(cur_out, 16 * i)
                e.memset(ACC[:, :], 0.0)
                if i == 0:
                    e.memset(v3(G, 257)[:, :, C:C + 1], 1.0)
                    e.drain()
                    e.tensor_tensor(x3, x3, over_tiles(bproj, C), ALU.add)
                    e.drain()
                    e.tensor_tensor(x3, x3, over_tiles(obias, C), ALU.add)
                e.drain()
                hop_dve(e, hops[i + 1])
                e.drain().then_inc(hop_done, 1)
                rendezvous(e, "dve", R[f"hop{i + 1}"] + 1)
            for i in range(4):
                with e.Fori(0, TURNS) as s:
                    add_banks(e, s, g1_mm, i * NT)
                    rendezvous(e, "dve", s + (R["gnn1"] + i * TURNS + 1))
            A = 0.5
            vals = [A] + [2 * A] * 15 + [A, SCALE1 ** 2, SCALE1 ** 4]
            for g, val in enumerate(vals):
                e.memset(coef[32 * (g % 4):32 * (g % 4) + 32, g // 4:g // 4 + 1], val / N)
            e.memset(MFT, 0.0)
            f3 = F0.rearrange("p (h g i) -> p h g i", h=8, i=32)
            e.memset(f3[:, :, FG - 1, :], 0.0)
            e.drain()
            e.memset(f3[:, :, FG - 1, 0:1], 1.0)
            rendezvous(e, "dve", R["m1w"] + 1)
            with e.Fori(0, TURNS) as s:
                m1A_dve(e, s)
                rendezvous(e, "dve", s + (R["m1A"] + 1))
            e.wait_ge(m_tp, 2)
            for c in range(FC):
                rows = min(P, FG * 32 - c * P)
                e.tensor_scalar(MF[0:rows, c * 8 * HV:(c + 1) * 8 * HV], bank(c, 8 * HV, 0, rows),
                                coef[0:rows, c:c + 1], None, ALU.mult)
            rendezvous(e, "dve", R["m1A_end"] + 1)
            with e.Fori(0, TURNS) as s:
                m1B_dve(e, s)
                rendezvous(e, "dve", s + (R["m1B"] + 1))
            rendezvous(e, "dve", R["lnd"] + 1)
            norm_dve(e, norms[3])
            with e.Fori(0, TURNS) as s:
                narrow_dve(e, s, LG, 8, 8, gl_mm)
                rendezvous(e, "dve", s + (R["gate1"] + 1))
            gates1_dve(e)
            e.drain()
            places_dve(e)
            rendezvous(e, "dve", R["gate1_end"] + 1)
            ffn1_dve(e)
            rendezvous(e, "dve", R["ffn1"] + 1)
            e.sem_inc(yg_used, TI)
            with e.Fori(0, TURNS) as s:
                combine_dve(e, s)
            rendezvous(e, "dve", R["ffn1_end"] + 1)
            e.drain().then_inc(x_done, 1)


_INS = ['x', 'src', 'dst', 'edge_weight', 'L0_gnn_weight', 'L0_mix_Wq', 'L0_mix_Wk', 'L0_mix_Wv', 'L0_mix_Wm',
        'L0_mix_W1', 'L0_mix_W2', 'L0_mix_g1', 'L0_mix_b1', 'L0_mix_g2', 'L0_mix_b2', 'L0_ffn_W_gat',
        'L0_ffn_att_src', 'L0_ffn_att_dst', 'L0_ffn_b_gat', 'L0_ffn_ln_gamma', 'L0_ffn_ln_beta', 'L0_ffn_W1',
        'L0_ffn_b1', 'L0_ffn_W2', 'L0_ffn_b2', 'L0_ffn_edge_index', 'L1_gnn_shared_weight', 'L1_gnn_output_bias',
        'L1_mix_Wqkv', 'L1_mix_bqkv', 'L1_mix_Wproj', 'L1_mix_bproj', 'L1_mix_temperature', 'L1_ffn_gate_w',
        'L1_ffn_gate_b', 'L1_ffn_W1', 'L1_ffn_b1', 'L1_ffn_W2', 'L1_ffn_b2']


def kernel(**inputs):
    import numpy as np
    import concourse.bacc as bacc
    from concourse.bass_utils import run_bass_kernel_spmd

    nc = bacc.Bacc("TRN2", target_bir_lowering=False, num_devices=1)
    arrays, args = {}, {}
    for name in _INS:
        arr = np.ascontiguousarray(inputs[name])
        arrays[f"in_{name}"] = arr
        args[name] = nc.dram_tensor(f"in_{name}", arr.shape, mybir.dt.from_np(arr.dtype), kind="ExternalInput").ap()
    out = nc.dram_tensor("out_0", (N, C), F32, kind="ExternalOutput").ap()
    gps_kernel(nc, args, out)
    r = run_bass_kernel_spmd(nc, [arrays], core_ids=[0])
    return r.results[0]["out_0"]
```

```python
from contextlib import ExitStack

import concourse.bass as bass
from concourse import mybir
from concourse.alu_op_type import AluOpType as ALU

ACT = mybir.ActivationFunctionType
AX = mybir.AxisListType
F32 = mybir.dt.float32
BF16 = mybir.dt.bfloat16
I32 = mybir.dt.int32

P = 128
N = 3125
C = 256
NT = -(-N // P)
NP = NT * P
TI = 5
TURNS = NT // TI
W = TI * P
HALF = W // 2
LAST = N - (NT - 1) * P
LN_EPS = 1e-5
BUCKETS = NT + 1

E_MAIN = 50000
E_GAT = 32768
GROUP = 16


def chunk_bound(edges):
    return -(-(-(-(edges + NT * (P - 1)) // P)) // GROUP) * GROUP


CH_MAIN = chunk_bound(E_MAIN)
CH_GAT = chunk_bound(E_GAT)
BIG = 1e30
LANE = 1


def gps_kernel(nc, a, out):
    EXP0, EXP1 = 4, 8
    HID = 512
    GH = 4
    GE = 4
    R2 = 17
    FG = R2 + 2
    FC = -(-FG * 32 // P)
    SCALE1 = float(32) ** 0.25

    ctx = ExitStack()
    with ctx:
        def sb(name, shape, dt=F32):
            return ctx.enter_context(nc.sbuf_tensor(name, shape, dt))

        def sem(name):
            return ctx.enter_context(nc.semaphore(name))

        def dram(name, shape, dt=F32):
            return nc.dram_tensor(name, shape, dt, kind="Internal").ap()

        xn_d = [dram(f"xn_d{i}", [NP, C]) for i in range(3)]
        cur_d = [dram(f"cur_d{i}", [NP, C]) for i in range(3)]
        src_tab_d = dram("src_tab_d", [NP, 32])
        dst_tab_d = dram("dst_tab_d", [NP, 8])
        PADROWS = 8
        rec_main_d = dram("rec_main_d", [P * (CH_MAIN + PADROWS), 4], I32)
        rec_gat_d = dram("rec_gat_d", [P * (CH_GAT + PADROWS), 4], I32)

        X = sb("X", [P, NT * C])
        ACC = sb("ACC", [P, NT * 257])
        rec_main = sb("rec_main", [P, CH_MAIN * 4], I32)
        rec_gat = sb("rec_gat", [P, CH_GAT * 4], I32)
        ident = sb("ident", [P, P])
        ident_b = sb("ident_b", [P, 4 * P], BF16)
        iota_row = sb("iota_row", [P, P])
        upper = sb("upper", [P, P])
        ones = sb("ones", [P, P])
        head_mask = sb("head_mask", [P, P])
        valid = sb("valid", [P, NT])
        eps_ln = sb("eps_ln", [P, 1])
        WT = sb("WT", [P, 16384])
        WS = sb("WS", [P, 2048])
        ROWS = sb("ROWS", [P, 2560])
        XS = sb("XS", [P, TI * C])
        XT = sb("XT", [P, 2 * W])
        BUF = sb("BUF", [P, 11520])
        bn = sb("bn", [P, NT * 6])
        mv = sb("mv", [P, NT * 2])
        sd = sb("sd", [P, NT])
        rs = sb("rs", [P, NT])
        gates = sb("gates", [P, NT * 8])
        tile_main = sb("tile_main", [1, CH_MAIN], I32)
        tile_gat = sb("tile_gat", [1, CH_GAT], I32)
        ib = [sb("ibA", [P, GROUP // 2], I32), sb("ibB", [P, GROUP // 2], I32)]
        ps = ctx.enter_context(nc.psum_tensor("ps", [P, 8 * 512], F32))

        def bank(b, n=512, off=0, rows=P):
            return ps[0:rows, b * 512 + off:b * 512 + off + n]

        def v3(ap, b):
            return ap.rearrange("p (a b) -> p a b", b=b)

        XS3 = v3(XS[:, :], C)
        XT3 = v3(XT[:, :], W)

        consts_ok = sem("consts_ok")
        x_in = sem("x_in")
        carried = sem("carried")
        round_pe, round_act, round_dve = sem("round_pe"), sem("round_act"), sem("round_dve")
        rounds = {"pe": round_pe, "act": round_act, "dve": round_dve}

        def rendezvous(e, who, n):
            e.drain().then_inc(rounds[who], 1)
            for other, s in rounds.items():
                if other != who:
                    e.wait_ge(s, n)

        def pool_wait(e, q, value):
            e.wait_ge(q, value)
            e.sem_inc(carried, 1)

        def tiles_of(table, k):
            return nc.values_load_multi_w_load_instructions(
                table[0:1, bass.ds(k * GROUP, GROUP)], [mybir.EngineType.DVE], min_val=0, max_val=NT - 1,
                skip_runtime_bounds_check_because="the sort writes counts of buckets, 0 to NT - 1")[1]

        R = {}
        count = 0
        for name, n in (("mixA", TURNS), ("mixA_end", 1), ("mixB", TURNS), ("hop0", 1), ("gnn0", TURNS),
                        ("lnb", 1), ("gatp", TURNS), ("gatp_end", 1), ("gatA", 1), ("gatB", 1), ("ffn0", TURNS),
                        ("lnc", 1), ("m1w", 1), ("hop1", 1), ("hop2", 1), ("hop3", 1), ("gnn1", TURNS),
                        ("m1A", 1), ("m1B", 1), ("lnd", 1), ("gate1", TURNS), ("gate1_end", 1),
                        ("ffn1", 1), ("ffn1_end", 1)):
            R[name] = count
            count += n

        class Sort:
            loaded = sem("edges_loaded")
            count_ok = sem("count_ok")
            sums_ok = sem("sums_ok")

            def __init__(s, number, name, edges, cols, per, turns, chunks, rec_sb, rec_d, tiles, at):
                s.n = number + 1
                s.name, s.edges, s.cols, s.per, s.turns, s.chunks = name, edges, cols, per, turns, chunks
                assert cols == 2 * per * turns and P * cols >= edges
                s.rec_sb, s.rec_d, s.tiles = rec_sb, rec_d, tiles
                s.rec = WT[:, at:at + cols * 4].bitcast(I32)
                s.pos = WT[:, at + cols * 4:at + cols * 5].bitcast(I32)
                s.ids = [sb(f"{name}_ids{i}", [P, per], I32) for i in range(2)]
                s.rows = [sb(f"{name}_rows{i}", [P, per * 4], I32) for i in range(2)]
                s.cleared = sem(name + "_cleared")
                s.pos_ok = sem(name + "_pos_ok")
                s.slot = sem(name + "_slot")
                s.scat = [sem(f"{name}_scat{i}") for i in range(2)]
                s.back = sem(name + "_back")

        main = Sort(0, "main", E_MAIN, 392, 14, 14, CH_MAIN, rec_main, rec_main_d, tile_main, 10240)
        gat = Sort(1, "gat", E_GAT, 256, 16, 8, CH_GAT, rec_gat, rec_gat_d, tile_gat, 12288)
        GAT_EARLY = 6
        SCOLS = 392
        s_dst = BUF[:, 0:SCOLS].bitcast(I32)
        s_tile = BUF[:, 400:400 + SCOLS].bitcast(I32)
        s_tilef = BUF[:, 800:800 + SCOLS]
        s_mask = BUF[:, 1200:1200 + SCOLS]
        s_scan = BUF[:, 1600:1600 + SCOLS]
        s_rank = BUF[:, 2000:2000 + SCOLS]
        s_tmp = BUF[:, 2400:2400 + SCOLS]
        s_src = BUF[:, 2800:2800 + SCOLS].bitcast(I32)
        s_w = BUF[:, 3200:3200 + SCOLS]
        s_tmpi = BUF[:, 3600:3600 + SCOLS].bitcast(I32)
        s_cnt = BUF[:, 4000:4000 + BUCKETS]
        s_base = BUF[:, 4032:4032 + BUCKETS]
        s_chk = BUF[:, 4064:4064 + BUCKETS]
        s_chki = BUF[:, 4096:4096 + BUCKETS].bitcast(I32)
        s_scan2 = BUF[:, 6900:6900 + SCOLS]
        s_mask2 = BUF[:, 7300:7300 + SCOLS]
        s_end = BUF[:, 4128:4128 + BUCKETS]
        s_iota = BUF[:, 4160:4160 + CH_MAIN]
        s_tidx = BUF[:, 4600:4600 + CH_MAIN]
        zeros = BUF[:, 5200:5200 + (CH_MAIN + PADROWS) * 4].bitcast(I32)
        sort_free = sem("sort_free")

        def sort_loads(sp, s, src, dst, w):
            full = s.edges // s.cols
            rest = s.edges - full * s.cols
            todo = [(s_src, src), (s_dst, dst)] + ([(s_w, w)] if w is not None else [])
            n = 0
            for tile, ap in todo:
                sp.dma_start(tile[0:full, 0:s.cols], ap[0:full * s.cols].rearrange("(p c) -> p c", c=s.cols)
                             ).then_inc(s.loaded, 16)
                n += 16
                if rest:
                    sp.dma_start(tile[full:full + 1, 0:rest], ap[full * s.cols:s.edges].rearrange("(p c) -> p c", p=1)
                                 ).then_inc(s.loaded, 16)
                    n += 16
            return n

        n_main = 96
        n_gat = n_main + 32

        def sort_dve(e, s, n_loaded, weighted):
            cols = s.cols
            dst, tile_i, tilef = s_dst[:, 0:cols], s_tile[:, 0:cols], s_tilef[:, 0:cols]
            mask, scan, rank, tmp = s_mask[:, 0:cols], s_scan[:, 0:cols], s_rank[:, 0:cols], s_tmp[:, 0:cols]
            tmpi = s_tmpi[:, 0:cols]
            e.wait_ge(s.loaded, n_loaded)
            e.tensor_scalar(tile_i, dst, 7, None, ALU.arith_shift_right)
            e.memset(rank, 0.0)
            e.drain()
            e.tensor_copy(tilef, tile_i)
            e.drain()
            for t in range(BUCKETS):
                e.tensor_scalar((mask, tmp)[t % 2], tilef, float(t), 0.0, ALU.is_equal, ALU.add, s_cnt[:, t:t + 1])
                if t % 2:
                    e.drain()
            e.drain().then_inc(s.count_ok, 1)
            e.wait_ge(s.sums_ok, s.n)
            e.tensor_scalar(s_chk, bank(7, BUCKETS, 64), float(P - 1), None, ALU.add)
            e.tensor_copy(s_base, bank(7, BUCKETS, 0))
            e.drain()
            e.tensor_copy(s_chki, s_chk)
            e.drain()
            e.tensor_scalar(s_chki, s_chki, 7, None, ALU.arith_shift_right)
            e.drain()
            e.tensor_copy(s_chk, s_chki)
            e.drain()
            e.tensor_tensor_scan(s_end, s_chk, s_chk, 0.0, ALU.add, ALU.max)
            e.drain()
            e.tensor_tensor(s_chk, s_end, s_chk, ALU.subtract)
            e.drain()
            e.tensor_scalar(s_chk, s_chk, float(P), None, ALU.mult)
            e.drain()
            e.tensor_tensor(s_base, s_base, s_chk, ALU.add)
            e.drain()
            scans, masks, sums = (scan, s_scan2[:, 0:cols]), (mask, s_mask2[:, 0:cols]), (rank, tmp)
            e.memset(tmp, 0.0)
            for t in range(0, BUCKETS, 2):
                for i in range(2):
                    e.tensor_scalar(masks[i], tilef, float(t + i), None, ALU.is_equal)
                e.drain()
                for i in range(2):
                    e.tensor_tensor_scan(scans[i], masks[i], masks[i], s_base[:, t + i:t + i + 1], ALU.add, ALU.max)
                e.drain()
                for i in range(2):
                    e.tensor_tensor(scans[i], masks[i], scans[i], ALU.mult)
                e.drain()
                for i in range(2):
                    e.tensor_tensor(sums[i], sums[i], scans[i], ALU.add)
            e.drain()
            e.scalar_tensor_tensor(rank, rank, -1.0, tmp, ALU.add, ALU.add)
            e.drain()
            e.tensor_copy(tmpi, rank)
            e.drain()
            e.tensor_scalar(tile_i, tmpi, 7, None, ALU.arith_shift_right)
            e.tensor_scalar(tmpi, tmpi, 127, None, ALU.bitwise_and)
            e.drain()
            e.tensor_copy(tmp, tile_i)
            e.tensor_copy(scan, tmpi)
            e.drain()
            e.scalar_tensor_tensor(tmp, scan, float(s.chunks + PADROWS), tmp, ALU.mult, ALU.add)
            e.drain()
            e.tensor_copy(s.pos[:, :], tmp)
            rec = v3(s.rec[:, :], 4)
            recf = v3(s.rec[:, :].bitcast(F32), 4)
            e.tensor_copy(rec[:, :, 0], s_src[:, 0:cols])
            e.tensor_scalar(tile_i, dst, 127, None, ALU.bitwise_and)
            e.drain()
            e.tensor_scalar(mask, tilef, float(NT), None, ALU.is_lt)
            e.tensor_copy(recf[:, :, LANE], tile_i)
            if weighted:
                e.tensor_copy(recf[:, :, 2], s_w[:, 0:cols])
            else:
                e.tensor_copy(rec[:, :, 2], dst)
            e.drain()
            e.tensor_copy(recf[:, :, 3], mask)
            e.drain().then_inc(s.pos_ok, 1)
            e.memset(s_tidx[0:1, 0:s.chunks], 0.0)
            e.drain()
            for t in range(NT):
                e.scalar_tensor_tensor(s_tidx[0:1, 0:s.chunks], s_iota[0:1, 0:s.chunks], s_end[0:1, t:t + 1],
                                       s_tidx[0:1, 0:s.chunks], ALU.is_ge, ALU.add)
                e.drain()
            e.tensor_scalar(s_tidx[0:1, 0:s.chunks], s_tidx[0:1, 0:s.chunks], float(NT - 1), None, ALU.min)
            e.drain()
            e.tensor_copy(s.tiles[0:1, :], s_tidx[0:1, 0:s.chunks])
            e.drain()

        def sorted_back(sp, s):
            for q in s.scat:
                sp.wait_ge(q, 16 * s.per * s.turns)
            sp.dma_start(s.rec_sb[:, :], s.rec_d.rearrange("(p c) f -> p (c f)", p=P)[:, 0:s.chunks * 4]
                         ).then_inc(s.back, 16)

        def sort_pe(pe, s):
            pe.wait_ge(s.count_ok, s.n)
            pe.matmul(bank(7, BUCKETS, 0), upper[:, :], s_cnt, start=True, stop=True)
            pe.matmul(bank(7, BUCKETS, 64), ones[:, :], s_cnt, start=True, stop=True).then_inc(s.sums_ok, 1)

        def sort_pool(e, s, first, last):
            if first == 0:
                pool_wait(e, s.pos_ok, 1)
                pool_wait(e, s.cleared, 16)
            else:
                for half in range(2):
                    pool_wait(e, s.scat[half], first * (16 * s.per))
            dest = s.rec_d

            def half_turn(k, half):
                col = k * (2 * s.per) + half * s.per
                e.tensor_copy(s.ids[half][:, :], s.pos[:, bass.ds(col, s.per)])
                e.tensor_copy(s.rows[half][:, :], s.rec[:, bass.ds(col * 4, s.per * 4)]).then_inc(s.slot, 1)
                pool_wait(e, s.slot, k * 2 + (half + 1))
                for j in range(s.per):
                    e.indirect_dma_start(dest, bass.IndirectOffsetOnAxis(ap=s.ids[half][:, j:j + 1], axis=0),
                                         s.rows[half][:, 4 * j:4 * j + 4], None).then_inc(s.scat[half], 16)

            half_turn(first, 0)
            with e.Fori(first, last - 1) as k:
                half_turn(k, 1)
                pool_wait(e, s.scat[0], (k + 1) * (16 * s.per))
                half_turn(k + 1, 0)
                pool_wait(e, s.scat[1], (k + 1) * (16 * s.per))
            half_turn(last - 1, 1)

        class Norm:
            var_ok, sd_ok, xn_ok, out = (sem("ln_" + x) for x in ("var_ok", "sd_ok", "xn_ok", "out"))

            def __init__(s, number):
                s.n = number + 1
                s.written = 16 * s.n

        norms = [Norm(i) for i in range(4)]

        def norm_dve(e, s):
            with e.Fori(0, TURNS) as t:
                for j in range(TI):
                    e.bn_stats(bn[:, bass.ds((t * TI + j) * 6, 6)], X[:, bass.ds((t * TI + j) * C, C)])
            e.drain()
            for t in range(NT):
                e.bn_aggr(mv[:, t * 2:t * 2 + 2], bn[:, t * 6:t * 6 + 6])
            e.drain().then_inc(s.var_ok, 1)
            e.wait_ge(s.sd_ok, s.n)
            e.reciprocal(rs[:, :], sd[:, :])
            e.drain()
            with e.Fori(0, TURNS) as t:
                for j in range(TI):
                    n = t * TI + j
                    e.tensor_scalar(ACC[:, bass.ds(n * 257, C)], X[:, bass.ds(n * C, C)], mv[:, bass.ds(n * 2, 1)],
                                    rs[:, bass.ds(n, 1)], ALU.subtract, ALU.mult)
            e.drain().then_inc(s.xn_ok, 1)

        def norm_act(e, s):
            e.wait_ge(s.var_ok, s.n)
            e.activation(sd[:, :], v3(mv[:, :], 2)[:, :, 1], ACT.Sqrt, bias=eps_ln[:, 0:1]).then_inc(s.sd_ok, 1)

        def acc_to_dram(sp, table, done):
            sp.dma_start(table.rearrange("(t p) c -> p t c", p=P), v3(ACC[:, :], 257)[:, :, 0:C]).then_inc(done, 16)

        class Front:
            xs_in, xt_tp, xt_out = sem("xs_in"), sem("xt_tp"), sem("xt_out")
            turns_before = loads = rows = 0

            def __init__(s, loads=TURNS):
                s.before, s.loads_before, s.rows_before = Front.turns_before, Front.loads, Front.rows
                Front.turns_before += TURNS
                Front.loads += loads
                Front.rows += 0 if loads else TURNS

            def tiles(s, turn, n):
                return turn * TI + (s.before * TI + n)

            def loaded(s, turn):
                return turn * 16 + (s.loads_before * 16 + 16)

        def rows_of(table, s):
            return table[bass.ds(s * W, W), :].rearrange("(j p) c -> p j c", p=P)

        def front_sp(sp, f, table, more=()):
            sp.dma_start(XS3, table[0:W, :].rearrange("(j p) c -> p j c", p=P)).then_inc(f.xs_in, 16)
            with sp.Fori(1, TURNS) as s:
                sp.wait_ge(f.xt_tp, f.tiles(s, 0))
                for q, per in more:
                    sp.wait_ge(q, s * per)
                sp.dma_start(XS3, rows_of(table, s)).then_inc(f.xs_in, 16)

        def front_pe(pe, f, s):
            for j in range(TI):
                if j == 0:
                    pe.wait_ge(f.xs_in, f.loaded(s))
                if j >= 2:
                    pe.wait_ge(f.xt_out, f.tiles(s, j - 1))
                for c in range(2):
                    mm = pe.transpose(bank(j % 2, P, c * P), XS3[:, j, c * P:(c + 1) * P], ident[:, :])
                mm.then_inc(f.xt_tp, 1)

        def front_act(e, f, s):
            for j in range(TI):
                e.wait_ge(f.xt_tp, f.tiles(s, j + 1))
                e.activation(XT3[:, :, j * P:(j + 1) * P], v3(bank(j % 2, 2 * P), P), ACT.Copy).then_inc(f.xt_out, 1)

        fronts = {n: Front({"fg": 0, "fp": 0, "fq": 0, "ff": NT, "f0": NT, "f1": NT, "f2": NT}.get(n, TURNS)) for n in ("fa", "fb", "fg", "fp", "ff", "f0", "f1", "f2", "f3", "fq")}

        wk_wv = v3(WT[:, 0:1024], 512)
        wq0 = v3(WT[:, 1024:1536], 256)
        wm0 = v3(WT[:, 1536:2048], 256)
        w1m = v3(WT[:, 2048:4096], 512)
        w2m = v3(WT[:, 4096:5120], 256)
        wg0 = v3(WT[:, 5120:5632], 256)
        g1r, b1r, g2r, b2r = (ROWS[:, i * C:(i + 1) * C] for i in range(4))
        w_in0 = sem("w_in0")

        MN = BUF[:, 0:TI * C]
        EX = BUF[:, 1280:1280 + TI * C]
        KS = BUF[:, 2560:2560 + TI * C]
        VS = BUF[:, 3840:3840 + TI * 258]
        KR = BUF[:, 5200:5200 + TI * C]
        KVA = WS[:, 0:258]
        KVB = WS[:, 260:516]
        ZB = WS[:, 516:772]
        VALS = WS[:, 780:785]
        kv_mm, kv_mn, kv_ex, ks_ok, vs_ok, kva_mm = (sem("kv_" + x) for x in ("mm", "mn", "ex", "ks", "vs", "acc"))
        vals_ok = sem("vals_ok")

        def mixA_pe(pe, s):
            f = fronts["fa"]
            front_pe(pe, f, s)
            for j in range(TI):
                pe.wait_ge(f.xt_out, f.tiles(s, j + 1))
                if j >= 3:
                    pe.wait_ge(vs_ok, s * TI + (j - 2))
                for c in range(2):
                    mm = pe.matmul(bank(2 + j % 3), XT3[:, c, j * P:(j + 1) * P], wk_wv[:, c, :],
                                   start=(c == 0), stop=(c == 1))
                mm.then_inc(kv_mm, 1)
            for j in range(TI):
                pe.wait_ge(ks_ok, s * TI + (j + 1))
                pe.wait_ge(vs_ok, s * TI + (j + 1))
                for h in range(2):
                    mm = pe.matmul(bank(5 + h, 129), KS[:, j * C + h * P:j * C + (h + 1) * P],
                                   VS[:, j * 258 + h * 129:j * 258 + (h + 1) * 129],
                                   start=(j == 0), stop=(j == TI - 1))
            mm.then_inc(kva_mm, 1)

        def mixA_act(e, s):
            front_act(e, fronts["fa"], s)
            for j in range(TI):
                if j == 0:
                    e.wait_ge(vals_ok, s + 1)
                e.wait_ge(kv_mm, s * TI + (j + 1))
                e.activation(KR[:, j * C:(j + 1) * C], bank(2 + j % 3, C), ACT.Copy)
                e.activation(v3(VS[:, j * 258:(j + 1) * 258], 129)[:, :, 0:P], v3(bank(2 + j % 3, C, C), P),
                             ACT.Copy, scale=VALS[:, j:j + 1])
                e.activation(v3(VS[:, j * 258:(j + 1) * 258], 129)[:, :, P:P + 1], v3(ones[:, 0:2], 1),
                             ACT.Copy, scale=VALS[:, j:j + 1])
                e.drain().then_inc(vs_ok, 1)
            for j in range(TI):
                e.wait_ge(kv_mn, s * TI + (j + 1))
                e.activation(EX[:, j * C:(j + 1) * C], MN[:, j * C:(j + 1) * C], ACT.Exp).then_inc(kv_ex, 1)

        def mixA_dve(e, s):
            e.tensor_copy(VALS, valid[:, bass.ds(s * TI, TI)]).then_inc(vals_ok, 1)
            for j in range(TI):
                e.wait_ge(vs_ok, s * TI + (j + 1))
                e.tensor_scalar(MN[:, j * C:(j + 1) * C], KR[:, j * C:(j + 1) * C], 0.0, None, ALU.min
                                ).then_inc(kv_mn, 1)
            for i in range(TI):
                e.wait_ge(kv_ex, s * TI + (i + 1))
                e.scalar_tensor_tensor(KS[:, i * C:(i + 1) * C], KR[:, i * C:(i + 1) * C], 0.0,
                                       EX[:, i * C:(i + 1) * C], ALU.max, ALU.add).then_inc(ks_ok, 1)
            e.wait_ge(kva_mm, s + 1)
            for h in range(2):
                e.tensor_tensor(KVA[:, h * 129:(h + 1) * 129], bank(5 + h, 129), KVA[:, h * 129:(h + 1) * 129], ALU.add)

        QN = BUF[:, 0:4 * HALF]
        QE = BUF[:, 1280:1280 + 4 * HALF]
        QT = v3(BUF[:, 2560:2560 + 2 * W], W)
        RD = BUF[:, 0:4 * HALF]
        MT = v3(BUF[:, 3840:3840 + 2 * W], W)
        LM = BUF[:, 5120:5120 + TI * C]
        XM = v3(BUF[:, 6400:6400 + 2 * W], W)
        HT = BUF[:, 7680:7680 + 4 * W]
        (q_mm, q_mn, q_ex, q_ok, nd_mm, mt_ok, m_mm, m_var, m_sd, lm_ok, lm_tp, xm_ok, h_mm, ht_ok, y_mm, y_var,
         y_sd, xb_ok) = (sem("b_" + x) for x in (
             "q_mm", "q_mn", "q_ex", "q_ok", "nd_mm", "mt_ok", "m_mm", "m_var", "m_sd", "lm_ok", "lm_tp", "xm_ok",
             "h_mm", "ht_ok", "y_mm", "y_var", "y_sd", "xb_ok"))
        NUMBANK = (6, 7, 0, 1)

        def mixB_pe(pe, s):
            f = fronts["fb"]
            front_pe(pe, f, s)
            pe.wait_ge(f.xt_out, f.tiles(s, TI))
            for i in range(4):
                mc, hf = i // 2, i % 2
                for c in range(2):
                    mm = pe.matmul(bank(2 + i, HALF), wq0[:, c, mc * P:(mc + 1) * P],
                                   XT3[:, c, hf * HALF:(hf + 1) * HALF], start=(c == 0), stop=(c == 1))
                mm.then_inc(q_mm, 1)
            for i in range(4):
                mc, hf = i // 2, i % 2
                pe.wait_ge(q_ok, s * 4 + (i + 1))
                q = QT[:, mc, hf * HALF:(hf + 1) * HALF]
                pe.matmul(bank(NUMBANK[i], HALF), KVB[:, mc * P:(mc + 1) * P], q, start=True, stop=True)
                pe.matmul(bank(2 + i, HALF), ZB[:, mc * P:(mc + 1) * P], q, start=True, stop=True).then_inc(nd_mm, 1)
            pe.wait_ge(mt_ok, s + 1)
            for j in range(TI):
                for c in range(2):
                    mm = pe.matmul(bank(2 + j, C), MT[:, c, j * P:(j + 1) * P], wm0[:, c, :],
                                   start=(c == 0), stop=(c == 1))
                mm.then_inc(m_mm, 1)
            for j in range(TI):
                if j == 0:
                    pe.wait_ge(lm_ok, s + 1)
                if j >= 2:
                    pe.wait_ge(xm_ok, s * TI + (j - 1))
                for c in range(2):
                    mm = pe.transpose(bank(j % 2, P, c * P), LM[:, j * C + c * P:j * C + (c + 1) * P], ident[:, :])
                mm.then_inc(lm_tp, 1)
            pe.wait_ge(xm_ok, s * TI + TI)
            for i in range(8):
                mc, hf = i // 2, i % 2
                if i >= 6:
                    pe.wait_ge(ht_ok, s * 8 + (i - 5))
                for c in range(4):
                    src = XT3 if c < 2 else XM
                    mm = pe.matmul(bank(2 + i % 6, HALF), w1m[:, c, mc * P:(mc + 1) * P],
                                   src[:, c % 2, hf * HALF:(hf + 1) * HALF], start=(c == 0), stop=(c == 3))
                mm.then_inc(h_mm, 1)
            pe.wait_ge(ht_ok, s * 8 + 8)
            for j in range(TI):
                for c in range(4):
                    mm = pe.matmul(bank(2 + j, C), HT[:, c * W + j * P:c * W + (j + 1) * P], w2m[:, c, :],
                                   start=(c == 0), stop=(c == 3))
                mm.then_inc(y_mm, 1)

        def mixB_act(e, s):
            front_act(e, fronts["fb"], s)
            for i in range(4):
                e.wait_ge(q_mn, s * 4 + (i + 1))
                e.activation(QE[:, i * HALF:(i + 1) * HALF], QN[:, i * HALF:(i + 1) * HALF], ACT.Exp).then_inc(q_ex, 1)
            e.wait_ge(m_var, s + 1)
            e.activation(sd[:, 0:TI], v3(mv[:, 0:2 * TI], 2)[:, :, 1], ACT.Sqrt, bias=eps_ln[:, 0:1]).then_inc(m_sd, 1)
            for j in range(TI):
                e.wait_ge(lm_tp, s * TI + (j + 1))
                e.activation(XM[:, :, j * P:(j + 1) * P], v3(bank(j % 2, 2 * P), P), ACT.Copy).then_inc(xm_ok, 1)
            for i in range(8):
                mc, hf = i // 2, i % 2
                e.wait_ge(h_mm, s * 8 + (i + 1))
                e.activation(HT[:, mc * W + hf * HALF:mc * W + (hf + 1) * HALF], bank(2 + i % 6, HALF), ACT.Relu
                             ).then_inc(ht_ok, 1)
            e.wait_ge(y_var, s + 1)
            e.activation(sd[:, 0:TI], v3(mv[:, 0:2 * TI], 2)[:, :, 1], ACT.Sqrt, bias=eps_ln[:, 0:1]).then_inc(y_sd, 1)

        def norm_five(e, s, mm, var, sdq, g, b):
            for j in range(TI):
                e.wait_ge(mm, s * TI + (j + 1))
                e.bn_stats(bn[:, j * 6:(j + 1) * 6], bank(2 + j, C))
            e.drain()
            for j in range(TI):
                e.bn_aggr(mv[:, 2 * j:2 * j + 2], bn[:, j * 6:(j + 1) * 6])
            e.drain().then_inc(var, 1)
            e.wait_ge(sdq, s + 1)
            e.reciprocal(rs[:, 0:TI], sd[:, 0:TI])
            e.drain()
            for j in range(TI):
                e.tensor_scalar(LM[:, j * C:(j + 1) * C], bank(2 + j, C), mv[:, 2 * j:2 * j + 1], rs[:, j:j + 1],
                                ALU.subtract, ALU.mult)
            e.drain()
            lm3 = v3(LM, C)
            e.tensor_tensor(lm3, lm3, g.rearrange("p (o c) -> p o c", o=1).to_broadcast([P, TI, C]), ALU.mult)
            e.drain()
            e.tensor_tensor(lm3, lm3, b.rearrange("p (o c) -> p o c", o=1).to_broadcast([P, TI, C]), ALU.add)
            e.drain()

        def mixB_dve(e, s):
            e.wait_ge(Front.xs_in, fronts["fb"].loaded(s))
            e.tensor_tensor(X[:, bass.ds(s * (TI * C), TI * C)], X[:, bass.ds(s * (TI * C), TI * C)], XS[:, :], ALU.add
                            ).then_inc(xb_ok, 1)
            for i in range(4):
                e.wait_ge(q_mm, s * 4 + (i + 1))
                e.tensor_scalar(QN[:, i * HALF:(i + 1) * HALF], bank(2 + i, HALF), 0.0, None, ALU.min).then_inc(q_mn, 1)
            for i in range(4):
                e.wait_ge(q_ex, s * 4 + (i + 1))
                e.scalar_tensor_tensor(QT[:, i // 2, (i % 2) * HALF:(i % 2 + 1) * HALF], bank(2 + i, HALF), 0.0,
                                       QE[:, i * HALF:(i + 1) * HALF], ALU.max, ALU.add).then_inc(q_ok, 1)
            for i in range(4):
                e.wait_ge(nd_mm, s * 4 + (i + 1))
                e.tensor_scalar(RD[:, i * HALF:(i + 1) * HALF], bank(2 + i, HALF), 1e-6, None, ALU.add)
            e.drain()
            e.reciprocal(RD, RD)
            e.drain()
            for i in range(4):
                e.tensor_tensor(MT[:, i // 2, (i % 2) * HALF:(i % 2 + 1) * HALF], bank(NUMBANK[i], HALF),
                                RD[:, i * HALF:(i + 1) * HALF], ALU.mult)
            e.drain().then_inc(mt_ok, 1)
            norm_five(e, s, m_mm, m_var, m_sd, g1r, b1r)
            e.drain().then_inc(lm_ok, 1)
            norm_five(e, s, y_mm, y_var, y_sd, g2r, b2r)
            e.tensor_tensor(X[:, bass.ds(s * (TI * C), TI * C)], X[:, bass.ds(s * (TI * C), TI * C)], LM, ALU.add)

        G = BUF[:, 0:GROUP * 257]
        OH = BUF[:, 4112:4112 + GROUP * P]
        HOT = BUF[:, 6160:6160 + GROUP * P]
        WTS = BUF[:, 8208:8208 + GROUP]
        HB = 4

        QKV = BUF[:, 8224:8224 + 3 * C]
        qkv_d = dram("qkv_d", [NP, 3 * C])
        qkv_ev, qkv_st = sem("qkv_ev"), sem("qkv_st")

        class Hop:
            ids = sem("hop_ids")
            rows = [sem(f"hop_rows{i}") for i in range(4)]
            hot, oh, mm, add = sem("hop_hot"), sem("hop_oh"), sem("hop_mm"), sem("hop_add")

            def __init__(s, number, table, field):
                s.table, s.field = table, field
                s.turns0 = number * (CH_MAIN // GROUP)

        hops = [Hop(0, xn_d[0], 3), Hop(1, xn_d[2], 2), Hop(2, cur_d[0], 2), Hop(3, cur_d[1], 2)]

        def hop_pool(e, s):
            with e.Fori(0, CH_MAIN // GROUP) as k:
                for half in range(2):
                    pool_wait(e, s.mm, k * GROUP + (s.turns0 * GROUP + 8 * (half + 1)))
                    e.tensor_copy(ib[half][:, :], v3(rec_main[:, bass.ds((k * GROUP + 8 * half) * 4, 32)], 4)[:, :, 0]
                                  ).then_inc(s.ids, 1)
                    pool_wait(e, s.ids, k * 2 + (s.turns0 * 2 + half + 1))
                    for j in range(8):
                        slot = 8 * half + j
                        e.indirect_dma_start(G[:, slot * 257:slot * 257 + C], None, s.table,
                                             bass.IndirectOffsetOnAxis(ap=ib[half][:, j:j + 1], axis=0)
                                             ).then_inc(s.rows[slot // 4], 16)

        HTURNS = CH_MAIN // GROUP
        assert HTURNS == NT + 1

        def hop_pe(pe, s, first=0, last=HTURNS, part=None):
            with pe.Fori(first, last) as k:
                for j in range(GROUP):
                    if part is not None and j == 1:
                        f = fronts[f"f{part}"]
                        pe.wait_ge(Front.xs_in, k * 16 + (f.loads_before * 16 + 16))
                        for c in range(2):
                            mm = pe.transpose(bank(4, P, c * P), XS[:, c * P:(c + 1) * P], ident[:, :])
                        mm.then_inc(f.xt_tp, 1)
                    if part is not None and j == 7:
                        pe.wait_ge(f.xt_out, k + (f.before * TI + 1))
                        for c in range(2):
                            mm = pe.matmul(bank(5, C), XT[:, c * P:(c + 1) * P], wsh[:, 2 * part + c, :], start=(c == 0),
                                           stop=(c == 1))
                        if part > 0:
                            mm.then_inc(g1_mm, 1)
                    if part == 0 and j in (9, 11):
                        c = (j - 9) // 2
                        if c == 0:
                            pe.wait_ge(qkv_ev, k + 1)
                        pe.matmul(bank(6), XT[:, c * P:(c + 1) * P], wqkvT[:, c, C:3 * C], start=(c == 0), stop=(c == 1))
                    if part == 0 and j == 13:
                        for c in range(2):
                            mm = pe.matmul(bank(7, C), XT[:, c * P:(c + 1) * P], wqkvT[:, c, 0:C], start=(c == 0),
                                           stop=(c == 1))
                        mm.then_inc(g1_mm, 1)
                    if j % 4 == 0:
                        pe.wait_ge(s.rows[j // 4], k * 64 + (s.turns0 * 64 + 64))
                    pe.wait_ge(s.oh, k * GROUP + (s.turns0 * GROUP + j + 1))
                    pe.wait_ge(s.add, k * GROUP + (s.turns0 * GROUP + j + 1))
                    pe.matmul(bank(j % HB, 257), OH[:, j * P:(j + 1) * P], G[:, j * 257:(j + 1) * 257],
                              start=True, stop=True).then_inc(s.mm, 1)

        def one_hots(e, dst, lanes, k, op):
            lane = v3(lanes[:, bass.ds(k * (GROUP * 4), GROUP * 4)], 4)[:, :, LANE:LANE + 1].to_broadcast([P, GROUP, P])
            column = iota_row[:, :].rearrange("p (o c) -> p o c", o=1).to_broadcast([P, GROUP, P])
            return e.tensor_tensor(v3(dst, P), column, lane, op)

        def hop_act(e, s, first=0, last=HTURNS, part=None):
            with e.Fori(first, last) as k:
                e.wait_ge(s.hot, k + (s.turns0 + 1))
                for j in range(GROUP):
                    e.wait_ge(s.mm, k * GROUP + (s.turns0 * GROUP + j + 1))
                    e.activation(OH[:, j * P:(j + 1) * P], HOT[:, j * P:(j + 1) * P], ACT.Copy, scale=WTS[:, j:j + 1]
                                 ).then_inc(s.oh, 1)
                    if part is not None and j == 5:
                        f = fronts[f"f{part}"]
                        e.wait_ge(f.xt_tp, k + (f.before * TI + 1))
                        e.activation(XT[:, 0:C], bank(4, C), ACT.Copy).then_inc(f.xt_out, 1)
                if part == 0:
                    e.wait_ge(qkv_st, k * 16 + 16)
                    e.wait_ge(g1_mm, k + 1)
                    e.activation(QKV[:, 0:C], bank(7, C), ACT.Copy)
                    e.activation(QKV[:, C:3 * C], bank(6), ACT.Copy)
                    e.drain().then_inc(qkv_ev, 1)

        def hop_hots(e, s, k):
            recf = rec_main[:, :].bitcast(F32)
            e.tensor_scalar(WTS, v3(recf[:, bass.ds(k * (GROUP * 4), GROUP * 4)], 4)[:, :, s.field], 1.0, None, ALU.mult)
            one_hots(e, HOT, recf, k, ALU.is_equal)
            e.drain().then_inc(s.hot, 1)

        def hop_dve(e, s, part=None):
            def turn(k, last):
                tiles = tiles_of(tile_main, k)
                for j in range(GROUP):
                    e.wait_ge(s.mm, k * GROUP + (s.turns0 * GROUP + j + 1 + GROUP))
                    dst = ACC[:, bass.ds(tiles[j] * 257, 257)]
                    e.tensor_tensor(dst, bank(j % HB, 257), dst, ALU.add)
                    e.drain().then_inc(s.add, 1)
                    if j == 8 and not last:
                        e.wait_ge(s.oh, k * GROUP + (s.turns0 * GROUP + GROUP))
                        hop_hots(e, s, k + 1)
                if part is not None and not last:
                    e.wait_ge(g1_mm, k + (part * NT + 1))
                    x = X[:, bass.ds(k * C, C)]
                    e.tensor_tensor(x, bank(5, C), x, ALU.add)

            hop_hots(e, s, 0)
            with e.Fori(0, HTURNS - 1) as k:
                turn(k, False)
            turn(HTURNS - 1, True)

        DEG = WS[:, 800:825]
        g0_rows, g0_mm, deg_ok, dsd_ok = sem("g0_rows"), sem("g0_mm"), sem("deg_ok"), sem("dsd_ok")

        def gnn0_pe(pe, s):
            f = fronts["fg"]
            for j in range(TI):
                if j == 0:
                    pe.wait_ge(g0_rows, s + 1)
                if j >= 2:
                    pe.wait_ge(f.xt_out, f.tiles(s, j - 1))
                for c in range(2):
                    mm = pe.transpose(bank(j % 2, P, c * P), XS3[:, j, c * P:(c + 1) * P], ident[:, :])
                mm.then_inc(f.xt_tp, 1)
            for j in range(TI):
                pe.wait_ge(f.xt_out, f.tiles(s, j + 1))
                for c in range(2):
                    mm = pe.matmul(bank(2 + j, C), XT3[:, c, j * P:(j + 1) * P], wg0[:, c, :],
                                   start=(c == 0), stop=(c == 1))
                mm.then_inc(g0_mm, 1)

        def gnn0_dve(e, s):
            for j in range(TI):
                e.tensor_scalar(XS3[:, j, :], ACC[:, bass.ds((s * TI + j) * 257, C)], DEG[:, bass.ds(s * TI + j, 1)],
                                None, ALU.mult)
            e.drain().then_inc(g0_rows, 1)
            add_banks(e, s, g0_mm)

        def add_banks(e, s, mm, before=0):
            for j in range(TI):
                e.wait_ge(mm, s * TI + (before + j + 1))
                x = X[:, bass.ds((s * TI + j) * C, C)]
                e.tensor_tensor(x, bank(2 + j, C), x, ALU.add)

        def narrow_pe(pe, f, s, w, n, mm):
            for j in range(TI):
                if j == 0:
                    pe.wait_ge(g0_rows, s + (f.rows_before + 1))
                if j >= 2:
                    pe.wait_ge(f.xt_out, f.tiles(s, j - 1))
                for c in range(2):
                    m = pe.transpose(bank(j % 2, P, c * P), XS3[:, j, c * P:(c + 1) * P], ident[:, :])
                m.then_inc(f.xt_tp, 1)
            for j in range(TI):
                pe.wait_ge(f.xt_out, f.tiles(s, j + 1))
                for c in range(2):
                    m = pe.matmul(bank(2 + j, n), XT3[:, c, j * P:(j + 1) * P], w[:, c, :], start=(c == 0), stop=(c == 1))
                m.then_inc(mm, 1)

        def narrow_dve(e, s, dst, pitch, n, mm, before=0):
            e.tensor_scalar(XS3, v3(ACC[:, bass.ds(s * (TI * 257), TI * 257)], 257)[:, :, 0:C], 1.0, None, ALU.mult
                            ).then_inc(g0_rows, 1)
            for j in range(TI):
                e.wait_ge(mm, s * TI + (before + j + 1))
                e.tensor_scalar(dst[:, bass.ds((s * TI + j) * pitch, n)], bank(2 + j, n), 1.0, None, ALU.mult)

        wgat = v3(WS[:, 900:932], 16)
        wgate = v3(WS[:, 940:956], 8)
        attrow = ROWS[:, 1024:1104]
        SRT = WT[:, 8192:8192 + NT * 20]
        DTT = WT[:, 8700:8700 + NT * 8]
        MX = WT[:, 8900:9000]
        ES = WT[:, 9000:9100]
        SC = WT[:, 9100:9200]
        AG = WT[:, 9200:9200 + NT * 20]
        GT = WT[:, 9700:9700 + NT * 16]
        GG = WT[:, 10240:10240 + CH_GAT * 20]
        STB = BUF[:, 2624:2624 + NT * 32]
        SPL = BUF[:, 3424:3474].bitcast(BF16)
        REST = BUF[:, 3480:3580]
        GSL = BUF[:, 0:GROUP * 32]
        DSL = BUF[:, 320:320 + GROUP * 8]
        EE = BUF[:, 448:448 + GROUP * 4]
        MSG = BUF[:, 512:512 + GROUP * 20]
        RED = BUF[:, 832:832 + GROUP * 4]
        OM = BUF[:, 1024:2048].bitcast(BF16)
        ASRC = BUF[:, 2048:2048 + GH * 96]
        SELF = BUF[:, 2592:2592 + GROUP]
        AT = BUF[0:96, 3600:3856].bitcast(BF16)
        SEL = BUF[:, 2568:2568 + GROUP // 2].bitcast(BF16)
        OHG = BUF[:, 4096:4096 + GROUP * P]
        gp_mm, src_ready, src_out, dst_ready, dst_out = (sem(x) for x in (
            "gp_mm", "src_ready", "src_out", "dst_ready", "dst_out"))
        gat_ids = sem("gat_ids")
        gat_rows = [sem(f"gat_rows{i}") for i in range(2)]
        gat_oh, gat_mm, gat_add, gat_tp, gat_at, gat_msg, gat_e, gat_ex = (sem("gat_" + x) for x in (
            "oh", "mm", "add", "tp", "at", "msg", "e", "ex"))
        gat_kept = sem("gat_kept")
        GTURNS = CH_GAT // GROUP
        sc_var, sc_sd, sc_e, sc_ex = (sem("sc_" + x) for x in ("var", "sd", "e", "ex"))

        def gat_pool(e, second):
            t0 = GTURNS if second else 0
            slots, width, table, field = (DSL, 8, dst_tab_d, 2) if second else (GSL, 32, src_tab_d, 0)
            with e.Fori(0, GTURNS) as k:
                for half in range(2):
                    if second:
                        pool_wait(e, gat_e, k * 2 + (half + 1))
                    else:
                        pool_wait(e, gat_kept, k * 2 + (half + 1))
                    e.tensor_copy(ib[half][:, :], v3(rec_gat[:, bass.ds((k * GROUP + 8 * half) * 4, 32)], 4)[:, :, field]
                                  ).then_inc(gat_ids, 1)
                    pool_wait(e, gat_ids, k * 2 + (t0 * 2 + half + 1))
                    for j in range(8):
                        slot = 8 * half + j
                        e.indirect_dma_start(slots[:, slot * width:(slot + 1) * width], None, table,
                                             bass.IndirectOffsetOnAxis(ap=ib[half][:, j:j + 1], axis=0)
                                             ).then_inc(gat_rows[half], 16)

        def gatA_act(e, first, last, dense):
            with e.Fori(first, last) as k:
                e.wait_ge(gat_tp, k + 1)
                for half in range(2):
                    e.wait_ge(gat_rows[half], k * 128 + 128)
                    e.sem_inc(carried, 1)
                    rows = v3(GSL[:, 256 * half:256 * half + 256], 32)
                    e.activation(v3(GG[:, bass.ds((k * GROUP + 8 * half) * 20, 160)], 20), rows[:, :, 0:20], ACT.Copy)
                    for q in range(3):
                        e.activation(ASRC.rearrange("p (h q j) -> p q j h", h=GH, q=3)[:, q, 8 * half:8 * half + 8],
                                     rows[:, :, 20 + 4 * q:24 + 4 * q], ACT.Copy)
                    e.drain().then_inc(gat_kept, 1)
                e.wait_ge(gat_tp, k + 2)
                e.activation(AT, bank(4, 512, 0, 96), ACT.Copy).then_inc(gat_at, 1)
                if dense:
                    dense_act(e, k)

        def gatA_pe(pe, first, last, dense):
            with pe.Fori(first, last) as k:
                for half in range(2):
                    pe.wait_ge(gat_kept, k * 2 + (3 + half))
                pe.wait_ge(gat_at, k + 1)
                for h in range(GH):
                    mm = pe.transpose(bank(4, P, h * P, 96), ASRC[:, h * 96:(h + 1) * 96], ident[:, :])
                mm.then_inc(gat_tp, 1)
                pe.wait_ge(gat_at, k + 2)
                pe.wait_ge(gat_oh, k + 1)

                def scores(x):
                    for j in range(4 * x, 4 * x + 4):
                        pe.wait_ge(gat_add, k * GROUP + (j + 1))
                        pe.matmul(bank(j % 4), SEL[0:96, j:j + 1].to_broadcast([96, P]), AT, start=True, stop=False)
                        pe.matmul(bank(j % 4), OM[:, j * P:(j + 1) * P], ident_b[:, :], start=False, stop=True
                                  ).then_inc(gat_mm, 1)

                if dense:
                    dense_pe(pe, k, scores)
                else:
                    for x in range(GROUP // 4):
                        scores(x)

        def gatA_dve(e):
            with e.Fori(0, GTURNS) as k:
                one_hots(e, OM, rec_gat[:, :].bitcast(F32), k, ALU.not_equal)
                e.drain().then_inc(gat_oh, 1)
                tiles = tiles_of(tile_gat, k)
                for j in range(GROUP):
                    e.wait_ge(gat_mm, k * GROUP + (j + 1 + GROUP))
                    e.tensor_reduce(RED[:, j * 4:j * 4 + 4], v3(bank(j % 4), P), AX.X, ALU.max)
                    e.drain().then_inc(gat_add, 1)
                    m = MX[:, bass.ds(tiles[j] * 4, 4)]
                    e.tensor_tensor(m, m, RED[:, j * 4:j * 4 + 4], ALU.max)
                e.drain()

        def gatB_act(e):
            with e.Fori(0, GTURNS) as k:
                def scores():
                    e.wait_ge(gat_e, k * 2 + 4)
                    e.activation(EE, EE, ACT.Exp).then_inc(gat_ex, 1)

                dense_act(e, k + DA, scores)

        def gatB_pe(pe):
            g0 = GTURNS * GROUP
            with pe.Fori(0, GTURNS) as k:

                def sums(x):
                    for j in range(4 * x, 4 * x + 4):
                        pe.wait_ge(gat_msg, k + 1)
                        pe.wait_ge(gat_add, k * GROUP + (g0 + j + 1))
                        pe.matmul(bank(j % 4, 20), OHG[:, j * P:(j + 1) * P], MSG[:, j * 20:(j + 1) * 20],
                                  start=True, stop=True).then_inc(gat_mm, 1)

                dense_pe(pe, k + DA, sums)

        def gatB_dve(e):
            g0 = GTURNS * GROUP
            EE3 = v3(EE, 4)

            def scores(k, half):
                gg = v3(GG[:, bass.ds((k * GROUP + 8 * half) * 20, 160)], 20)
                ee = EE[:, 32 * half:32 * half + 32]
                ee3, dsl = v3(ee, 4), v3(DSL[:, 64 * half:64 * half + 64], 8)
                e.wait_ge(gat_rows[half], k * 128 + (GTURNS * 128 + 128))
                seq(e, lambda: e.tensor_tensor(ee3, gg[:, :, 16:20], dsl[:, :, 0:4], ALU.add),
                    lambda: e.scalar_tensor_tensor(ee, ee, 0.2, ee, ALU.mult, ALU.max),
                    lambda: e.tensor_tensor(ee3, ee3, dsl[:, :, 4:8], ALU.subtract),
                    lambda: e.tensor_scalar(ee, ee, 0.0, None, ALU.min))
                e.drain().then_inc(gat_e, 1)

            def turn(k, last):
                one_hots(e, OHG, rec_gat[:, :].bitcast(F32), k, ALU.is_equal)
                gg = v3(GG[:, bass.ds(k * (GROUP * 20), GROUP * 20)], 20)
                e.wait_ge(gat_ex, k + 1)
                e.tensor_tensor(v3(MSG, 20)[:, :, 0:16].rearrange("p g (h e) -> p g h e", h=GH),
                                gg[:, :, 0:16].rearrange("p g (h e) -> p g h e", h=GH),
                                EE3.rearrange("p g (h o) -> p g h o", o=1).to_broadcast([P, GROUP, GH, GE]), ALU.mult)
                e.tensor_copy(v3(MSG, 20)[:, :, 16:20], EE3)
                e.drain().then_inc(gat_msg, 1)
                tiles = tiles_of(tile_gat, k)
                for j in range(GROUP):
                    e.wait_ge(gat_mm, k * GROUP + (g0 + j + 1 + GROUP))
                    dst = AG[:, bass.ds(tiles[j] * 20, 20)]
                    e.tensor_tensor(dst, bank(j % 4, 20), dst, ALU.add)
                    e.drain().then_inc(gat_add, 1)
                    if j % 8 == 7 and not last:
                        scores(k + 1, j // 8)

            for half in range(2):
                scores(0, half)
            with e.Fori(0, GTURNS - 1) as k:
                turn(k, False)
            turn(GTURNS - 1, True)

        def seq(e, *steps):
            for step in steps:
                step()
                e.drain()

        def over_tiles(row, n):
            return row.rearrange("p (o c) -> p o c", o=1).to_broadcast([P, NT, n])

        def head_sum(e, dst, tab, att, tmp):
            seq(e, lambda: e.tensor_tensor(v3(tmp, 16), tab, over_tiles(att, 16), ALU.mult),
                lambda: e.tensor_reduce(dst, tmp.rearrange("p (t h e) -> p t h e", h=GH, e=GE), AX.X, ALU.add))

        def gat_tables_dve(e):
            srt, dtt = v3(SRT, 20), v3(DTT, 8)
            head_sum(e, srt[:, :, 16:20], srt[:, :, 0:16], attrow[:, 0:16], GT)
            stb, spl, rest = v3(STB, 32), v3(SPL, 4), v3(REST, 4)
            part = [stb[:, :, 20 + 4 * q:24 + 4 * q] for q in range(3)]
            seq(e, lambda: e.tensor_copy(stb[:, :, 0:20], srt),
                lambda: e.tensor_copy(spl, srt[:, :, 16:20]),
                lambda: e.tensor_copy(part[0], spl),
                lambda: e.tensor_tensor(rest, srt[:, :, 16:20], part[0], ALU.subtract),
                lambda: e.tensor_copy(spl, rest),
                lambda: e.tensor_copy(part[1], spl),
                lambda: e.tensor_tensor(part[2], rest, part[1], ALU.subtract))
            e.drain().then_inc(src_ready, 1)
            e.memset(ASRC, 0.0)
            e.tensor_tensor(SELF, ident[:, 0:GROUP], ident[:, 32:32 + GROUP], ALU.add)
            e.drain()
            e.tensor_tensor(SEL, SELF, ident[:, 64:64 + GROUP], ALU.add)
            head_sum(e, dtt[:, :, 0:4], srt[:, :, 0:16], attrow[:, 16:32], GT)
            e.tensor_copy(v3(MX, 4), srt[:, :, 16:20])
            rf = v3(rec_gat[:, :].bitcast(F32), 4)
            e.wait_ge(gat.back, 16)
            lane = rf[:, :, LANE]
            seq(e, lambda: e.scalar_tensor_tensor(lane, lane, 1.0, rf[:, :, 3], ALU.add, ALU.mult),
                lambda: e.tensor_scalar(lane, lane, -1.0, None, ALU.add))

        def gat_max_dve(e):
            srt, dtt, mx, es, ag = v3(SRT, 20), v3(DTT, 8), v3(MX, 4), v3(ES, 4), v3(AG, 20)
            seq(e, lambda: e.tensor_tensor(mx, mx, dtt[:, :, 0:4], ALU.add),
                lambda: e.scalar_tensor_tensor(dtt[:, :, 4:8], mx, 0.2, mx, ALU.mult, ALU.max))
            e.drain().then_inc(dst_ready, 1)
            seq(e, lambda: e.tensor_tensor(es, srt[:, :, 16:20], dtt[:, :, 0:4], ALU.add),
                lambda: e.scalar_tensor_tensor(ES, ES, 0.2, ES, ALU.mult, ALU.max),
                lambda: e.tensor_tensor(es, es, dtt[:, :, 4:8], ALU.subtract))
            e.drain().then_inc(sc_e, 1)
            e.wait_ge(sc_ex, 1)
            e.tensor_copy(ag[:, :, 16:20], es)
            e.tensor_tensor(ag[:, :, 0:16].rearrange("p g (h e) -> p g h e", h=GH),
                            srt[:, :, 0:16].rearrange("p g (h e) -> p g h e", h=GH),
                            es.rearrange("p g (h o) -> p g h o", o=1).to_broadcast([P, NT, GH, GE]), ALU.mult)
            e.drain()

        def top_two(e, s, n, rank, tmp, sel):
            s3, r3, t3 = v3(s, n), v3(rank, n), v3(tmp, n)
            e.memset(rank, 0.0)
            for j in range(n):
                sj = s3[:, :, j:j + 1]
                e.tensor_tensor(t3[:, :, 0:j + 1], sj.to_broadcast([P, NT, j + 1]), s3[:, :, 0:j + 1], ALU.is_gt)
                if j + 1 < n:
                    e.tensor_tensor(t3[:, :, j + 1:n], sj.to_broadcast([P, NT, n - j - 1]), s3[:, :, j + 1:n], ALU.is_ge)
                e.drain()
                e.tensor_tensor(rank, rank, tmp, ALU.add)
                e.drain()
            e.tensor_scalar(sel, rank, 2.0, None, ALU.is_lt)
            e.drain()

        def bc(col, n):
            return col.rearrange("p (t o) -> p t o", o=1).to_broadcast([P, NT, n])

        def gat_scores_dve(e):
            ag, gt, es, sc = v3(AG, 20), v3(GT, 16), v3(ES, 4), v3(SC, 4)
            col, col2 = sd[:, :], rs[:, :]
            g4 = gt.rearrange("p t (h e) -> p t h e", h=GH)
            seq(e, lambda: e.tensor_scalar(es, ag[:, :, 16:20], 1e-16, None, ALU.add),
                lambda: e.reciprocal(ES, ES),
                lambda: e.tensor_tensor(g4, ag[:, :, 0:16].rearrange("p t (h e) -> p t h e", h=GH),
                                        es.rearrange("p g (h o) -> p g h o", o=1).to_broadcast([P, NT, GH, GE]), ALU.mult),
                lambda: e.tensor_tensor(gt, gt, over_tiles(attrow[:, 32:48], 16), ALU.add),
                lambda: e.tensor_reduce(col, gt, AX.X, ALU.add),
                lambda: e.tensor_scalar(col, col, 1.0 / 16, None, ALU.mult),
                lambda: e.tensor_tensor(gt, gt, bc(col, 16), ALU.subtract),
                lambda: e.tensor_tensor(ag[:, :, 0:16], gt, gt, ALU.mult),
                lambda: e.tensor_reduce(col, ag[:, :, 0:16], AX.X, ALU.add),
                lambda: e.tensor_scalar(col, col, 1.0 / 16, LN_EPS, ALU.mult, ALU.add))
            e.drain().then_inc(sc_var, 1)
            e.wait_ge(sc_sd, 1)
            seq(e, lambda: e.reciprocal(col, col2),
                lambda: e.tensor_tensor(gt, gt, bc(col, 16), ALU.mult),
                lambda: e.tensor_tensor(gt, gt, over_tiles(attrow[:, 48:64], 16), ALU.mult),
                lambda: e.tensor_tensor(gt, gt, over_tiles(attrow[:, 64:80], 16), ALU.add),
                lambda: e.tensor_reduce(sc, GT.rearrange("p (t h e) -> p t e h", h=GH, e=GE), AX.X, ALU.add),
                lambda: e.tensor_scalar(SC, SC, 1.0 / GH, None, ALU.mult),
                lambda: e.tensor_reduce(col, sc, AX.X, ALU.max))
            top_two(e, SC, EXP0, MX, GT[:, 0:100], ES)
            g = gates[:, 0:NT * EXP0]
            e.tensor_tensor(v3(g, 4), sc, bc(col, 4), ALU.subtract)
            e.drain().then_inc(sc_e, 1)
            e.wait_ge(sc_ex, 2)
            seq(e, lambda: e.tensor_tensor(g, g, ES, ALU.mult),
                lambda: e.tensor_reduce(col, v3(g, 4), AX.X, ALU.add),
                lambda: e.reciprocal(col2, col),
                lambda: e.tensor_tensor(v3(g, 4), v3(g, 4), bc(col2, 4), ALU.mult))

        DA = NT - GTURNS
        FH = BUF[:, 6144:6144 + 2 * HID]
        YE = BUF[:, 7168:7168 + EXP0 * C]
        YL = BUF[:, 0:2 * TI * EXP0 * C]
        GTS = BUF[0:8, 10240:10240 + W]
        GC = WS[:, 1270:1270 + TI * 8]
        B1T = WS[:, 960:992]
        B2R = WS[0:8, 1010:1266]
        y0_d = dram("y0_d", [NP, EXP0 * C])
        (moe_gc, moe_gt, moe_gts, moe_b2, moe_h, moe_ha, moe_y, moe_ya, moe_out, moe_used) = (
            sem("moe_" + x) for x in ("gc", "gt", "gts", "b2", "h", "ha", "y", "ya", "out", "used"))
        moe_in = [sem(f"moe_in{i}") for i in range(2)]
        w_ffn, rows_ffn = sem("w_ffn"), sem("rows_ffn")
        w1e = WT[:, 0:EXP0 * 1024].rearrange("p (e k n) -> p e k n", e=EXP0, k=2)
        w2e = WT[:, EXP0 * 1024:EXP0 * 2048].rearrange("p (e k n) -> p e k n", e=EXP0, k=4)

        def dense_pe(pe, n, between):
            f = fronts["ff"]
            pe.wait_ge(moe_ya, n * EXP0 + 1)
            pe.wait_ge(Front.xs_in, n * 16 + (f.loads_before * 16 + 16))
            for c in range(2):
                mm = pe.transpose(bank(7, P, c * P), XS[:, c * P:(c + 1) * P], ident[:, :])
            mm.then_inc(f.xt_tp, 1)

            def hidden(x):
                for mc in range(4):
                    for c in range(2):
                        mm = pe.matmul(bank(5 + x % 2, P, mc * P), w1e[:, x, c, mc * P:(mc + 1) * P],
                                       XT[:, c * P:(c + 1) * P], start=(c == 0), stop=(c == 1), skip_group_check=True)
                mm.then_inc(moe_h, 1)

            pe.wait_ge(f.xt_out, n + (f.before * TI + 1))
            hidden(0)
            hidden(1)
            for x in range(EXP0):
                pe.wait_ge(moe_ha, n * EXP0 + (x + 1))
                if x:
                    pe.wait_ge(moe_ya, n * EXP0 + (x + 1))
                for c in range(4):
                    mm = pe.matmul(bank(7, C), FH[:, (x % 2) * HID + c * P:(x % 2) * HID + (c + 1) * P], w2e[:, x, c, :],
                                   start=(c == 0), stop=(c == 3))
                mm.then_inc(moe_y, 1)
                between(x)
                if x + 2 < EXP0:
                    hidden(x + 2)

        def dense_act(e, n, between=None):
            f = fronts["ff"]
            e.wait_ge(f.xt_tp, n + (f.before * TI + 1))
            e.activation(XT[:, 0:C], bank(7, C), ACT.Copy).then_inc(f.xt_out, 1)
            if between:
                between()

            def gelu(x):
                e.wait_ge(moe_h, n * EXP0 + (x + 1))
                for mc in range(4):
                    at = (x % 2) * HID + mc * P
                    a_ = e.activation(FH[:, at:at + P], bank(5 + x % 2, P, mc * P), ACT.Gelu,
                                      bias=B1T[:, x * 4 + mc:x * 4 + mc + 1])
                a_.then_inc(moe_ha, 1)

            gelu(0)
            e.wait_ge(moe_out, n * 16 + 16)
            gelu(1)
            for x in range(EXP0):
                e.wait_ge(moe_y, n * EXP0 + (x + 1))
                e.activation(YE[:, x * C:(x + 1) * C], bank(7, C), ACT.Copy).then_inc(moe_ya, 1)
                if x + 2 < EXP0:
                    gelu(x + 2)

        def dense_load(sp, n):
            sp.wait_ge(Front.xt_tp, n + fronts["ff"].before * TI)
            sp.dma_start(XS[:, 0:C], xn_d[1][bass.ds(n * P, P), :]).then_inc(Front.xs_in, 16)

        def dense_store(sp, n):
            sp.wait_ge(moe_ya, n * EXP0 + (EXP0 + 1))
            sp.dma_start(y0_d[bass.ds(n * P, P), :], YE).then_inc(moe_out, 16)

        def turn_results(sp, s, slot):
            at = slot * TI * EXP0 * C
            sp.dma_start(YL[:, at:at + TI * EXP0 * C].rearrange("p (j c) -> p j c", j=TI),
                         y0_d[s * W:(s + 1) * W, :].rearrange("(j p) c -> p j c", p=P)).then_inc(moe_in[slot], 16)

        def mix_pe(pe, s):
            pe.wait_ge(moe_gc, s + 1)
            for j in range(TI):
                mm = pe.transpose(bank(6 + j // 4, P, (j % 4) * P, EXP0), GC[:, j * EXP0:(j + 1) * EXP0], ident[:, :])
            mm.then_inc(moe_gt, 1)
            pe.wait_ge(moe_gts, s + 1)
            for j in range(TI):
                pe.matmul(bank(1 + j, C), GTS[0:EXP0, j * P:(j + 1) * P], B2R[0:EXP0, :], start=True, stop=True
                          ).then_inc(moe_b2, 1)

        def mix_act(e, s):
            e.wait_ge(moe_gt, s + 1)
            e.activation(GTS[0:EXP0, 0:4 * P], bank(6, 4 * P, 0, EXP0), ACT.Copy)
            e.activation(GTS[0:EXP0, 4 * P:5 * P], bank(7, P, 0, EXP0), ACT.Copy)
            e.drain().then_inc(moe_gts, 1)

        def mix_dve(e, s):
            e.tensor_copy(GC[:, 0:TI * EXP0], gates[:, s * (TI * EXP0):(s + 1) * (TI * EXP0)]).then_inc(moe_gc, 1)
            e.wait_ge(moe_in[s % 2], s // 2 * 16 + 16)
            for x in range(EXP0):
                e.drain()
                for j in range(TI):
                    row = X[:, (s * TI + j) * C:(s * TI + j + 1) * C]
                    at = (s % 2) * TI * EXP0 * C + (j * EXP0 + x) * C
                    e.scalar_tensor_tensor(row, YL[:, at:at + C], GC[:, j * EXP0 + x:j * EXP0 + x + 1], row, ALU.mult, ALU.add)
            e.drain().then_inc(moe_used, 1)
            for j in range(TI):
                row = X[:, (s * TI + j) * C:(s * TI + j + 1) * C]
                e.wait_ge(moe_b2, s * TI + (j + 1))
                e.tensor_tensor(row, bank(1 + j, C), row, ALU.add)

        wsh = v3(WT[:, 0:2048], C)
        g1_mm = sem("g1_mm")

        def tile_loads(sp, i, table):
            f = fronts[f"f{i}"]

            def load(n):
                sp.wait_ge(f.xt_tp, n + f.before * TI)
                sp.dma_start(XS[:, 0:C], table[bass.ds(n * P, P), :]).then_inc(f.xs_in, 16)

            def store(n):
                sp.wait_ge(qkv_ev, n + 2)
                sp.dma_start(qkv_d[bass.ds(n * P, P), :], QKV).then_inc(qkv_st, 16)

            load(0)
            with sp.Fori(1, NT) as n:
                load(n)
                if i == 0:
                    store(n - 1)
            if i == 0:
                store(NT - 1)

        def gnn1_pe(pe, i, s):
            f = fronts[f"f{i}"]
            front_pe(pe, f, s)
            for j in range(TI):
                pe.wait_ge(f.xt_out, f.tiles(s, j + 1))
                for c in range(2):
                    mm = pe.matmul(bank(2 + j, C), XT3[:, c, j * P:(j + 1) * P], wsh[:, 2 * i + c, :],
                                   start=(c == 0), stop=(c == 1))
                mm.then_inc(g1_mm, 1)

        wqkv = v3(WT[:, 2048:3584], C)
        wqkvT = v3(WT[:, 3584:5120], 768)
        wproj = v3(WT[:, 5120:5632], C)
        wprojT = v3(WT[:, 5632:6144], C)
        HV = 33
        MF = WT[:, 6144:6144 + FC * 8 * HV]
        F0 = WT[:, 7680:7680 + 8 * FC * P]
        F1 = BUF[:, 0:8 * FC * P]
        HS = 4 * FG * 32
        MFT = BUF[0:HV, 0:2 * HS]
        YT = WT[0:HV, 12800:12800 + 8 * P]
        V4 = BUF[:, 7680:7680 + 2 * 4 * HV]
        v_in = moe_in
        V_BEFORE = (16 * 3, 16 * 2)
        assert TURNS == 5
        K2 = BUF[:, 9088:9088 + 2 * 512]
        SQ = WT[:, 13824:13824 + TI * C]
        QA = ACC[:, 0:NT * C]
        RNA, RIA = WT[:, 15104:15304], WT[:, 15304:15504]
        OB = BUF[:, 6400:6400 + C]
        XO = BUF[:, 7680:7680 + C]
        RN = WS[:, 1320:1360]
        TS = WS[:, 1400:1408]
        coef = WS[:, 1000:1000 + FC]
        bq, bk, bv = ROWS[:, 0:C], ROWS[:, C:2 * C], ROWS[:, 2 * C:3 * C]
        bproj, obias, temp = ROWS[:, 768:1024], ROWS[:, 1104:1360], ROWS[:, 1360:1368]
        w_in1, rows_in1 = sem("w_in1"), sem("rows_in1")
        (m_tp, m_in, m_sq, m_rt, m_f, m_fu, m_fq, m_ft, m_y1, m_ob, m_xo, m_xe, m_xa, m_p) = (
            sem("m1_" + x) for x in ("tp", "in", "sq", "rt", "f", "fu", "fq", "ft", "y", "ob", "xo",
                                     "xe", "xa", "p"))
        m_k2, m_fp, m_ma, m_yt, m_z = (sem("m1_" + x) for x in ("k2", "fp", "ma", "yt", "z"))

        def weights_pe(pe):
            pe.wait_ge(w_in1, 48)
            blocks = [(wqkv[:, r, c * P:(c + 1) * P]) for c in range(2) for r in range(6)]
            blocks += [(wproj[:, r, c * P:(c + 1) * P]) for c in range(2) for r in range(2)]
            for i, b in enumerate(blocks):
                mm = pe.transpose(bank(i // 4, P, (i % 4) * P), b, ident[:, :])
            mm.then_inc(m_tp, 1)

        def weights_act(e):
            e.wait_ge(m_tp, 1)
            e.activation(WT[:, 3584:4096], bank(0), ACT.Copy)
            e.activation(WT[:, 4096:4608], bank(1), ACT.Copy)
            e.activation(WT[:, 4608:5120], bank(2), ACT.Copy)
            e.activation(WT[:, 5632:6144], bank(3), ACT.Copy)

        def features(e, dst, k2, heads, offsets, linear=True):
            k3 = v3(k2, 64)
            f3 = dst.rearrange("p (h g i) -> p h g i", h=heads, i=32)
            for r in offsets:
                e.tensor_tensor(f3[:, :, r, :], k3[:, :, 0:32], k3[:, :, r:r + 32], ALU.mult)
            if linear:
                e.tensor_scalar(f3[:, :, R2, :], k3[:, :, 0:32], 1.0, None, ALU.mult)

        def norms_dve(e, rows, norms):
            seq(e, lambda: e.tensor_tensor(v3(SQ, C), rows, rows, ALU.mult),
                lambda: e.tensor_reduce(norms, v3(SQ, 32), AX.X, ALU.add))

        def over_five(row, n):
            return row.rearrange("p (o c) -> p o c", o=1).to_broadcast([P, TI, n])

        def m1_loads(sp):
            def rows(lo):
                sp.dma_start(v3(QA, C), qkv_d[:, lo:lo + C].rearrange("(t p) c -> p t c", p=P)).then_inc(m_in, 16)

            def values(t, half, slot, k):
                slot_free(sp, t, half, k)
                lo = 2 * C + half * P
                sp.dma_start(v3(V4[:, slot * 4 * HV:(slot + 1) * 4 * HV], HV)[:, :, 1:HV],
                             v3(qkv_d[bass.ds(t * P, P), lo:lo + P], 32)).then_inc(v_in[slot], 16)

            sp.wait_ge(qkv_st, 16 * NT + 16)
            sp.wait_ge(round_dve, R["gnn1"])
            rows(C)
            pairs(sp, values)
            sp.wait_ge(m_k2, 2 * NT)
            rows(0)

        def double_rows(e, factors, src, k2, heads):
            r = factors.rearrange("p (h o) -> p h o", o=1).to_broadcast([P, heads, 32])
            for half in range(2):
                e.tensor_tensor(v3(k2, 64)[:, :, 32 * half:32 * half + 32], v3(src, 32), r, ALU.mult)
            e.drain()

        def pairs(e, step):
            for half in range(2):
                step(0, half, 0, 0)
                step(1, half, 1, 0)
                with e.Fori(1, NT // 2) as k:
                    for slot in range(2):
                        step(k * 2 + slot, half, slot, k)
                step(NT - 1, half, 0, NT // 2)

        def slot_free(e, t, half, k, q=None, wait=None):
            q, wait = q or m_fu, wait or e.wait_ge
            n = half * NT + t
            if half == 1 and isinstance(t, int) and t == 0:
                wait(q, n)
            elif not (half == 0 and isinstance(t, int) and t < 2):
                wait(q, n - 1)

        def m1A_pe(pe, t, half, slot, k):
            n = half * NT + t
            first, last = isinstance(t, int) and t == 0, isinstance(t, int) and t == NT - 1
            pe.wait_ge(m_f, n + 1)
            pe.wait_ge(m_fp, n + 1)
            pe.wait_ge(v_in[slot], (k + (half * (NT // 2 + 1 - slot) + 1)) * 16 + V_BEFORE[slot])
            if first and half:
                pe.wait_ge(m_ma, 1)
            for h in range(4):
                v = V4[:, (slot * 4 + h) * HV:(slot * 4 + h + 1) * HV]
                at = slot * 4 * FC * P + h * FC * P
                pe.matmul(bank(3 + h, 512, 0, HV), v, F0[:, at:at + 512], start=first, stop=last)
                mm = pe.matmul(bank(7, 96, h * 96, HV), v, F0[:, at + 512:at + 608],
                               start=(first and h == 0), stop=last, skip_group_check=True)
            mm.then_inc(m_fu, 1)

        def m1A_end_pe(pe):
            pe.wait_ge(m_ma, 2)
            for c in range(FC):
                rows = min(P, FG * 32 - c * P)
                for h in range(8):
                    at = (h // 4) * HS + ((h % 4) * 512 + c * P if c < 4 else 2048 + (h % 4) * 96)
                    mm = pe.transpose(bank(c, HV, h * HV, rows), MFT[:, at:at + rows], ident[0:HV, 0:HV])
            mm.then_inc(m_tp, 1)

        POOL_R = 12

        def m1A_pool(e, t, half, slot, k):
            def wait(q, value):
                pool_wait(e, q, value)

            wait(m_k2, half * NT + t + 1)
            slot_free(e, t, half, k, wait=wait)
            features(e, F0[:, slot * 2560:(slot + 1) * 2560], K2[:, slot * 512:slot * 512 + 256], 4, range(POOL_R, R2), False)
            e.drain().then_inc(m_fp, 1)

        def m1A_dve(e, t, half, slot, k):
            n = half * NT + t
            first, last = isinstance(t, int) and t == 0, isinstance(t, int) and t == NT - 1
            if half and first:
                take_sums(e, 0)
            v4 = V4[:, slot * 4 * HV:(slot + 1) * 4 * HV]
            if first:
                e.memset(v3(v4, HV)[:, :, 0:1], 1.0)
            if last:
                e.wait_ge(v_in[slot], (k + (half * (NT // 2 + 1 - slot) + 1)) * 16 + V_BEFORE[slot])
                e.tensor_scalar(v4, v4, valid[:, NT - 1:NT], None, ALU.mult)
            k2 = K2[:, slot * 512:slot * 512 + 256]
            slot_free(e, t, half, k, q=m_fp)
            double_rows(e, RIA[:, bass.ds(t * 8 + half * 4, 4)], QA[:, bass.ds(t * C + half * P, P)], k2, 4)
            e.drain().then_inc(m_k2, 1)
            slot_free(e, t, half, k)
            features(e, F0[:, slot * 2560:(slot + 1) * 2560], k2, 4, range(POOL_R))
            e.drain().then_inc(m_f, 1)

        def take_sums(e, half):
            e.wait_ge(m_fu, (half + 1) * NT)
            e.tensor_copy(MFT[:, half * HS:(half + 1) * HS], ps[0:HV, 3 * 512:3 * 512 + HS])
            e.drain().then_inc(m_ma, 1)

        def factors_dve(e, bias, scale, round):
            e.wait_ge(m_in, 16 * round)
            if scale != 1.0:
                e.tensor_scalar(bias, bias, scale, None, ALU.mult)
                e.drain()
            for s in range(TURNS):
                q = QA[:, s * TI * C:(s + 1) * TI * C]
                e.scalar_tensor_tensor(v3(q, C), v3(q, C), scale, over_five(bias, C), ALU.mult, ALU.add)
                e.drain()
                norms_dve(e, v3(q, C), RNA[:, s * 8 * TI:(s + 1) * 8 * TI])
            e.drain().then_inc(m_sq, 1)
            e.wait_ge(m_rt, round)
            seq(e, lambda: e.tensor_scalar(RNA, RNA, 1e-12, None, ALU.max),
                lambda: e.reciprocal(RIA, RNA))

        def factors_act(e, round):
            e.wait_ge(m_sq, round)
            e.activation(RNA, RNA, ACT.Sqrt).then_inc(m_rt, 1)

        def sums_dve(e):
            e.wait_ge(m_tp, 2)
            for c in range(FC):
                rows = min(P, FG * 32 - c * P)
                e.tensor_scalar(MF[0:rows, c * 8 * HV:(c + 1) * 8 * HV], bank(c, 8 * HV, 0, rows),
                                coef[0:rows, c:c + 1], None, ALU.mult)
            e.drain()
            for c in range(FC):
                rows = min(P, FG * 32 - c * P)
                m = v3(MF[0:rows, c * 8 * HV:(c + 1) * 8 * HV], HV)
                part = v3(SQ[0:rows, 0:C], 32)
                seq(e, lambda: e.tensor_tensor(part, m[:, :, 0:1].to_broadcast([rows, 8, 32]), v3(bv[0:rows, :], 32), ALU.mult),
                    lambda: e.tensor_tensor(m[:, :, 1:HV], m[:, :, 1:HV], part, ALU.add))

        TB = (4, 5, 0)

        def steps(e, step):
            def has(n):
                return [0 <= n - i < NT for i in range(4)]
            for n in range(3):
                step(n, has(n))
            with e.Fori(3, NT) as n:
                step(n, [True] * 4)
            for n in range(NT, NT + 3):
                step(n, has(n))

        def m1B_pe(pe, n, has):
            if has[0]:
                pe.wait_ge(m_f, n + (2 * NT + 1))
                for i in range(10):
                    if i >= 3:
                        pe.wait_ge(m_ft, n * 10 + (i - 2))
                    b = TB[i % 3]
                    for q in range(4):
                        if i < 8:
                            at = i * FC * P + q * P
                            mm = pe.transpose(bank(b, P, q * P), F0[:, at:at + P], ident[:, :])
                        else:
                            at = ((i - 8) * 4 + q) * FC * P + 4 * P
                            mm = pe.transpose(bank(b, P, q * P, 96), F0[:, at:at + 96], ident[:, :])
                    mm.then_inc(m_fq, 1)
            if has[1]:
                pe.wait_ge(m_yt, n)
                pe.sem_inc(carried, 1)
                for h in range(8):
                    mm = pe.transpose(bank(2, HV, h * HV), YT[:, h * P:(h + 1) * P], ident[0:HV, 0:HV])
                mm.then_inc(m_z, 1)
            if has[2]:
                pe.wait_ge(m_ob, n - 1)
                for c in range(2):
                    mm = pe.transpose(bank(3, P, c * P), OB[:, c * P:(c + 1) * P], ident[:, :])
                mm.then_inc(m_xo, 1)
            if has[0]:
                pe.wait_ge(m_ft, n * 10 + 10)
                for h in range(8):
                    for c in range(FC):
                        rows = min(P, FG * 32 - c * P)
                        at = h * 512 + c * P if c < 4 else 4096 + h * P
                        mm = pe.matmul(bank(6 + h // 4, P, (h % 4) * P, HV),
                                       MF[0:rows, c * 8 * HV + h * HV:c * 8 * HV + (h + 1) * HV], F1[0:rows, at:at + P],
                                       start=(c == 0), stop=(c == FC - 1), skip_group_check=True)
                mm.then_inc(m_y1, 1)
            if has[2]:
                pe.wait_ge(m_xe, n - 1)
                if has[3]:
                    pe.wait_ge(m_xa, n - 2)
                for c in range(2):
                    mm = pe.matmul(bank(1, C), XO[:, c * P:(c + 1) * P], wprojT[:, c, :], start=(c == 0), stop=(c == 1))
                mm.then_inc(m_p, 1)

        def m1B_act(e, n, has):
            if has[1]:
                e.wait_ge(m_y1, n)
                if has[2]:
                    e.wait_ge(m_z, n - 1)
                e.activation(YT, ps[0:HV, 6 * 512:8 * 512], ACT.Copy).then_inc(m_yt, 1)
            if has[0]:
                for i in range(10):
                    e.wait_ge(m_fq, n * 10 + (i + 1))
                    if i < 8:
                        e.activation(F1[:, i * 512:(i + 1) * 512], bank(TB[i % 3]), ACT.Copy).then_inc(m_ft, 1)
                    else:
                        e.activation(F1[0:96, 4096 + (i - 8) * 512:4096 + (i - 7) * 512], bank(TB[i % 3], 512, 0, 96),
                                     ACT.Copy).then_inc(m_ft, 1)
            if has[2]:
                e.wait_ge(m_xo, n - 1)
                e.activation(XO, bank(3, C), ACT.Copy).then_inc(m_xe, 1)

        def m1B_dve(e, n, has):
            if has[0]:
                double_rows(e, RIA[:, bass.ds(n * 8, 8)], QA[:, bass.ds(n * C, C)], K2[:, 0:512], 8)
                if has[1]:
                    e.wait_ge(m_fq, n * 10)
                features(e, F0, K2[:, 0:512], 8, range(R2))
                e.drain().then_inc(m_f, 1)
            if has[1]:
                e.wait_ge(m_z, n)
                y = v3(bank(2, 8 * HV), HV)
                e.reciprocal(RN[:, 0:8].rearrange("p (h o) -> p h o", o=1), y[:, :, 0:1])
                e.drain()
                if has[2]:
                    e.wait_ge(m_xo, n - 1)
                r = RN[:, 0:8].rearrange("p (h o) -> p h o", o=1).to_broadcast([P, 8, 32])
                e.tensor_tensor(v3(OB, 32), y[:, :, 1:HV], r, ALU.mult)
                e.drain().then_inc(m_ob, 1)
            if has[3]:
                e.wait_ge(m_p, n - 2)
                x = X[:, bass.ds((n - 3) * C, C)]
                e.tensor_tensor(x, bank(1, C), x, ALU.add)
                e.drain().then_inc(m_xa, 1)

        LG = BUF[:, 8192:8192 + NT * 8]
        GR = BUF[:, 8448:8448 + NT * 8]
        GM = BUF[:, 8704:8704 + NT * 8]
        GSEL = BUF[:, 8960:8960 + NT * 8]
        gbrow = ROWS[:, 2000:2008]
        

        def gates1_dve(e):
            col, col2 = sd[:, :], rs[:, :]
            lg = v3(LG, 8)
            seq(e, lambda: e.tensor_tensor(lg, lg, over_tiles(gbrow, 8), ALU.add),
                lambda: e.tensor_reduce(col, lg, AX.X, ALU.max),
                lambda: e.tensor_tensor(lg, lg, bc(col, 8), ALU.subtract))
            e.drain().then_inc(sc_e, 1)
            e.wait_ge(sc_ex, 3)
            seq(e, lambda: e.tensor_reduce(col, lg, AX.X, ALU.add),
                lambda: e.reciprocal(col2, col),
                lambda: e.tensor_tensor(lg, lg, bc(col2, 8), ALU.mult))
            top_two(e, LG, EXP1, GR, GM, GSEL)
            e.tensor_tensor(gates[:, :], LG, GSEL, ALU.mult)

        UC = 3
        PAIRS = -(-(-(-(2 * N + EXP1 * (P - 1)) // P)) // UC) * UC
        TRASH = (PAIRS + 1) * P
        PLACES = TRASH + 2 * P
        xs_d = dram("xs_d", [PLACES, C])
        ys_d = dram("ys_d", [PLACES, C])
        w1x, w2x = WT[:, 0:EXP1 * 1024], WT[:, EXP1 * 1024:EXP1 * 2048]
        B1X = BUF[:, 0:EXP1 * HID]
        B2X = BUF[:, 4096:4096 + EXP1 * C]
        XC = BUF[:, 6144:6144 + UC * C]
        HX = BUF[:, 6912:6912 + UC * HID]
        HXT = BUF[:, 8448:8448 + UC * HID]
        YX = BUF[:, 9984:9984 + UC * C]
        YG = BUF[:, 0:TI * 2 * C]
        PSEL = BUF[:, 9216:9216 + NT * 8]
        PTOT = BUF[:, 9420:9420 + NT * 8]
        PSCN = BUF[:, 9624:9624 + NT * 8]
        PPOS = BUF[:, 9828:9828 + NT * 8]
        PL = [WS[:, 0:NT], WS[:, 32:32 + NT]]
        PLI = [WS[:, 64:64 + NT].bitcast(I32), WS[:, 96:96 + NT].bitcast(I32)]
        PG = [WS[:, 128:128 + NT], WS[:, 160:160 + NT]]
        PINV = WS[:, 192:192 + NT]
        PLANE = [WS[:, 224:225], WS[:, 225:226]]
        PCH, PCHI, PEND = WS[:, 232:240], WS[:, 240:248].bitcast(I32), WS[:, 248:256]
        PTMP = WS[0:1, 256:320]
        expert_of = tile_gat[0:1, 0:64]
        assert PAIRS + UC < 64
        (px_sel, px_mm, px_ok, px_scat, fx_tp, fx_xt, fx_h, fx_hb, fx_g, fx_t2, fx_ht, fx_o, fx_y, ys_out, ys_free,
         yg_used) = (sem("x_" + x) for x in (
             "sel", "mm", "ok", "scat", "tp", "xt", "h", "hb", "g", "t2", "ht", "o", "y", "out", "free", "used"))
        xc_in = [sem(f"xc_in{i}") for i in range(UC)]
        yg_rows = [sem(f"yg_rows{i}") for i in range(TI)]
        x_zero = sem("x_zero")
        XZ = 1536
        x_zeros = -(-(PLACES // P * C) // XZ) + 1

        def places_pe(pe):
            pe.wait_ge(px_sel, 1)
            pe.matmul(bank(7, NT * 8), upper[:, :], PSEL, start=True, stop=True)
            pe.matmul(bank(6, NT * 8), ones[:, :], PSEL, start=True, stop=True)
            pe.matmul(bank(5, 1), upper[:, :], ones[:, 0:1], start=True, stop=True).then_inc(px_mm, 1)

        def places_dve(e):
            sel, tot, scn, pos = v3(PSEL, 8), v3(PTOT, 8), v3(PSCN, 8), v3(PPOS, 8)
            e.tensor_tensor(sel, v3(GSEL, 8), bc(valid[:, :], 8), ALU.mult)
            e.drain().then_inc(px_sel, 1)
            e.wait_ge(px_mm, 1)
            for i in range(2):
                e.tensor_scalar(PLANE[i], bank(5, 1), float(TRASH + i * P), None, ALU.add)
            e.tensor_copy(PTOT, bank(6, NT * 8))
            e.drain()
            for x in range(EXP1):
                e.tensor_tensor_scan(scn[:, :, x], tot[:, :, x], tot[:, :, x], 0.0, ALU.add, ALU.max)
            e.drain()
            seq(e, lambda: e.tensor_scalar(PCH, scn[:, NT - 1, :], float(P - 1), None, ALU.add),
                lambda: e.tensor_copy(PCHI, PCH),
                lambda: e.tensor_scalar(PCHI, PCHI, 7, None, ALU.arith_shift_right),
                lambda: e.tensor_copy(PCH, PCHI),
                lambda: e.tensor_tensor_scan(PEND, PCH, PCH, 0.0, ALU.add, ALU.max),
                lambda: e.tensor_tensor(PCH, PEND, PCH, ALU.subtract),
                lambda: e.tensor_scalar(PCH, PCH, float(P), 1.0, ALU.mult, ALU.add),
                lambda: e.tensor_tensor(pos, scn, tot, ALU.subtract),
                lambda: e.tensor_tensor(PPOS, PPOS, bank(7, NT * 8), ALU.add),
                lambda: e.tensor_tensor(pos, pos, PCH.rearrange("p (o x) -> p o x", o=1).to_broadcast([P, NT, 8]), ALU.add),
                lambda: e.tensor_tensor(PPOS, PPOS, PSEL, ALU.mult),
                lambda: e.tensor_reduce(PL[1], pos, AX.X, ALU.max),
                lambda: e.tensor_reduce(PL[0], pos, AX.X, ALU.add),
                lambda: e.tensor_tensor(PL[0], PL[0], PL[1], ALU.subtract))
            for i, tmp in enumerate((PTOT, PSCN)):
                seq(e, lambda: e.tensor_scalar(PINV, valid[:, :], 0.0, PLANE[i], ALU.is_equal, ALU.mult),
                    lambda: e.tensor_tensor(v3(tmp, 8), pos, bc(PL[i], 8), ALU.is_equal),
                    lambda: e.tensor_tensor(tmp, tmp, gates[:, :], ALU.mult),
                    lambda: e.tensor_reduce(PG[i], v3(tmp, 8), AX.X, ALU.add),
                    lambda: e.scalar_tensor_tensor(PL[i], PL[i], -1.0, PINV, ALU.add, ALU.max),
                    lambda: e.tensor_copy(PLI[i], PL[i]))
            e.drain().then_inc(px_ok, 1)
            e.memset(PTMP, 0.0)
            e.drain()
            for x in range(EXP1 - 1):
                e.scalar_tensor_tensor(PTMP, iota_row[0:1, 0:64], PEND[0:1, x:x + 1], PTMP, ALU.is_ge, ALU.add)
                e.drain()
            e.tensor_copy(expert_of[0:1, :], PTMP)
            e.drain()

        def experts(engine, k):
            return nc.values_load_multi_w_load_instructions(
                expert_of[0:1, bass.ds(k * UC, UC + 1)], [engine], min_val=0, max_val=EXP1 - 1,
                skip_runtime_bounds_check_because="a count of seven comparisons")[1]

        def scatter_pool(e):
            pool_wait(e, px_ok, 1)
            pool_wait(e, x_zero, 16 * x_zeros)
            for t in range(NT):
                for i in range(2):
                    e.indirect_dma_start(xs_d, bass.IndirectOffsetOnAxis(ap=PLI[i][:, t:t + 1], axis=0),
                                         ACC[:, t * 257:t * 257 + C], None).then_inc(px_scat, 16)

        def chunk_rows(table, c):
            return table[bass.ds(c * P, P), :]

        def loads_sp(sp):
            sp.wait_ge(px_scat, 16 * 2 * NT)
            for i in range(UC):
                sp.dma_start(XC[:, i * C:(i + 1) * C], xs_d[i * P:(i + 1) * P, :]).then_inc(xc_in[i], 16)
            with sp.Fori(1, PAIRS // UC) as k:
                for i in range(UC):
                    sp.wait_ge(fx_tp, k * UC + (i + 1 - UC))
                    sp.dma_start(XC[:, i * C:(i + 1) * C], chunk_rows(xs_d, k * UC + i)).then_inc(xc_in[i], 16)
            sp.wait_ge(fx_tp, PAIRS + 1 - UC)
            sp.dma_start(XC[:, 0:C], xs_d[PAIRS * P:(PAIRS + 1) * P, :]).then_inc(xc_in[0], 16)

        def chunk_in(pe, c, slot, turn):
            pe.wait_ge(xc_in[slot], turn * 16 + 16)
            for h in range(2):
                mm = pe.transpose(bank(0, P, h * P), XC[:, slot * C + h * P:slot * C + (h + 1) * P], ident[:, :])
            mm.then_inc(fx_tp, 1)

        def chunk_hidden(pe, c, slot, x):
            pe.wait_ge(fx_xt, c + 1)
            pe.wait_ge(fx_hb, c + 1)
            for h in range(2):
                mm = pe.matmul(bank(1 + slot, HID), XT[:, slot * C + h * P:slot * C + (h + 1) * P],
                               w1x[:, bass.ds(x * 1024 + h * HID, HID)], start=(h == 0), stop=(h == 1))
            mm.then_inc(fx_h, 1)

        def ffn1_pe(pe):
            chunk_in(pe, 0, 0, 0)
            chunk_hidden(pe, 0, 0, experts(mybir.EngineType.PE, 0)[0])
            with pe.Fori(0, PAIRS // UC) as k:
                x = experts(mybir.EngineType.PE, k)
                for i in range(UC):
                    c, nxt = k * UC + i, (i + 1) % UC
                    chunk_in(pe, c + 1, nxt, k + (i + 1) // UC)
                    pe.wait_ge(fx_g, c + 1)
                    for h in range(4):
                        mm = pe.transpose(bank(4, P, h * P), HX[:, i * HID + h * P:i * HID + (h + 1) * P], ident[:, :])
                    mm.then_inc(fx_t2, 1)
                    chunk_hidden(pe, c + 1, nxt, x[i + 1])
                    pe.wait_ge(fx_ht, c + 1)
                    pe.wait_ge(fx_y, c + 1)
                    for h in range(4):
                        mm = pe.matmul(bank(5 + i, C), HXT[:, i * HID + h * P:i * HID + (h + 1) * P],
                                       w2x[:, bass.ds(x[i] * 1024 + h * C, C)], start=(h == 0), stop=(h == 3))
                    mm.then_inc(fx_o, 1)

        def ffn1_act(e):
            def rows(c, slot):
                e.wait_ge(fx_tp, c + 1)
                e.activation(XT[:, slot * C:(slot + 1) * C], bank(0, C), ACT.Copy).then_inc(fx_xt, 1)

            def gelu(c, slot):
                e.wait_ge(fx_hb, c + (1 + UC))
                e.activation(HX[:, slot * HID:(slot + 1) * HID], HX[:, slot * HID:(slot + 1) * HID], ACT.Gelu
                             ).then_inc(fx_g, 1)

            rows(0, 0)
            gelu(0, 0)
            with e.Fori(0, PAIRS // UC) as k:
                for i in range(UC):
                    c, nxt = k * UC + i, (i + 1) % UC
                    rows(c + 1, nxt)
                    e.wait_ge(fx_t2, c + 1)
                    e.activation(HXT[:, i * HID:(i + 1) * HID], bank(4), ACT.Copy).then_inc(fx_ht, 1)
                    gelu(c + 1, nxt)

        def ffn1_dve(e):
            def bias(c, slot, x):
                e.wait_ge(fx_h, c + 1)
                e.tensor_tensor(HX[:, slot * HID:(slot + 1) * HID], bank(1 + slot, HID), B1X[:, bass.ds(x * HID, HID)],
                                ALU.add).then_inc(fx_hb, 1)

            e.wait_ge(w_ffn, 96)
            bias(0, 0, experts(mybir.EngineType.DVE, 0)[0])
            with e.Fori(0, PAIRS // UC) as k:
                x = experts(mybir.EngineType.DVE, k)
                for i in range(UC):
                    c, nxt = k * UC + i, (i + 1) % UC
                    bias(c + 1, nxt, x[i + 1])
                    if i == 0:
                        e.wait_ge(ys_free, k + 1)
                    e.wait_ge(fx_o, c + 1)
                    e.tensor_tensor(YX[:, i * C:(i + 1) * C], bank(5 + i, C), B2X[:, bass.ds(x[i] * C, C)], ALU.add
                                    ).then_inc(fx_y, 1)

        def ffn1_pool(e):
            with e.Fori(0, PAIRS // UC) as k:
                for i in range(UC):
                    pool_wait(e, fx_y, k * UC + (i + 1 + UC))
                    e.dma_start(chunk_rows(ys_d, k * UC + i), YX[:, i * C:(i + 1) * C]).then_inc(ys_out, 16)
                pool_wait(e, ys_out, k * (16 * UC) + 16 * UC)
                e.sem_inc(ys_free, 1)

        def gather_pool(e):
            for t in range(NT):
                if t == 0:
                    pool_wait(e, yg_used, TI)
                if t >= TI:
                    pool_wait(e, yg_used, t + 1)
                for i in range(2):
                    at = (t % TI * 2 + i) * C
                    e.indirect_dma_start(YG[:, at:at + C], None, ys_d,
                                         bass.IndirectOffsetOnAxis(ap=PLI[i][:, t:t + 1], axis=0)
                                         ).then_inc(yg_rows[t % TI], 16)

        def combine_dve(e, s):
            for j in range(TI):
                x = X[:, bass.ds((s * TI + j) * C, C)]
                e.wait_ge(yg_rows[j], s * 32 + 32)
                for i in range(2):
                    e.scalar_tensor_tensor(x, YG[:, (j * 2 + i) * C:(j * 2 + i + 1) * C], PG[i][:, bass.ds(s * TI + j, 1)],
                                           x, ALU.mult, ALU.add)
                    e.drain()
                e.sem_inc(yg_used, 1)

        block = ctx.enter_context(nc.Block())
        out_done = sem("out_done")
        dve_ready = sem("dve_ready")
        hop_done, cur_out = sem("hop_done"), sem("cur_out")
        hop_init = sem("hop_init")

        def broadcast_row(ap, n):
            return ap.rearrange(
                "(o n) -> o n", o=1).to_broadcast([P, n])

        @block.sync
        def _(sp):
            full = (NT - 1) * P
            sp.wait_ge(consts_ok, 1)
            sort_loads(sp, main, a["src"], a["dst"], a["edge_weight"])
            sp.dma_start(v3(X[:, 0:(NT - 1) * C], C), a["x"][0:full, :].rearrange("(t p) c -> p t c", p=P)
                         ).then_inc(x_in, 16)
            sp.dma_start(X[0:LAST, (NT - 1) * C:NT * C], a["x"][full:N, :]).then_inc(x_in, 16)
            for s in (main, gat):
                sp.dma_start(s.rec_d.rearrange("(p c) f -> p (c f)", p=P), zeros[:, 0:(s.chunks + PADROWS) * 4]
                             ).then_inc(s.cleared, 16)
            xz = xs_d.rearrange("(p r) c -> p (r c)", p=P)
            for i in range(x_zeros - 1):
                n = min(XZ, xz.shape[1] - i * XZ)
                sp.dma_start(xz[:, i * XZ:i * XZ + n], zeros[:, 0:n].bitcast(F32)).then_inc(x_zero, 16)
            sp.dma_start(ys_d[PAIRS * P:PLACES, :].rearrange("(p r) c -> p (r c)", p=P), zeros[:, 0:3 * C].bitcast(F32)
                         ).then_inc(x_zero, 16)
            for dst, src in ((wk_wv[:, :, 0:C], a["L0_mix_Wk"]), (wk_wv[:, :, C:2 * C], a["L0_mix_Wv"]),
                             (wq0, a["L0_mix_Wq"]), (wm0, a["L0_mix_Wm"]), (w1m, a["L0_mix_W1"]),
                             (w2m, a["L0_mix_W2"]), (wg0, a["L0_gnn_weight"])):
                sp.dma_start(dst, src.rearrange("(k p) n -> p k n", p=P)).then_inc(w_in0, 16)
            for dst, src in ((g1r, "L0_mix_g1"), (b1r, "L0_mix_b1"), (g2r, "L0_mix_g2"), (b2r, "L0_mix_b2")):
                sp.dma_start(dst, broadcast_row(a[src], C)).then_inc(w_in0, 16)
            sp.sem_inc(Hop.mm, GROUP)
            sp.sem_inc(Hop.add, HB)
            sp.sem_inc(gat_mm, GROUP)
            sp.sem_inc(gat_add, HB)
            sp.sem_inc(gat_at, 1)
            sp.sem_inc(gat_tp, 1)
            sp.sem_inc(gat_e, 2)
            sp.sem_inc(fx_hb, UC)
            sp.sem_inc(fx_y, UC)
            sp.sem_inc(ys_free, 1)
            sp.sem_inc(qkv_ev, 1)
            sp.sem_inc(qkv_st, 16)
            sp.sem_inc(moe_ya, 1)
            sp.sem_inc(moe_out, 16)
            sp.sem_inc(gat_kept, 2)
            sp.wait_ge(main.pos_ok, 1)
            sp.wait_ge(sort_free, 1)
            sort_loads(sp, gat, a["L0_ffn_edge_index"][0, :], a["L0_ffn_edge_index"][1, :], None)
            sp.wait_ge(norms[0].xn_ok, norms[0].n)
            acc_to_dram(sp, xn_d[0], norms[0].out)
            sp.wait_ge(norms[0].out, norms[0].written)
            sp.wait_ge(x_zero, 16 * x_zeros)
            front_sp(sp, fronts["fa"], xn_d[0])
            sp.wait_ge(Front.xt_tp, NT)
            front_sp(sp, fronts["fb"], xn_d[0], [(xb_ok, 1)])
            sorted_back(sp, main)
            for ap, n in ((a["L0_ffn_att_src"].rearrange("h e -> (h e)"), 0),
                          (a["L0_ffn_att_dst"].rearrange("h e -> (h e)"), 16), (a["L0_ffn_b_gat"], 32),
                          (a["L0_ffn_ln_gamma"], 48), (a["L0_ffn_ln_beta"], 64)):
                sp.dma_start(attrow[:, n:n + 16], broadcast_row(ap, 16)).then_inc(rows_ffn, 16)
            sp.dma_start(wgat, a["L0_ffn_W_gat"].rearrange("(k p) n -> p k n", p=P)).then_inc(rows_ffn, 16)
            sp.dma_start(wgate, a["L1_ffn_gate_w"].rearrange("(k p) n -> p k n", p=P)).then_inc(rows_ffn, 16)
            sp.dma_start(gbrow, broadcast_row(a["L1_ffn_gate_b"], 8)).then_inc(rows_ffn, 16)
            sp.dma_start(B1T[:, 0:16], a["L0_ffn_b1"].rearrange("e (m p) -> p (e m)", p=P), allow_slow_non_contiguous=True).then_inc(rows_ffn, 16)
            sp.dma_start(B2R[0:EXP0, :], a["L0_ffn_b2"]).then_inc(rows_ffn, 16)
            sp.wait_ge(round_pe, R["lnb"] + 1)
            sp.dma_start(w1e, a["L0_ffn_W1"].rearrange("e (k p) n -> p e k n", p=P)).then_inc(w_ffn, 16)
            sp.dma_start(w2e, a["L0_ffn_W2"].rearrange("e (k p) n -> p e k n", p=P)).then_inc(w_ffn, 16)
            sp.wait_ge(norms[1].xn_ok, norms[1].n)
            acc_to_dram(sp, xn_d[1], norms[1].out)
            sorted_back(sp, gat)
            sp.wait_ge(src_ready, 1)
            sp.dma_start(src_tab_d.rearrange("(t p) c -> p t c", p=P), v3(STB, 32)).then_inc(src_out, 16)
            sp.wait_ge(norms[1].out, norms[1].written)
            dense_load(sp, 0)
            with sp.Fori(1, DA) as n:
                dense_load(sp, n)
                dense_store(sp, n - 1)
            sp.wait_ge(dst_ready, 1)
            sp.dma_start(dst_tab_d.rearrange("(t p) c -> p t c", p=P), v3(DTT, 8)).then_inc(dst_out, 16)
            with sp.Fori(DA, NT) as n:
                dense_load(sp, n)
                dense_store(sp, n - 1)
            dense_store(sp, NT - 1)
            sp.wait_ge(moe_out, 16 * NT + 16)
            sp.wait_ge(round_dve, R["gatB"] + 1)
            for s in range(TURNS):
                if s >= 2:
                    sp.wait_ge(moe_used, s - 1)
                turn_results(sp, s, s % 2)
            sp.wait_ge(round_pe, R["lnc"] + 1)
            sp.dma_start(wsh, a["L1_gnn_shared_weight"].rearrange("(k p) n -> p k n", p=P)).then_inc(w_in1, 16)
            sp.dma_start(wqkv, a["L1_mix_Wqkv"].rearrange("(k p) n -> p k n", p=P)).then_inc(w_in1, 16)
            sp.dma_start(wproj, a["L1_mix_Wproj"].rearrange("(k p) n -> p k n", p=P)).then_inc(w_in1, 16)
            sp.dma_start(ROWS[:, 0:768], broadcast_row(a["L1_mix_bqkv"], 768)).then_inc(rows_in1, 16)
            sp.dma_start(bproj, broadcast_row(a["L1_mix_bproj"], C)).then_inc(rows_in1, 16)
            sp.dma_start(obias, broadcast_row(a["L1_gnn_output_bias"], C)).then_inc(rows_in1, 16)
            sp.dma_start(temp, broadcast_row(a["L1_mix_temperature"].rearrange("a h b c -> (a h b c)"), 8)
                         ).then_inc(rows_in1, 16)
            sp.wait_ge(norms[2].xn_ok, norms[2].n)
            acc_to_dram(sp, xn_d[2], norms[2].out)
            sp.wait_ge(norms[2].out, norms[2].written)
            for i in range(3):
                if i:
                    sp.wait_ge(cur_out, 16 * i)
                tile_loads(sp, i, ([xn_d[2]] + cur_d)[i])
                sp.wait_ge(hop_done, i + 1)
                acc_to_dram(sp, cur_d[i], cur_out)
            sp.wait_ge(cur_out, 48)
            sp.wait_ge(Front.xt_tp, fronts["f3"].before * TI)
            front_sp(sp, fronts["f3"], cur_d[2])
            m1_loads(sp)
            sp.wait_ge(round_pe, R["lnd"] + 1)
            sp.dma_start(w1x.rearrange("p (e k n) -> p e k n", e=EXP1, k=2),
                         a["L1_ffn_W1"].rearrange("e (k p) n -> p e k n", p=P)).then_inc(w_ffn, 16)
            sp.dma_start(w2x.rearrange("p (e k n) -> p e k n", e=EXP1, k=4),
                         a["L1_ffn_W2"].rearrange("e (k p) n -> p e k n", p=P)).then_inc(w_ffn, 16)
            sp.dma_start(B1X, broadcast_row(a["L1_ffn_b1"].rearrange("e n -> (e n)"), EXP1 * HID)).then_inc(w_ffn, 16)
            sp.dma_start(B2X, broadcast_row(a["L1_ffn_b2"].rearrange("e n -> (e n)"), EXP1 * C)).then_inc(w_ffn, 16)
            loads_sp(sp)
            sp.wait_ge(round_dve, R["ffn1_end"] + 1)
            sp.dma_start(out[0:full, :].rearrange("(t p) c -> p t c", p=P), v3(X[:, 0:(NT - 1) * C], C)
                         ).then_inc(out_done, 16)
            sp.dma_start(out[full:N, :], X[0:LAST, (NT - 1) * C:NT * C]).then_inc(out_done, 16)
            sp.wait_ge(out_done, 32)

        @block.gpsimd
        def _(e):
            e.memset(s_src, 0)
            e.memset(s_dst, NP)
            e.memset(s_w, 0.0)
            e.memset(X[:, (NT - 1) * C:NT * C], 0.0)
            e.memset(zeros, 0)
            e.drain().then_inc(consts_ok, 1)
            e.memset(ones[:, :], 1.0)
            e.memset(eps_ln[:, :], LN_EPS)
            e.memset(valid[:, :], 1.0)
            e.iota(iota_row[:, :], [[1, P]], base=0, channel_multiplier=0, allow_small_or_imprecise_dtypes=True)
            e.iota(s_iota, [[1, CH_MAIN]], base=0, channel_multiplier=0, allow_small_or_imprecise_dtypes=True)
            e.drain()
            e.affine_select(out=ident[:, :], in_=ones[:, :], compare_op=ALU.is_equal, fill=0.0, base=0,
                            pattern=[[1, P]], channel_multiplier=-1)
            e.affine_select(out=upper[:, :], in_=ones[:, :], compare_op=ALU.is_gt, fill=0.0, base=0,
                            pattern=[[1, P]], channel_multiplier=-1)
            e.affine_select(out=v3(head_mask[:, :], 32), in_=v3(ones[:, :], 32), compare_op=ALU.is_ge, fill=0.0,
                            base=0, pattern=[[-32, 4], [0, 32]], channel_multiplier=1)
            e.affine_select(out=valid[:, NT - 1:NT], in_=ones[:, 0:1], compare_op=ALU.is_gt, fill=0.0, base=LAST,
                            pattern=[[0, 1]], channel_multiplier=-1)
            e.drain()
            e.affine_select(out=v3(head_mask[:, :], 32), in_=v3(head_mask[:, :], 32), compare_op=ALU.is_ge, fill=0.0,
                            base=31, pattern=[[32, 4], [0, 32]], channel_multiplier=-1)
            for b in range(4):
                e.tensor_scalar(ident_b[:, b * P:(b + 1) * P], ident[:, :], -BIG, None, ALU.mult)
            e.drain().then_inc(consts_ok, 1)
            sort_pool(e, main, 0, main.turns)
            sort_pool(e, gat, 0, GAT_EARLY)
            pool_wait(e, hop_init, 1)
            hop_pool(e, hops[0])
            sort_pool(e, gat, GAT_EARLY, gat.turns)
            pool_wait(e, src_out, 16)
            pool_wait(e, dve_ready, 1)
            gat_pool(e, False)
            pool_wait(e, dst_out, 16)
            gat_pool(e, True)
            for i in range(3):
                if i == 0:
                    pool_wait(e, hop_init, 2)
                    pool_wait(e, norms[2].out, norms[2].written)
                else:
                    pool_wait(e, cur_out, 16 * i)
                hop_pool(e, hops[i + 1])
            pairs(e, lambda *step: m1A_pool(e, *step))
            scatter_pool(e)
            ffn1_pool(e)
            gather_pool(e)

        @block.tensor
        def _(pe):
            sort_pe(pe, main)
            sort_pe(pe, gat)
            pe.wait_ge(w_in0, 16 * 11)
            with pe.Fori(0, TURNS) as s:
                mixA_pe(pe, s)
                rendezvous(pe, "pe", s + (R["mixA"] + 1))
            rendezvous(pe, "pe", R["mixA_end"] + 1)
            with pe.Fori(0, TURNS) as s:
                mixB_pe(pe, s)
                rendezvous(pe, "pe", s + (R["mixB"] + 1))
            hop_pe(pe, hops[0])
            rendezvous(pe, "pe", R["hop0"] + 1)
            with pe.Fori(0, TURNS) as s:
                gnn0_pe(pe, s)
                rendezvous(pe, "pe", s + (R["gnn0"] + 1))
            rendezvous(pe, "pe", R["lnb"] + 1)
            pe.wait_ge(rows_ffn, 160)
            with pe.Fori(0, TURNS) as s:
                narrow_pe(pe, fronts["fp"], s, wgat, 16, gp_mm)
                rendezvous(pe, "pe", s + (R["gatp"] + 1))
            rendezvous(pe, "pe", R["gatp_end"] + 1)
            pe.wait_ge(w_ffn, 32)
            gatA_pe(pe, 0, DA, True)
            gatA_pe(pe, DA, GTURNS, False)
            rendezvous(pe, "pe", R["gatA"] + 1)
            gatB_pe(pe)
            rendezvous(pe, "pe", R["gatB"] + 1)
            for s in range(TURNS):
                mix_pe(pe, s)
                rendezvous(pe, "pe", s + (R["ffn0"] + 1))
            rendezvous(pe, "pe", R["lnc"] + 1)
            weights_pe(pe)
            rendezvous(pe, "pe", R["m1w"] + 1)
            for i in range(3):
                hop_pe(pe, hops[i + 1], 0, NT, i)
                hop_pe(pe, hops[i + 1], NT)
                rendezvous(pe, "pe", R[f"hop{i + 1}"] + 1)
            with pe.Fori(0, TURNS) as s:
                gnn1_pe(pe, 3, s)
                rendezvous(pe, "pe", s + (R["gnn1"] + 1))
            pairs(pe, lambda *step: m1A_pe(pe, *step))
            m1A_end_pe(pe)
            rendezvous(pe, "pe", R["m1A"] + 1)
            steps(pe, lambda n, has: m1B_pe(pe, n, has))
            rendezvous(pe, "pe", R["m1B"] + 1)
            rendezvous(pe, "pe", R["lnd"] + 1)
            with pe.Fori(0, TURNS) as s:
                narrow_pe(pe, fronts["fq"], s, wgate, 8, gp_mm)
                rendezvous(pe, "pe", s + (R["gate1"] + 1))
            places_pe(pe)
            rendezvous(pe, "pe", R["gate1_end"] + 1)
            pe.wait_ge(w_ffn, 96)
            ffn1_pe(pe)
            rendezvous(pe, "pe", R["ffn1"] + 1)
            rendezvous(pe, "pe", R["ffn1_end"] + 1)

        @block.scalar
        def _(e):
            e.wait_ge(consts_ok, 2)
            norm_act(e, norms[0])
            with e.Fori(0, TURNS) as s:
                mixA_act(e, s)
                rendezvous(e, "act", s + (R["mixA"] + 1))
            rendezvous(e, "act", R["mixA_end"] + 1)
            with e.Fori(0, TURNS) as s:
                mixB_act(e, s)
                rendezvous(e, "act", s + (R["mixB"] + 1))
            hop_act(e, hops[0])
            e.wait_ge(deg_ok, 1)
            e.activation(sd[:, :], DEG, ACT.Sqrt).then_inc(dsd_ok, 1)
            rendezvous(e, "act", R["hop0"] + 1)
            with e.Fori(0, TURNS) as s:
                front_act(e, fronts["fg"], s)
                rendezvous(e, "act", s + (R["gnn0"] + 1))
            rendezvous(e, "act", R["lnb"] + 1)
            norm_act(e, norms[1])
            with e.Fori(0, TURNS) as s:
                front_act(e, fronts["fp"], s)
                rendezvous(e, "act", s + (R["gatp"] + 1))
            rendezvous(e, "act", R["gatp_end"] + 1)
            e.wait_ge(rows_ffn, 160)
            gatA_act(e, 0, DA, True)
            gatA_act(e, DA, GTURNS, False)
            rendezvous(e, "act", R["gatA"] + 1)
            e.wait_ge(sc_e, 1)
            e.activation(ES, ES, ACT.Exp).then_inc(sc_ex, 1)
            gatB_act(e)
            rendezvous(e, "act", R["gatB"] + 1)
            e.wait_ge(sc_var, 1)
            e.activation(rs[:, :], sd[:, :], ACT.Sqrt).then_inc(sc_sd, 1)
            e.wait_ge(sc_e, 2)
            e.activation(gates[:, 0:NT * EXP0], gates[:, 0:NT * EXP0], ACT.Exp).then_inc(sc_ex, 1)
            for s in range(TURNS):
                mix_act(e, s)
                rendezvous(e, "act", s + (R["ffn0"] + 1))
            rendezvous(e, "act", R["lnc"] + 1)
            norm_act(e, norms[2])
            weights_act(e)
            rendezvous(e, "act", R["m1w"] + 1)
            for i in range(3):
                hop_act(e, hops[i + 1], 0, NT, i)
                hop_act(e, hops[i + 1], NT)
                rendezvous(e, "act", R[f"hop{i + 1}"] + 1)
            with e.Fori(0, TURNS) as s:
                front_act(e, fronts["f3"], s)
                rendezvous(e, "act", s + (R["gnn1"] + 1))
            factors_act(e, 1)
            factors_act(e, 2)
            rendezvous(e, "act", R["m1A"] + 1)
            steps(e, lambda n, has: m1B_act(e, n, has))
            rendezvous(e, "act", R["m1B"] + 1)
            rendezvous(e, "act", R["lnd"] + 1)
            norm_act(e, norms[3])
            with e.Fori(0, TURNS) as s:
                front_act(e, fronts["fq"], s)
                rendezvous(e, "act", s + (R["gate1"] + 1))
            e.wait_ge(sc_e, 3)
            e.activation(LG, LG, ACT.Exp).then_inc(sc_ex, 1)
            rendezvous(e, "act", R["gate1_end"] + 1)
            ffn1_act(e)
            rendezvous(e, "act", R["ffn1"] + 1)
            rendezvous(e, "act", R["ffn1_end"] + 1)

        @block.vector
        def _(e):
            e.wait_ge(consts_ok, 2)
            sort_dve(e, main, n_main, True)
            e.drain().then_inc(sort_free, 1)
            e.wait_ge(x_in, 32)
            norm_dve(e, norms[0])
            sort_dve(e, gat, n_gat, False)
            e.memset(KVA, 0.0)
            e.drain()
            with e.Fori(0, TURNS) as s:
                mixA_dve(e, s)
                rendezvous(e, "dve", s + (R["mixA"] + 1))
            for h in range(2):
                e.tensor_tensor(KVB[:, h * P:(h + 1) * P], KVA[:, h * 129:h * 129 + P], head_mask[:, :], ALU.mult)
                e.tensor_scalar(ZB[:, h * P:(h + 1) * P], head_mask[:, :], KVA[:, h * 129 + P:h * 129 + P + 1], None,
                                ALU.mult)
            rendezvous(e, "dve", R["mixA_end"] + 1)
            with e.Fori(0, TURNS) as s:
                mixB_dve(e, s)
                rendezvous(e, "dve", s + (R["mixB"] + 1))
            e.memset(v3(ACC[:, :], 257)[:, :, C:C + 1], 0.0)
            e.memset(v3(G, 257)[:, :, C:C + 1], 1.0)
            e.wait_ge(main.back, 16)
            e.drain().then_inc(hop_init, 1)
            hop_dve(e, hops[0])
            e.tensor_scalar(DEG, v3(ACC[:, :], 257)[:, :, C], 1.0, None, ALU.max)
            e.drain().then_inc(deg_ok, 1)
            e.wait_ge(dsd_ok, 1)
            e.reciprocal(DEG, sd[:, :])
            rendezvous(e, "dve", R["hop0"] + 1)
            with e.Fori(0, TURNS) as s:
                gnn0_dve(e, s)
                rendezvous(e, "dve", s + (R["gnn0"] + 1))
            rendezvous(e, "dve", R["lnb"] + 1)
            norm_dve(e, norms[1])
            e.wait_ge(rows_ffn, 160)
            with e.Fori(0, TURNS) as s:
                narrow_dve(e, s, SRT, 20, 16, gp_mm)
                rendezvous(e, "dve", s + (R["gatp"] + 1))
            gat_tables_dve(e)
            e.drain().then_inc(dve_ready, 1)
            rendezvous(e, "dve", R["gatp_end"] + 1)
            gatA_dve(e)
            rendezvous(e, "dve", R["gatA"] + 1)
            gat_max_dve(e)
            gatB_dve(e)
            rendezvous(e, "dve", R["gatB"] + 1)
            gat_scores_dve(e)
            for s in range(TURNS):
                mix_dve(e, s)
                rendezvous(e, "dve", s + (R["ffn0"] + 1))
            rendezvous(e, "dve", R["lnc"] + 1)
            e.sem_inc(hop_init, 1)
            norm_dve(e, norms[2])
            rendezvous(e, "dve", R["m1w"] + 1)
            x3 = v3(X[:, :], C)
            e.wait_ge(rows_in1, 64)
            e.tensor_scalar(TS, temp, SCALE1, None, ALU.mult)
            e.wait_ge(norms[2].out, norms[2].written)
            for i in range(3):
                if i:
                    e.wait_ge(cur_out, 16 * i)
                e.memset(ACC[:, :], 0.0)
                if i == 0:
                    e.memset(v3(G, 257)[:, :, C:C + 1], 1.0)
                    e.drain()
                    e.tensor_tensor(x3, x3, over_tiles(bproj, C), ALU.add)
                    e.drain()
                    e.tensor_tensor(x3, x3, over_tiles(obias, C), ALU.add)
                e.drain()
                hop_dve(e, hops[i + 1], i)
                e.drain().then_inc(hop_done, 1)
                rendezvous(e, "dve", R[f"hop{i + 1}"] + 1)
            with e.Fori(0, TURNS) as s:
                add_banks(e, s, g1_mm, 3 * NT)
                rendezvous(e, "dve", s + (R["gnn1"] + 1))
            A = 0.5
            vals = [A] + [2 * A] * 15 + [A, SCALE1 ** 2, SCALE1 ** 4]
            for g, val in enumerate(vals):
                e.memset(coef[32 * (g % 4):32 * (g % 4) + 32, g // 4:g // 4 + 1], val / N)
            e.memset(v3(V4, HV)[:, :, 0:1], 1.0)
            f3 = F0.rearrange("p (h g i) -> p h g i", h=8, i=32)
            e.memset(f3[:, :, FG - 1, :], 0.0)
            e.drain()
            e.memset(f3[:, :, FG - 1, 0:1], 1.0)
            factors_dve(e, bk, 1.0, 1)
            e.tensor_scalar(RIA, RIA, SCALE1, None, ALU.mult)
            e.drain()
            pairs(e, lambda *step: m1A_dve(e, *step))
            take_sums(e, 1)
            factors_dve(e, bq, SCALE1, 2)
            e.tensor_tensor(v3(RIA, 8), v3(RIA, 8), over_tiles(TS, 8), ALU.mult)
            sums_dve(e)
            rendezvous(e, "dve", R["m1A"] + 1)
            steps(e, lambda n, has: m1B_dve(e, n, has))
            rendezvous(e, "dve", R["m1B"] + 1)
            rendezvous(e, "dve", R["lnd"] + 1)
            norm_dve(e, norms[3])
            with e.Fori(0, TURNS) as s:
                narrow_dve(e, s, LG, 8, 8, gp_mm, NT)
                rendezvous(e, "dve", s + (R["gate1"] + 1))
            gates1_dve(e)
            e.drain()
            places_dve(e)
            rendezvous(e, "dve", R["gate1_end"] + 1)
            ffn1_dve(e)
            rendezvous(e, "dve", R["ffn1"] + 1)
            e.sem_inc(yg_used, TI)
            with e.Fori(0, TURNS) as s:
                combine_dve(e, s)
            rendezvous(e, "dve", R["ffn1_end"] + 1)


_INS = ['x', 'src', 'dst', 'edge_weight', 'L0_gnn_weight', 'L0_mix_Wq', 'L0_mix_Wk', 'L0_mix_Wv', 'L0_mix_Wm',
        'L0_mix_W1', 'L0_mix_W2', 'L0_mix_g1', 'L0_mix_b1', 'L0_mix_g2', 'L0_mix_b2', 'L0_ffn_W_gat',
        'L0_ffn_att_src', 'L0_ffn_att_dst', 'L0_ffn_b_gat', 'L0_ffn_ln_gamma', 'L0_ffn_ln_beta', 'L0_ffn_W1',
        'L0_ffn_b1', 'L0_ffn_W2', 'L0_ffn_b2', 'L0_ffn_edge_index', 'L1_gnn_shared_weight', 'L1_gnn_output_bias',
        'L1_mix_Wqkv', 'L1_mix_bqkv', 'L1_mix_Wproj', 'L1_mix_bproj', 'L1_mix_temperature', 'L1_ffn_gate_w',
        'L1_ffn_gate_b', 'L1_ffn_W1', 'L1_ffn_b1', 'L1_ffn_W2', 'L1_ffn_b2']


def kernel(**inputs):
    import numpy as np
    import concourse.bacc as bacc
    from concourse.bass_utils import run_bass_kernel_spmd

    nc = bacc.Bacc("TRN2", target_bir_lowering=False, num_devices=1)
    arrays, args = {}, {}
    for name in _INS:
        arr = np.ascontiguousarray(inputs[name])
        arrays[f"in_{name}"] = arr
        args[name] = nc.dram_tensor(f"in_{name}", arr.shape, mybir.dt.from_np(arr.dtype), kind="ExternalInput").ap()
    out = nc.dram_tensor("out_0", (N, C), F32, kind="ExternalOutput").ap()
    gps_kernel(nc, args, out)
    r = run_bass_kernel_spmd(nc, [arrays], core_ids=[0])
    return r.results[0]["out_0"]
```
